# Optimizing a Trainium2 kernel written in Bass

```python
import numpy as np
import jax
import jax.numpy as jnp

def _softmax(x, axis=-1):
    return jax.nn.softmax(x, axis=axis)

def _gelu(x):
    return jax.nn.gelu(x, approximate=True)

def _silu(x):
    return jax.nn.silu(x)

def _sigmoid(x):
    return jax.nn.sigmoid(x)

def _layernorm(x, axis=-1, eps=1e-05):
    m = jnp.mean(x, axis=axis, keepdims=True)
    v = jnp.var(x, axis=axis, keepdims=True)
    return (x - m) / jnp.sqrt(v + eps)

def _scatter_add(tgt, idx, src, axis=0):
    return tgt.at[idx].add(src)

def _segment_sum(src, seg, n):
    return jax.ops.segment_sum(src, seg, n)
kernel_name = 'mk_xattn_ffn_d1_seqx_r4_aff8f9'

def setup_inputs(seed: int=0):
    np.random.seed(seed)
    _w = jnp.asarray

    def _rec_inputs():
        import jax
        import jax.numpy as jnp
        _rk = jax.random.key(seed)
        x = 7.22e-05 + 1 * jax.random.normal(jax.random.fold_in(_rk, 1), (4, 512, 512), jnp.float32)
        _lenS = 512 - jax.random.randint(jax.random.fold_in(_rk, 7), (4,), 0, max(1, 512 // 4) + 1, jnp.int32)
        _lenS2 = 512 - jax.random.randint(jax.random.fold_in(_rk, 8), (4,), 0, max(1, 512 // 4) + 1, jnp.int32)
        _ctx_1024P = jax.random.normal(jax.random.fold_in(_rk, 11), (4, 16, 256), jnp.float32)
        _ctx_1024c = jax.random.dirichlet(jax.random.fold_in(_rk, 511), 0.3 * jnp.ones((16,), jnp.float32), (4, 512))
        _ctx_1024t = jnp.einsum('bsk,bkd->bsd', _ctx_1024c, _ctx_1024P)
        _ctx_1024t = _ctx_1024t * jax.lax.rsqrt(jnp.mean(jnp.square(_ctx_1024t)) + 1e-12) * 0.953939
        ctx_1024 = -1.39393e-06 + 0.999914 * (_ctx_1024t + 0.3 * jax.random.normal(jax.random.fold_in(_rk, 611), (4, 512, 256), jnp.float32))
        fside_BxSx2_0 = jax.random.uniform(jax.random.fold_in(_rk, 12), (4, 512, 2), jnp.float32, 0.0, 0.999707)
        return (x, ctx_1024, fside_BxSx2_0)
    x, ctx_1024, fside_BxSx2_0 = _rec_inputs()

    def _L0_xattn_setup():
        import jax, jax.numpy as jnp
        import numpy as np
        DIM = 512
        CTX_DIM = 256
        N_HEADS = 32
        HEAD_DIM = DIM // N_HEADS
        POS_DIM = 2
        B, N, CTXN = (2, 512, 512)
        ROPE_BASE = 10000.0

        def apply_axial_rope(x, pos):
            b, n, h, d = x.shape
            p = pos.shape[-1]
            dpa = d // p
            half = dpa // 2
            freqs = ROPE_BASE ** (-jnp.arange(half, dtype=x.dtype) / half)
            ang = pos[..., :, None] * freqs
            cos = jnp.cos(ang)[:, :, None, :, :]
            sin = jnp.sin(ang)[:, :, None, :, :]
            xr = x.reshape(b, n, h, p, half, 2)
            x1, x2 = (xr[..., 0], xr[..., 1])
            out = jnp.stack([x1 * cos - x2 * sin, x1 * sin + x2 * cos], axis=-1)
            return out.reshape(b, n, h, d)
        key = jax.random.key(seed)
        ks = jax.random.split(key, 8)
        x = jax.random.normal(ks[0], (B, N, DIM), jnp.float32)
        ctx = jax.random.normal(ks[1], (B, CTXN, CTX_DIM), jnp.float32)
        pos_map = jax.random.uniform(ks[2], (B, N, POS_DIM), jnp.float32)
        ctx_pos_map = jax.random.uniform(ks[3], (B, CTXN, POS_DIM), jnp.float32)
        Wq = jax.random.normal(ks[4], (DIM, DIM), jnp.float32) / np.sqrt(DIM)
        Wkv = jax.random.normal(ks[5], (CTX_DIM, 2 * DIM), jnp.float32) / np.sqrt(CTX_DIM)
        Wout = jax.random.normal(ks[6], (DIM, DIM), jnp.float32) / np.sqrt(DIM)
        bout = jnp.zeros((DIM,), jnp.float32)
        return {'x': x, 'ctx': ctx, 'pos_map': pos_map, 'ctx_pos_map': ctx_pos_map, 'Wq': Wq, 'Wkv': Wkv, 'Wout': Wout, 'bout': bout}
    _L0_xattn_all = _L0_xattn_setup()
    _L0_xattn_in = {k: v for k, v in _L0_xattn_all.items() if k in ('Wq', 'Wkv', 'Wout', 'bout')}
    del _L0_xattn_all

    def _L0_ffn_setup():
        import jax, jax.numpy as jnp
        import numpy as np
        EPS = 1e-06
        Q_B = 128.0

        def layer_norm(x):
            mean = jnp.mean(x, axis=-1, keepdims=True)
            var = jnp.var(x, axis=-1, keepdims=True)
            return (x - mean) / jnp.sqrt(var + EPS)

        def absmax_quant(x):
            gamma = jnp.max(jnp.abs(x), axis=-1, keepdims=True)
            x_hat = jnp.clip(x * Q_B / gamma, -Q_B + EPS, Q_B - EPS)
            return x_hat * gamma / Q_B

        def ternarize_weights(w):
            gamma = jnp.mean(jnp.abs(w))
            return jnp.sign(jnp.round(w / (gamma + EPS))) * gamma

        def bitlinear(x, w):
            xn = layer_norm(x)
            x_hat = xn + jax.lax.stop_gradient(absmax_quant(xn) - xn)
            w_hat = w + jax.lax.stop_gradient(ternarize_weights(w) - w)
            return jnp.einsum('bsd,od->bso', x_hat, w_hat)
        key = jax.random.key(seed)
        k1, k2, k3 = jax.random.split(key, 3)
        B, S, D = (4, 512, 512)
        x = jax.random.normal(k1, (B, S, D), dtype=jnp.float32)
        w_fc = jax.random.normal(k2, (4 * D, D), dtype=jnp.float32) / np.sqrt(D)
        w_proj = jax.random.normal(k3, (D, 4 * D), dtype=jnp.float32) / np.sqrt(4 * D)
        return {'x': x, 'w_fc': w_fc, 'w_proj': w_proj}
    _L0_ffn_all = _L0_ffn_setup()
    _L0_ffn_in = {k: v for k, v in _L0_ffn_all.items() if k in ('w_fc', 'w_proj')}
    del _L0_ffn_all
    return {'x': x, 'ctx_1024': ctx_1024, 'fside_BxSx2_0': fside_BxSx2_0, 'L0_xattn_Wq': _L0_xattn_in['Wq'], 'L0_xattn_Wkv': _L0_xattn_in['Wkv'], 'L0_xattn_Wout': _L0_xattn_in['Wout'], 'L0_xattn_bout': _L0_xattn_in['bout'], 'L0_ffn_w_fc': _L0_ffn_in['w_fc'], 'L0_ffn_w_proj': _L0_ffn_in['w_proj']}

def reference(x, ctx_1024, fside_BxSx2_0, L0_xattn_Wq, L0_xattn_Wkv, L0_xattn_Wout, L0_xattn_bout, L0_ffn_w_fc, L0_ffn_w_proj):
    import jax
    import jax.numpy as jnp

    def _L0_xattn_ref(x, ctx, pos_map, ctx_pos_map, Wq, Wkv, Wout, bout):
        import jax, jax.numpy as jnp
        import numpy as np
        DIM = 512
        CTX_DIM = 256
        N_HEADS = 32
        HEAD_DIM = DIM // N_HEADS
        POS_DIM = 2
        B, N, CTXN = (2, 512, 512)
        ROPE_BASE = 10000.0

        def apply_axial_rope(x, pos):
            b, n, h, d = x.shape
            p = pos.shape[-1]
            dpa = d // p
            half = dpa // 2
            freqs = ROPE_BASE ** (-jnp.arange(half, dtype=x.dtype) / half)
            ang = pos[..., :, None] * freqs
            cos = jnp.cos(ang)[:, :, None, :, :]
            sin = jnp.sin(ang)[:, :, None, :, :]
            xr = x.reshape(b, n, h, p, half, 2)
            x1, x2 = (xr[..., 0], xr[..., 1])
            out = jnp.stack([x1 * cos - x2 * sin, x1 * sin + x2 * cos], axis=-1)
            return out.reshape(b, n, h, d)
        b, n, _ = x.shape
        ctx_n = ctx.shape[1]
        q = (x @ Wq).reshape(b, n, N_HEADS, HEAD_DIM)
        k, v = jnp.split(ctx @ Wkv, 2, axis=-1)
        k = k.reshape(b, ctx_n, N_HEADS, HEAD_DIM)
        v = v.reshape(b, ctx_n, N_HEADS, HEAD_DIM)
        q = apply_axial_rope(q, pos_map)
        k = apply_axial_rope(k, ctx_pos_map)
        scale = 1.0 / np.sqrt(HEAD_DIM).astype(np.float32)
        logits = jnp.einsum('bqhd,bkhd->bhqk', q, k) * scale
        w = jax.nn.softmax(logits, axis=-1)
        attn = jnp.einsum('bhqk,bkhd->bqhd', w, v)
        attn = attn.reshape(b, n, N_HEADS * HEAD_DIM)
        return attn @ Wout + bout

    def _L0_ffn_ref(x, w_fc, w_proj):
        import jax, jax.numpy as jnp
        import numpy as np
        EPS = 1e-06
        Q_B = 128.0

        def layer_norm(x):
            mean = jnp.mean(x, axis=-1, keepdims=True)
            var = jnp.var(x, axis=-1, keepdims=True)
            return (x - mean) / jnp.sqrt(var + EPS)

        def absmax_quant(x):
            gamma = jnp.max(jnp.abs(x), axis=-1, keepdims=True)
            x_hat = jnp.clip(x * Q_B / gamma, -Q_B + EPS, Q_B - EPS)
            return x_hat * gamma / Q_B

        def ternarize_weights(w):
            gamma = jnp.mean(jnp.abs(w))
            return jnp.sign(jnp.round(w / (gamma + EPS))) * gamma

        def bitlinear(x, w):
            xn = layer_norm(x)
            x_hat = xn + jax.lax.stop_gradient(absmax_quant(xn) - xn)
            w_hat = w + jax.lax.stop_gradient(ternarize_weights(w) - w)
            return jnp.einsum('bsd,od->bso', x_hat, w_hat)
        h = bitlinear(x, w_fc)
        h = jax.nn.gelu(h, approximate=False)
        return bitlinear(h, w_proj)
    x = x + _L0_xattn_ref(_layernorm(x, axis=-1), ctx_1024, fside_BxSx2_0, fside_BxSx2_0, L0_xattn_Wq, L0_xattn_Wkv, L0_xattn_Wout, L0_xattn_bout)
    x = x + _L0_ffn_ref(_layernorm(x, axis=-1), L0_ffn_w_fc, L0_ffn_w_proj)
    return x

_drawn_inputs = setup_inputs


def setup_inputs(seed=0):
    import zlib

    import numpy as np

    out = dict(_drawn_inputs(seed))
    spreads = {'L0_xattn_bout': (0.0, 0.1)}
    factors = {}
    for name, (base, spread) in spreads.items():
        noise = np.random.default_rng([zlib.crc32(name.encode()), seed]).standard_normal(out[name].shape)
        drawn = base * np.exp(spread * noise) if base else spread * noise
        out[name] = jnp.asarray(drawn.astype(out[name].dtype))
    for name, factor in factors.items():
        out[name] = (out[name] * factor).astype(out[name].dtype)
    return out
```

```python
import math
from contextlib import ExitStack

import concourse.bass as bass
from concourse import mybir

F32 = mybir.dt.float32
BF16 = mybir.dt.bfloat16
F16 = mybir.dt.float16
ACT = mybir.ActivationFunctionType
ALU = mybir.AluOpType
AX = mybir.AxisListType

P = 128
BATCH, SEQ, DIM, CTX = 4, 512, 512, 256
HEADS, HEAD = 32, 16
FFN = 4 * DIM
ROWS = BATCH * SEQ
TILES = ROWS // P
CHUNKS = SEQ // P
KX, KC = DIM // P, CTX // P
KF = FFN // P
GH = 4
HG = HEADS // GH
GROUPS = BATCH * HG
GW = GH * HEAD
PARTS = 3
STACK = 6 * HEAD
AXES, FREQS = 2, 4
ANGLES = AXES * FREQS
LN_EPS, FFN_EPS = 1e-5, 1e-6
Q_B = 128.0
ROUNDER = 1.5 * 2.0 ** 23
TWO_PI_HIGH = 6.28125
TWO_PI_LOW = 2 * math.pi - TWO_PI_HIGH
PI_BELOW = 3.1415925
TURN = 4


class At:

    def __init__(self, turn, k):
        self.turn, self.k = turn, k
        self.looped = not isinstance(turn, int)
        self.n = turn * TURN + k
        self.quad = turn + k // TURN

    def back(self, by):
        return At(self.turn, self.k - by)

    def within(self, count):
        return self.looped or 0 <= self.k < count

    @property
    def use_of_two(self):
        return self.turn * 2 + self.k // 2 + 1

    def slot(self, m):
        return self.k % m


def run_steps(eng, count, later, head, step):
    for s in range(head):
        step(At(0, s))
    turns = (count - head) // TURN
    with eng.Fori(0, turns) as turn:
        for u in range(TURN):
            step(At(turn, head + u))
    for s in range(head + turns * TURN, count + later):
        step(At(0, s))


def need(eng, semaphore, value):
    if not isinstance(value, int) or value > 0:
        eng.wait_ge(semaphore, value)


def need_apart(eng, semaphore, value, over):
    if not isinstance(value, int) or value > 0:
        eng.wait_ge(semaphore, value).then_inc(over, 1)


def allocators(nc, stack, stage):

    def sb(name, shape, dt):
        return stack.enter_context(nc.sbuf_tensor(f"{stage}_{name}", shape, dt))

    def pb(name, shape, dt):
        return stack.enter_context(nc.psum_tensor(f"{stage}_{name}", shape, dt))

    def sem(name):
        return stack.enter_context(nc.semaphore(f"{stage}_{name}"))

    return sb, pb, sem


def project(nc, x, ctx, pos, wq, wkv, ident, v_all, q_parts, k_parts):
    with ExitStack() as stack:
        sb, pb, sem = allocators(nc, stack, "project")
        x_sb = sb("x_sb", [P, TURN, DIM], F32)
        ctx_sb = sb("ctx_sb", [P, TURN, CTX], F32)
        w_raw = sb("w_raw", [P, KX, DIM], F32)
        wk_raw = sb("wk_raw", [P, KC, DIM], F32)
        wq_sb = sb("wq_sb", [P, KX, DIM], F32)
        wk_sb = sb("wk_sb", [P, KC, DIM], F32)
        wv_sb = sb("wv_sb", [P, KC, DIM], F32)
        pos_sb = sb("pos_sb", [P, TILES, AXES], F32)
        angle = sb("angle", [P, TILES, AXES, FREQS], F32)
        whole = sb("whole", [P, TILES * ANGLES], F32)
        over = sb("over", [P, TILES * ANGLES], F32)
        shifted = sb("shifted", [P, TILES * ANGLES], F32)
        cosine = sb("cosine", [P, TILES, ANGLES, 2], F32)
        sine = sb("sine", [P, TILES, ANGLES], F32)
        neg_sine = sb("neg_sine", [P, TILES, ANGLES], F32)
        stats = sb("stats", [P, 2, 6], F32)
        moments = sb("moments", [P, 2, 2], F32)
        half_power = sb("half_power", [P, 1], F32)
        rstd = sb("rstd", [P, 2, 2], F32)
        xn = sb("xn", [P, 2, DIM], F32)
        xT = sb("xT", [P, 2, DIM], F32)
        ctxT = sb("ctxT", [P, 2, CTX], F32)
        straight = [sb(f"straight_{s}", [P, DIM], F32) for s in "kq"]
        crossed = [sb(f"crossed_{s}", [P, DIM], F32) for s in "kq"]
        rotated = [sb(f"rotated_{s}", [P, DIM], F32) for s in "kq"]
        rest = [sb(f"rest_{s}", [P, DIM], F32) for s in "kq"]
        parts = sb("parts", [P, 2, 2, PARTS, KX, 2 * P], BF16)
        banks = pb("banks", [P, 8, DIM], F32)
        xT_bank, ctxT_bank, v_bank = banks[:, 0], banks[:, 1, 0:CTX], banks[:, 2]
        in_bank = [banks[:, 3], banks[:, 4]]
        turned_bank = [banks[:, 5], banks[:, 6]]

        w_loaded = {w: sem(f"{w}_loaded") for w in ("wk", "wv", "wq", "pos")}
        x_loaded = [sem(f"x_loaded_{i}") for i in range(TURN)]
        ctx_loaded = [sem(f"ctx_loaded_{i}") for i in range(TURN)]
        w_ordered = sem("w_ordered")
        tables_step, angles_ready, sines_ready, tables_ready = (
            sem("tables_step"), sem("angles_ready"), sem("sines_ready"), sem("tables_ready"))
        stats_done, stats_ready, power_ready, rstd_ready = (
            sem("stats_done"), sem("stats_ready"), sem("power_ready"), sem("rstd_ready"))
        xn_ready, x_turned, ctx_turned, xT_saved, ctxT_saved = (
            sem("xn_ready"), sem("x_turned"), sem("ctx_turned"), sem("xT_saved"), sem("ctxT_saved"))
        v_projected, v_saved = sem("v_projected"), sem("v_saved")
        projected = [sem(f"{s}_projected") for s in "kq"]
        multiplied = [sem(f"{s}_multiplied") for s in "kq"]
        summed = [sem(f"{s}_summed") for s in "kq"]
        turned = [sem(f"{s}_turned") for s in "kq"]
        first_done = [sem(f"{s}_first_done") for s in "kq"]
        rest_done = [sem(f"{s}_rest_done") for s in "kq"]
        second_done = [sem(f"{s}_second_done") for s in "kq"]
        third_done = [sem(f"{s}_third_done") for s in "kq"]
        parts_stored = [sem(f"parts_stored_{i}") for i in range(2)]
        PAIR_STORES = 16 * 2 * 2 * PARTS
        START = 1

        waited = sem("waited")
        block = stack.enter_context(nc.Block())

        @block.sync
        def _(sp):
            x_rows = x.rearrange("b (c p) d -> (b c) p d", p=P)
            ctx_rows = ctx.rearrange("b (c p) d -> (b c) p d", p=P)
            wkv_rows = wkv.rearrange("(k p) n -> p k n", p=P)

            def load_ctx(at):
                need(sp, ctx_turned, at.n - TURN + 1)
                sp.dma_start(ctx_sb[:, at.slot(TURN)], ctx_rows[at.n]).then_inc(ctx_loaded[at.slot(TURN)], 16)

            def load_x(at):
                need(sp, xn_ready, at.n - TURN + 1)
                sp.dma_start(x_sb[:, at.slot(TURN)], x_rows[at.n]).then_inc(x_loaded[at.slot(TURN)], 16)

            load_ctx(At(0, 0))
            sp.dma_start(wk_raw[:], wkv_rows[:, :, 0:DIM]).then_inc(w_loaded["wk"], 16)
            load_x(At(0, 0))
            sp.dma_start(wv_sb[:], wkv_rows[:, :, DIM:2 * DIM]).then_inc(w_loaded["wv"], 16)
            sp.dma_start(w_raw[:], wq.rearrange("(k p) n -> p k n", p=P)).then_inc(w_loaded["wq"], 16)
            sp.dma_start(pos_sb[:], pos.rearrange("b (c p) a -> p (b c) a", p=P)).then_inc(w_loaded["pos"], 16)

            def store(at):
                pair = at.slot(4) // 2
                for s, where in ((0, k_parts), (1, q_parts)):
                    view = where.rearrange("(b k g) t e c -> b g t e k c", b=BATCH, k=KX)
                    sp.wait_ge(second_done[s], at.n + 1)
                    sp.wait_ge(third_done[s], at.n + 1)
                    for part in range(PARTS):
                        for g in range(2):
                            sp.dma_start(view[at.quad, g, part, :, :, pair * 2 * P:(pair + 1) * 2 * P],
                                         parts[g * GW:(g + 1) * GW, pair, s, part]).then_inc(parts_stored[pair], 16)

            def step(at):
                if at.within(TILES) and not (isinstance(at.n, int) and at.n == 0):
                    load_ctx(at)
                    load_x(at)
                if at.back(6).within(TILES) and at.back(6).slot(2) == 1:
                    store(at.back(6))

            run_steps(sp, TILES, 6, 8, step)
            for pair in range(2):
                sp.wait_ge(parts_stored[pair], PAIR_STORES * BATCH + START)

        @block.tensor
        def _(pe):
            def turn_inputs(at):
                r = at.slot(2)
                pe.wait_ge(ctx_loaded[at.slot(TURN)], at.quad * 16 + 16)
                need(pe, ctxT_saved, at.n)
                for k in range(KC):
                    mm = nc.tensor.transpose(ctxT_bank[:, k * P:(k + 1) * P],
                                             ctx_sb[:, at.slot(TURN), k * P:(k + 1) * P], ident[:])
                mm.then_inc(ctx_turned, 1)
                pe.wait_ge(xn_ready, at.n + 1)
                need(pe, xT_saved, at.n)
                for k in range(KX):
                    mm = nc.tensor.transpose(xT_bank[:, k * P:(k + 1) * P], xn[:, r, k * P:(k + 1) * P], ident[:])
                mm.then_inc(x_turned, 1)

            def product(out, lhs, rhs, blocks, done):
                for k in range(blocks):
                    mm = nc.tensor.matmul(out, lhs[:, k * P:(k + 1) * P], rhs[:, k, :],
                                          start=(k == 0), stop=(k == blocks - 1))
                mm.then_inc(done, 1)

            def project_kv(at):
                r = at.slot(2)
                pe.wait_ge(ctxT_saved, at.n + 1)
                need(pe, multiplied[0], at.n)
                product(in_bank[0], ctxT[:, r], wk_sb, KC, projected[0])
                need(pe, v_saved, at.n)
                product(v_bank, ctxT[:, r], wv_sb, KC, v_projected)

            def project_q(at):
                pe.wait_ge(xT_saved, at.n + 1)
                need(pe, multiplied[1], at.n)
                product(in_bank[1], xT[:, at.slot(2)], wq_sb, KX, projected[1])

            def turn_rotated(at):
                for s in range(2):
                    pe.wait_ge(summed[s], at.n + 1)
                    need(pe, rest_done[s], at.n)
                    for k in range(KX):
                        mm = nc.tensor.transpose(turned_bank[s][:, k * P:(k + 1) * P],
                                                 rotated[s][:, k * P:(k + 1) * P], ident[:])
                    mm.then_inc(turned[s], 1)

            pe.wait_ge(w_ordered, 2)
            pe.wait_ge(w_loaded["wv"], 16)

            def step(at):
                if at.back(2).within(TILES):
                    turn_inputs(at.back(2))
                if at.back(3).within(TILES):
                    project_kv(at.back(3))
                if at.back(4).within(TILES):
                    turn_rotated(at.back(4))
                if at.back(3).within(TILES):
                    project_q(at.back(3))

            run_steps(pe, TILES, 4, 5, step)

        @block.vector
        def _(dve):
            def make_tables():
                flat = angle[:].rearrange("p t a f -> p (t a f)")
                done = [0]

                def then(ins, more=1):
                    done[0] += more
                    ins.then_inc(tables_step, 1)

                def settled():
                    dve.wait_ge(tables_step, done[0])

                def reduce(values):
                    then(dve.tensor_scalar(whole[:], values, 1 / (2 * math.pi), ROUNDER, ALU.mult, ALU.add))
                    settled()
                    then(dve.tensor_scalar(over[:], whole[:], -ROUNDER, None, ALU.add))
                    settled()
                    then(dve.scalar_tensor_tensor(whole[:], over[:], -TWO_PI_HIGH, values, ALU.mult, ALU.add))
                    settled()
                    then(dve.scalar_tensor_tensor(values, over[:], -TWO_PI_LOW, whole[:], ALU.mult, ALU.add))
                    settled()

                def clamp(values):
                    then(dve.tensor_scalar(values, values, PI_BELOW, -PI_BELOW, ALU.min, ALU.max))

                dve.wait_ge(w_loaded["pos"], 16)
                for f in range(FREQS):
                    then(dve.tensor_scalar(angle[:, :, :, f], pos_sb[:], 10000.0 ** (-f / FREQS), None, ALU.mult))
                settled()
                reduce(flat)
                then(dve.tensor_scalar(shifted[:], flat, math.pi / 2, None, ALU.add))
                settled()
                reduce(shifted[:])
                clamp(flat)
                clamp(shifted[:])
                settled()
                dve.engine_nop().then_inc(angles_ready, 1)
                dve.wait_ge(sines_ready, 2)
                dve.tensor_scalar(neg_sine[:], sine[:], -1.0, None, ALU.mult).then_inc(tables_ready, 1)

            def statistics(at):
                r = at.slot(2)
                dve.wait_ge(x_loaded[at.slot(TURN)], at.quad * 16 + 16)
                dve.bn_stats(stats[:, r], x_sb[:, at.slot(TURN)]).then_inc(stats_done, 1)
                need_apart(dve, stats_done, at.n + 1, waited)
                need_apart(dve, xn_ready, at.n - 1, waited)
                dve.bn_aggr(moments[:, r], stats[:, r]).then_inc(stats_ready, 1)

            def normalise(at):
                r = at.slot(2)
                dve.wait_ge(rstd_ready, at.n + 1)
                need(dve, x_turned, at.n - 1)
                dve.tensor_scalar(xn[:, r], x_sb[:, at.slot(TURN)], moments[:, r, 0:1], rstd[:, r, 1:2],
                                  ALU.subtract, ALU.mult).then_inc(xn_ready, 1)

            def rope_products(at, s):
                table = lambda t, w: t.unsqueeze(1).unsqueeze(3).to_broadcast([P, HG, w, GH])
                cos = cosine[:, at.n].rearrange("p a r -> p (a r)")
                dve.wait_ge(projected[s], at.n + 1)
                need(dve, summed[s], at.n)
                view = lambda t: t.rearrange("p (g d h) -> p g d h", g=HG, h=GH)
                pairs = lambda t, r: t.rearrange("p (g a r h) -> p g a r h", g=HG, r=2, h=GH)[:, :, :, r]
                dve.tensor_tensor(view(straight[s][:]), view(in_bank[s]), table(cos, HEAD), ALU.mult)
                dve.tensor_tensor(pairs(crossed[s][:], 0), pairs(in_bank[s], 1),
                                  table(neg_sine[:, at.n], ANGLES), ALU.mult)
                dve.tensor_tensor(pairs(crossed[s][:], 1), pairs(in_bank[s], 0),
                                  table(sine[:, at.n], ANGLES), ALU.mult).then_inc(multiplied[s], 1)

            def take_first(at, s):
                dve.wait_ge(turned[s], at.n + 1)
                dve.wait_ge(first_done[s], at.n + 1)
                need(dve, second_done[s], at.n)
                need(dve, third_done[s], at.n)
                dve.tensor_tensor(rest[s][:].rearrange("p (k c) -> p k c", k=KX),
                                  turned_bank[s].rearrange("p (k c) -> p k c", k=KX),
                                  part_now(at, s, 0), ALU.subtract).then_inc(rest_done[s], 1)

            def part_now(at, s, part):
                half = at.slot(2)
                return parts[:, at.slot(4) // 2, s, part, :, half * P:(half + 1) * P]

            statistics(At(0, 0))
            make_tables()
            dve.wait_ge(tables_ready, 1)

            def step(at):
                if at.within(TILES) and not (isinstance(at.n, int) and at.n == 0):
                    statistics(at)
                if at.back(1).within(TILES):
                    normalise(at.back(1))
                if at.back(3).within(TILES):
                    rope_products(at.back(3), 0)
                if at.back(4).within(TILES):
                    take_first(at.back(4), 0)
                    take_first(at.back(4), 1)
                if at.back(3).within(TILES):
                    rope_products(at.back(3), 1)

            run_steps(dve, TILES, 4, 5, step)

        @block.scalar
        def _(act):
            def part_now(at, s, part):
                half = at.slot(2)
                return parts[:, at.slot(4) // 2, s, part, :, half * P:(half + 1) * P]

            def order_weights():
                order = lambda t, k: t.rearrange("p k (g h d) -> p (k g) d h", h=GH, d=HEAD)
                plain = lambda t: t.rearrange("p k (g d h) -> p (k g) d h", h=GH, d=HEAD)
                act.wait_ge(w_loaded["wk"], 16)
                nc.scalar.copy(plain(wk_sb[:]), order(wk_raw[:], KC)).then_inc(w_ordered, 1)
                act.wait_ge(w_loaded["wq"], 16)
                nc.scalar.copy(plain(wq_sb[:]), order(w_raw[:], KX)).then_inc(w_ordered, 1)

            def save_inputs(at):
                r = at.slot(2)
                act.wait_ge(ctx_turned, at.n + 1)
                need(act, v_projected, at.n - 1)
                nc.scalar.copy(ctxT[:, r], ctxT_bank).then_inc(ctxT_saved, 1)
                act.wait_ge(x_turned, at.n + 1)
                need(act, projected[1], at.n - 1)
                nc.scalar.copy(xT[:, r], xT_bank).then_inc(xT_saved, 1)

            def save_v(at):
                need_apart(act, v_projected, at.n + 1, waited)
                out = v_all[:].rearrange("p (b g) c e -> p b c g e", b=BATCH)[:, at.quad, at.slot(CHUNKS)]
                nc.scalar.copy(out, v_bank.rearrange("p (g e) -> p g e", g=HG)).then_inc(v_saved, 1)

            def first_two(at, s):
                pair = at.slot(4) // 2
                need(act, parts_stored[pair], at.quad * PAIR_STORES + START)
                act.wait_ge(turned[s], at.n + 1)
                nc.scalar.copy(part_now(at, s, 0), turned_bank[s].rearrange("p (k c) -> p k c", k=KX)
                               ).then_inc(first_done[s], 1)
                act.wait_ge(rest_done[s], at.n + 1)
                nc.scalar.copy(part_now(at, s, 1), rest[s][:].rearrange("p (k c) -> p k c", k=KX)
                               ).then_inc(second_done[s], 1)

            order_weights()
            act.wait_ge(angles_ready, 1)
            nc.scalar.activation(sine[:].rearrange("p t a -> p (t a)"), angle[:].rearrange("p t a f -> p (t a f)"),
                                 ACT.Sin).then_inc(sines_ready, 1)
            nc.scalar.activation(cosine[:].rearrange("p t a r -> p (t a) r"),
                                 shifted[:].unsqueeze(2).to_broadcast([P, TILES * ANGLES, 2]),
                                 ACT.Sin).then_inc(sines_ready, 1)

            def step(at):
                if at.back(2).within(TILES):
                    save_inputs(at.back(2))
                if at.back(4).within(TILES):
                    first_two(at.back(4), 0)
                if at.back(3).within(TILES):
                    save_v(at.back(3))
                if at.back(4).within(TILES):
                    first_two(at.back(4), 1)

            run_steps(act, TILES, 4, 5, step)

        @block.gpsimd
        def _(pool):
            def spread(at):
                r = at.slot(2)
                need_apart(pool, stats_ready, at.n + 1, waited)
                need_apart(pool, xn_ready, at.n - 1, waited)
                pool.tensor_scalar(rstd[:, r, 0:1], moments[:, r, 1:2], LN_EPS, None, ALU.add).then_inc(power_ready, 1)
                pool.wait_ge(power_ready, at.n + 2)
                pool.tensor_tensor(rstd[:, r, 1:2], rstd[:, r, 0:1], half_power[:], ALU.pow).then_inc(rstd_ready, 1)

            def sum_products(at, s):
                pool.wait_ge(multiplied[s], at.n + 1)
                need(pool, turned[s], at.n)
                pool.tensor_tensor(rotated[s][:], straight[s][:], crossed[s][:], ALU.add).then_inc(summed[s], 1)

            def last_part(at, s):
                half = at.slot(2)
                now = lambda part: parts[:, at.slot(4) // 2, s, part, :, half * P:(half + 1) * P]
                pool.wait_ge(second_done[s], at.n + 1)
                pool.tensor_tensor(now(2), rest[s][:].rearrange("p (k c) -> p k c", k=KX), now(1),
                                   ALU.subtract).then_inc(third_done[s], 1)

            pool.memset(half_power[:], -0.5).then_inc(power_ready, 1)
            for pair in range(2):
                pool.sem_inc(parts_stored[pair], START)

            def step(at):
                if at.within(TILES):
                    spread(at)
                if at.back(3).within(TILES):
                    sum_products(at.back(3), 0)
                if at.back(4).within(TILES):
                    last_part(at.back(4), 0)
                    last_part(at.back(4), 1)
                if at.back(3).within(TILES):
                    sum_products(at.back(3), 1)

            run_steps(pool, TILES, 4, 5, step)


def attend(nc, ident16, v_all, q_parts, k_parts, o_all):
    with ExitStack() as stack:
        sb, pb, sem = allocators(nc, stack, "attend")
        q_stack = sb("q_stack", [P, TURN, GH, SEQ], BF16)
        k_stack = sb("k_stack", [P, TURN, GH, SEQ], BF16)
        probs = sb("probs", [P, CHUNKS, GH, SEQ], F32)
        v_ones = sb("v_ones", [P, 2, CHUNKS, GH, 2 * HEAD], F32)
        maxima = sb("maxima", [P, 2, GH * CHUNKS], F32)
        neg_max = sb("neg_max", [P, 2, GH * CHUNKS], F32)
        max_parts = sb("max_parts", [P, 2, 2 * GH * CHUNKS], BF16)
        max_rows = sb("max_rows", [2 * GH * CHUNKS, 2, P], BF16)
        banks = pb("banks", [P, 8, SEQ], F32)
        score_slot = [banks[:, 0:2], banks[:, 2:4]]
        PV_BANK = banks[:, 7]
        ST_BANK = [4 + k % 3 for k in range(15)] + [5]
        ST_BEFORE = [max(j for j in range(k - 16, k) if ST_BANK[j % 16] == ST_BANK[k]) for k in range(16)]
        STACK_LOADS = 16 * 7

        stacks_loaded = [sem(f"stacks_loaded_{i}") for i in range(TURN)]
        max_loaded = [sem(f"max_loaded_{i}") for i in range(TURN)]
        ones_ready, v_staged = sem("ones_ready"), sem("v_staged")
        scores_ready, scores_read = sem("scores_ready"), sem("scores_read")
        neg_ready, high_ready, split_ready = sem("neg_ready"), sem("high_ready"), sem("split_ready")
        st_ready, exp_done = sem("st_ready"), sem("exp_done")
        pv_done, o_saved = sem("pv_done"), sem("o_saved")


        def score_use(at, j):
            first = at.n * 9 - 1 if at.looped or at.n > 0 else 0
            return first + j + (1 if j >= 2 and (at.looped or at.n > 0) else 0)

        def turn_use(at):
            return at.n * 9 + 10 - (2 if not at.looped and at.n == GROUPS - 1 else 0)

        def score_parity(at, j):
            return (9 * at.k - 1 + j + (j >= 2)) % 2 if at.looped or at.n > 0 else j % 2

        def turn_parity(at):
            return (9 * at.k + 10) % 2

        waited = sem("waited")
        block = stack.enter_context(nc.Block())

        @block.sync
        def _(sp):
            def load_stacks(at):
                slot = at.slot(TURN)
                need(sp, st_ready, (at.n - TURN + 1) * 16)
                for stack_sb, where, runs in (
                    (q_stack, q_parts, ((0, 0, 3), (3, 0, 2), (5, 0, 1))),
                    (k_stack, k_parts, ((0, 1, 1), (1, 0, 1), (2, 0, 1), (3, 0, 3))),
                ):
                    src = where[at.n].rearrange("t (d h) c -> (t d) (h c)", h=GH)
                    for to, part, count in runs:
                        sp.dma_start(
                            stack_sb[to * HEAD:(to + count) * HEAD, slot].rearrange("p h c -> p (h c)"),
                            src[part * HEAD:(part + count) * HEAD],
                        ).then_inc(stacks_loaded[slot], 16)

            def load_max(at):
                sp.wait_ge(scores_read, turn_use(at) + 1)
                sp.dma_start(
                    q_stack[STACK:STACK + 2, at.slot(TURN)].rearrange("p h (c q) -> p (h c) q", c=CHUNKS),
                    max_rows[:, at.slot(2)],
                ).then_inc(max_loaded[at.slot(TURN)], 16)

            def step(at):
                if at.within(GROUPS):
                    load_stacks(at)
                if at.back(2).within(GROUPS):
                    load_max(at.back(2))

            run_steps(sp, GROUPS, 3, 4, step)

        @block.tensor
        def _(pe):
            def scores(at, j):
                head, slot = j // 2, at.slot(TURN)
                if j == 0:
                    pe.wait_ge(stacks_loaded[slot], at.quad * STACK_LOADS + STACK_LOADS)
                need(pe, scores_read, score_use(at, j) - 1)
                for i in range(2):
                    c = j % 2 * 2 + i
                    mm = nc.tensor.matmul(score_slot[score_parity(at, j)][:, i],
                                          q_stack[0:STACK, slot, head, c * P:(c + 1) * P],
                                          k_stack[0:STACK, slot, head, :], start=True, stop=True)
                mm.then_inc(scores_ready, 1)

            def turn_max(at):
                pe.wait_ge(split_ready, at.n + 1)
                need(pe, scores_read, turn_use(at) - 1)
                out = score_slot[turn_parity(at)][0:2 * GH * CHUNKS, 0, 0:P // 2].bitcast(BF16)
                nc.tensor.transpose(out, max_parts[:, at.slot(2)], ident16[:]).then_inc(scores_ready, 1)

            def scores_turned(at, k):
                c, head, slot = k // GH, k % GH, at.slot(TURN)
                if k == 0:
                    pe.wait_ge(max_loaded[slot], at.quad * 16 + 16)
                need(pe, exp_done, at.n * 16 + ST_BEFORE[k] + 1)
                nc.tensor.matmul(banks[:, ST_BANK[k]], k_stack[0:STACK + 2, slot, head, c * P:(c + 1) * P],
                                 q_stack[0:STACK + 2, slot, head, :], start=True, stop=True).then_inc(st_ready, 1)

            def weigh_v(at, c):
                pe.wait_ge(exp_done, at.n * 16 + GH * (c + 1))
                if c == 0:
                    pe.wait_ge(v_staged, at.n + 1)
                    need(pe, o_saved, at.n)
                for j in range(GH):
                    mm = nc.tensor.matmul(PV_BANK[32 * j:32 * j + 32], v_ones[:, at.slot(2), c, j, :],
                                          probs[:, c, j, :], start=(c == 0), stop=(c == CHUNKS - 1))
                mm.then_inc(pv_done, 1)

            pe.wait_ge(ones_ready, 2)

            def step(at):
                turned, before = at.back(2), at.back(3)
                for c in range(CHUNKS):
                    if turned.within(GROUPS):
                        scores_turned(turned, 4 * c)
                        scores_turned(turned, 4 * c + 1)
                    if c == 1 and at.back(1).within(GROUPS):
                        turn_max(at.back(1))
                    if at.within(GROUPS):
                        scores(at, 2 * c)
                    if c == 0 and before.within(GROUPS):
                        weigh_v(before, CHUNKS - 1)
                    if c > 0 and turned.within(GROUPS):
                        weigh_v(turned, c - 1)
                    if turned.within(GROUPS):
                        scores_turned(turned, 4 * c + 2)
                        scores_turned(turned, 4 * c + 3)
                    if at.within(GROUPS):
                        scores(at, 2 * c + 1)

            run_steps(pe, GROUPS, 3, 4, step)

        @block.vector
        def _(dve):
            def row_maxima(at, j):
                dve.wait_ge(scores_ready, score_use(at, j) + 1)
                if j == 0:
                    need(dve, split_ready, at.n - 1)
                dve.tensor_reduce(maxima[:, at.slot(2), 2 * j:2 * j + 2], score_slot[score_parity(at, j)],
                                  AX.X, ALU.max).then_inc(scores_read, 1)

            def save_turned(at):
                dve.wait_ge(scores_ready, turn_use(at) + 1)
                last = at.back(2)
                if last.looped or last.n >= 0:
                    dve.wait_ge(max_loaded[last.slot(TURN)], last.quad * 16 + 16)
                dve.tensor_copy(max_rows[:, at.slot(2)],
                                score_slot[turn_parity(at)][0:2 * GH * CHUNKS, 0, 0:P // 2].bitcast(BF16)
                                ).then_inc(scores_read, 1)

            dve.memset(v_ones[:], 1.0).then_inc(ones_ready, 1)
            dve.memset(k_stack[STACK:STACK + 2], 1.0).then_inc(ones_ready, 1)

            def step(at):
                for j in range(2 * GH):
                    if j == 2 and at.back(1).within(GROUPS):
                        save_turned(at.back(1))
                    if at.within(GROUPS):
                        row_maxima(at, j)

            run_steps(dve, GROUPS, 2, 4, step)

        @block.scalar
        def _(act):
            def exponentials(at, k):
                c, head = k // GH, k % GH
                act.wait_ge(st_ready, at.n * 16 + k + 1)
                if head == 0:
                    need(act, pv_done, (at.n - 1) * CHUNKS + c + 1)
                nc.scalar.activation(probs[:, c, head, :], banks[:, ST_BANK[k]], ACT.Exp,
                                     scale=1 / math.sqrt(HEAD)).then_inc(exp_done, 1)

            def save_sums(at):
                need_apart(act, pv_done, (at.n + 1) * CHUNKS, waited)
                nc.scalar.copy(o_all[:, at.n], PV_BANK).then_inc(o_saved, 1)

            def step(at):
                for k in range(16):
                    if at.back(2).within(GROUPS):
                        exponentials(at.back(2), k)
                    if k == 3 and at.back(3).within(GROUPS):
                        save_sums(at.back(3))

            run_steps(act, GROUPS, 3, 4, step)

        @block.gpsimd
        def _(pool):
            def stage_v(at):
                need(pool, pv_done, (at.n - 1) * CHUNKS)
                pool.tensor_copy(v_ones[:, at.slot(2), :, :, 0:HEAD],
                                 v_all[:, at.n].rearrange("p c (h d) -> p c h d", h=GH)).then_inc(v_staged, 1)

            def split_maxima(at):
                r, half = at.slot(2), GH * CHUNKS
                need_apart(pool, scores_read, score_use(at, 7) + 1, waited)
                pool.tensor_scalar(neg_max[:, r], maxima[:, r], -1.0, None, ALU.mult).then_inc(neg_ready, 1)
                need_apart(pool, neg_ready, at.n + 1, waited)
                if at.looped or at.n >= 2:
                    need_apart(pool, scores_ready, turn_use(at.back(2)) + 1, waited)
                pool.tensor_scalar(max_parts[:, r, 0:half], neg_max[:, r], 1.0, None, ALU.mult
                                   ).then_inc(high_ready, 1)
                pool.wait_ge(high_ready, at.n + 1)
                pool.tensor_tensor(max_parts[:, r, half:2 * half], neg_max[:, r], max_parts[:, r, 0:half],
                                   ALU.subtract).then_inc(split_ready, 1)

            pool.wait_ge(ones_ready, 1)

            def step(at):
                if at.back(2).within(GROUPS):
                    stage_v(at.back(2))
                if at.within(GROUPS):
                    split_maxima(at)

            run_steps(pool, GROUPS, 2, 4, step)


def ternarise(nc, w_fc, w_proj, ident16, fcT, projT, gammas):
    with ExitStack() as stack:
        sb, pb, sem = allocators(nc, stack, "ternarise")
        WIDTH = FFN * DIM // P
        raw = [sb(f"raw_{w}", [P, WIDTH], F32) for w in ("fc", "proj")]
        ternary = [sb(f"ternary_{w}", [P, WIDTH], F16) for w in ("fc", "proj")]
        below = sb("below", [P, 2, FFN], F16)
        sums = sb("sums", [P, 2], F32)
        gamma_eps = sb("gamma_eps", [P, 2], F32)
        limit = sb("limit", [P, 2, 2], F32)
        ones = sb("ones", [P, P], F32)
        banks = pb("banks", [P, 8, DIM], F32)
        loaded = [sem(f"raw_loaded_{w}") for w in ("fc", "proj")]
        ones_ready, summed, total_ready = sem("ones_ready"), sem("summed"), sem("total_ready")
        gamma_ready, limits_ready, cut, ternary_ready = (
            sem("gamma_ready"), sem("limits_ready"), sem("cut"), sem("ternary_ready"))
        turned, saved = sem("turned"), sem("saved")
        PIECES = WIDTH // FFN
        waited = sem("waited")
        block = stack.enter_context(nc.Block())

        @block.sync
        def _(sp):
            sp.dma_start(raw[0][:].rearrange("p (o d) -> p o d", d=DIM),
                         w_fc.rearrange("(o p) d -> p o d", p=P)).then_inc(loaded[0], 16)
            sp.dma_start(raw[1][:].rearrange("p (o d) -> p o d", d=FFN),
                         w_proj.rearrange("(o p) d -> p o d", p=P)).then_inc(loaded[1], 16)

        @block.vector
        def _(dve):
            dve.memset(ones[:], 1.0).then_inc(ones_ready, 1)
            for w in range(2):
                dve.wait_ge(loaded[w], 16)
                dve.tensor_reduce(sums[:, w:w + 1], raw[w][:], AX.X, ALU.add,
                                  apply_absolute_value=True).then_inc(summed, 1)
            for w in range(2):
                dve.wait_ge(total_ready, w + 1)
                dve.tensor_scalar(gammas[:, w:w + 1], banks[:, w, 0:1], 1.0 / (FFN * DIM), None, ALU.mult
                                  ).then_inc(gamma_ready, 1)
                dve.wait_ge(gamma_ready, 3 * w + 1)
                dve.tensor_scalar(gamma_eps[:, w:w + 1], gammas[:, w:w + 1], FFN_EPS, None, ALU.add
                                  ).then_inc(gamma_ready, 1)
                dve.wait_ge(gamma_ready, 3 * w + 2)
                dve.tensor_scalar(limit[:, w, 0:1], gamma_eps[:, w:w + 1], 0.5, None, ALU.mult)
                dve.tensor_scalar(limit[:, w, 1:2], gamma_eps[:, w:w + 1], -0.5, None, ALU.mult
                                  ).then_inc(gamma_ready, 1)
                dve.wait_ge(gamma_ready, 3 * w + 3)
                for i in range(PIECES):
                    n, piece = w * PIECES + i, slice(i * FFN, (i + 1) * FFN)
                    need(dve, ternary_ready, n - 1)
                    dve.tensor_scalar(below[:, n % 2], raw[w][:, piece], limit[:, w, 1:2], None, ALU.is_lt
                                      ).then_inc(cut, 1)
                    dve.wait_ge(cut, n + 1)
                    dve.scalar_tensor_tensor(ternary[w][:, piece], raw[w][:, piece], limit[:, w, 0:1],
                                             below[:, n % 2], ALU.is_gt, ALU.subtract).then_inc(ternary_ready, 1)

        @block.tensor
        def _(pe):
            pe.wait_ge(ones_ready, 1)
            for w in range(2):
                pe.wait_ge(summed, w + 1)
                nc.tensor.matmul(banks[:, w, 0:1], ones[:], sums[:, w:w + 1], start=True, stop=True
                                 ).then_inc(total_ready, 1)
            for n in range(2 * PIECES * 2):
                pe.wait_ge(ternary_ready, n // 2 + 1)
                need(pe, saved, n - 1)
                out = banks[:, 2 + n % 2].bitcast(F16)
                w, first = n // (2 * PIECES), n % (2 * PIECES) * 8
                for i in range(8):
                    mm = nc.tensor.transpose(out[:, i * P:(i + 1) * P],
                                             ternary[w][:, (first + i) * P:(first + i + 1) * P], ident16[:])
                mm.then_inc(turned, 1)

        @block.scalar
        def _(act):
            for n in range(4 * PIECES):
                act.wait_ge(turned, n + 1)
                src = banks[:, 2 + n % 2].bitcast(F16)
                m = n % (2 * PIECES)
                if n < 2 * PIECES:
                    out = fcT[:].rearrange("p k (o q) -> p o k q", q=P)[:, 2 * m:2 * m + 2]
                    src = src.rearrange("p (o k q) -> p o k q", o=2, k=KX)
                    for o in range(2):
                        ins = nc.scalar.copy(out[:, o], src[:, o])
                else:
                    out = projT[:, m % 2 * 8:m % 2 * 8 + 8, m // 2 * P:(m // 2 + 1) * P]
                    ins = nc.scalar.copy(out, src.rearrange("p (k q) -> p k q", k=8))
                ins.then_inc(saved, 1)
            act.wait_ge(saved, 4 * PIECES)


def mix(nc, x, wout, bout, ident, ident16, o_all, gammas, x1, uT, row_scale):
    with ExitStack() as stack:
        sb, pb, sem = allocators(nc, stack, "mix")
        x_in = sb("x_in", [P, TURN, DIM], F32)
        o_in = sb("o_in", [P, 2, HG, P], F32)
        wout_sb = sb("wout_sb", [P, KX, DIM], F32)
        bout_sb = sb("bout_sb", [P, DIM], F32)
        x_bias = sb("x_bias", [P, 2, DIM], F32)
        inverse = sb("inverse", [P, HEADS], F32)
        attn = sb("attn", [P, 2, DIM], F32)
        attnT = sb("attnT", [P, 2, DIM], F32)
        stats = sb("stats", [P, 6], F32)
        moments = sb("moments", [P, 2, 2], F32)
        powers = sb("powers", [P, 2, 6], F32)
        gamma_128 = sb("gamma_128", [P, 1], F32)
        half_power = sb("half_power", [P, 1], F32)
        centred = sb("centred", [P, DIM], F32)
        absmax = sb("absmax", [P, 4], F32)
        u = sb("u", [P, DIM], F32)
        u_parts = sb("u_parts", [P, 2, 2, DIM], F16)
        banks = pb("banks", [P, 8, DIM], F32)
        rows_bank, attnT_bank, y_bank, uT_bank = banks[:, 0:2], banks[:, 2], banks[:, 3], banks[:, 4].bitcast(F16)

        x_in_loaded = [sem(f"x_in_loaded_{i}") for i in range(TURN)]
        o_in_loaded = [sem(f"o_in_loaded_{i}") for i in range(2)]
        wout_loaded, bout_loaded, power_set = sem("wout_loaded"), sem("bout_loaded"), sem("power_set")
        rows_ready, inverse_ready, attn_ready = sem("rows_ready"), sem("inverse_ready"), sem("attn_ready")
        attn_turned, attnT_saved, y_ready = sem("attn_turned"), sem("attnT_saved"), sem("y_ready")
        x_bias_ready, x1_ready, stats_done, stats_ready = (
            sem("x_bias_ready"), sem("x1_ready"), sem("stats_done"), sem("stats_ready"))
        spread_step, spread_ready, scale_ready = sem("spread_step"), sem("spread_ready"), sem("scale_ready")
        quant_step, u_step, u_ready, u_turned, uT_saved = (
            sem("quant_step"), sem("u_step"), sem("u_ready"), sem("u_turned"), sem("uT_saved"))
        waited = sem("waited")
        block = stack.enter_context(nc.Block())

        @block.sync
        def _(sp):
            x_rows = x.rearrange("b (c p) d -> (b c) p d", p=P)
            sp.dma_start(bout_sb[:], bout.rearrange("(a d) -> a d", a=1).to_broadcast([P, DIM])
                         ).then_inc(bout_loaded, 16)

            def load(at):
                need(sp, x_bias_ready, at.n - TURN + 1)
                sp.dma_start(x_in[:, at.slot(TURN)], x_rows[at.n]).then_inc(x_in_loaded[at.slot(TURN)], 16)
                need(sp, rows_ready, at.n - 1)
                c = at.slot(CHUNKS)
                sp.dma_start(o_in[:, at.slot(2)],
                             o_all[:].rearrange("p (b g) q -> p b g q", b=BATCH)[:, at.quad, :, c * P:(c + 1) * P]
                             ).then_inc(o_in_loaded[at.slot(2)], 16)

            load(At(0, 0))
            sp.dma_start(wout_sb[:], wout.rearrange("(k p) n -> p k n", p=P)).then_inc(wout_loaded, 16)
            for s in range(1, TURN):
                load(At(0, s))
            run_steps(sp, TILES - TURN, 0, 0, lambda at: load(at.back(-TURN)))

        @block.tensor
        def _(pe):
            def turn_sums(at):
                need(pe, attn_ready, at.n)
                pe.wait_ge(o_in_loaded[at.slot(2)], at.use_of_two * 16)
                for g in range(HG):
                    mm = nc.tensor.transpose(rows_bank[:, g // 4, g % 4 * P:(g % 4 + 1) * P],
                                             o_in[:, at.slot(2), g, :], ident[:])
                mm.then_inc(rows_ready, 1)

            def turn_attn(at):
                pe.wait_ge(attn_ready, at.n + 1)
                need(pe, attnT_saved, at.n)
                for k in range(KX):
                    mm = nc.tensor.transpose(attnT_bank[:, k * P:(k + 1) * P],
                                             attn[:, at.slot(2), k * P:(k + 1) * P], ident[:])
                mm.then_inc(attn_turned, 1)

            def project_out(at):
                pe.wait_ge(attnT_saved, at.n + 1)
                need(pe, x1_ready, at.n)
                for k in range(KX):
                    mm = nc.tensor.matmul(y_bank, attnT[:, at.slot(2), k * P:(k + 1) * P], wout_sb[:, k, :],
                                          start=(k == 0), stop=(k == KX - 1))
                mm.then_inc(y_ready, 1)

            def turn_u(at):
                pe.wait_ge(u_ready, at.n + 1)
                need(pe, uT_saved, at.n)
                for part in range(2):
                    for k in range(KX):
                        i = part * KX + k
                        mm = nc.tensor.transpose(uT_bank[:, i * P:(i + 1) * P],
                                                 u_parts[:, at.slot(2), part, k * P:(k + 1) * P], ident16[:])
                mm.then_inc(u_turned, 1)

            pe.wait_ge(wout_loaded, 16)

            def step(at):
                if at.within(TILES):
                    turn_sums(at)
                if at.back(1).within(TILES):
                    turn_attn(at.back(1))
                if at.back(4).within(TILES):
                    turn_u(at.back(4))
                if at.back(2).within(TILES):
                    project_out(at.back(2))

            run_steps(pe, TILES, 4, 5, step)

        @block.vector
        def _(dve):
            def divide(at):
                rows = rows_bank.rearrange("p a (m e) -> p (a m) e", e=2 * HEAD)
                dve.wait_ge(rows_ready, at.n + 1)
                dve.reciprocal(inverse[:], rows[:, :, HEAD]).then_inc(inverse_ready, 1)
                dve.wait_ge(inverse_ready, at.n + 1)
                need(dve, attn_turned, at.n - 1)
                dve.tensor_tensor(attn[:, at.slot(2)].rearrange("p (m d) -> p m d", d=HEAD), rows[:, :, 0:HEAD],
                                  inverse[:].unsqueeze(2).to_broadcast([P, HEADS, HEAD]), ALU.mult
                                  ).then_inc(attn_ready, 1)

            def add_residual(at):
                dve.wait_ge(y_ready, at.n + 1)
                dve.wait_ge(x_bias_ready, at.n + 1)
                dve.tensor_tensor(x1[:, at.n], y_bank, x_bias[:, at.slot(2)], ALU.add).then_inc(x1_ready, 1)
                need_apart(dve, x1_ready, at.n + 1, waited)
                dve.bn_stats(stats[:], x1[:, at.n]).then_inc(stats_done, 1)
                need_apart(dve, stats_done, at.n + 1, waited)
                need_apart(dve, scale_ready, at.n - 1, waited)
                dve.bn_aggr(moments[:, at.slot(2)], stats[:]).then_inc(stats_ready, 1)

            def quantise(at):
                r, steps = at.slot(2), at.n * 5
                dve.wait_ge(stats_ready, at.n + 1)
                dve.tensor_scalar(centred[:], x1[:, at.n], moments[:, r, 0:1], None, ALU.subtract
                                  ).then_inc(quant_step, 1)
                dve.wait_ge(quant_step, steps + 1)
                dve.tensor_reduce(absmax[:, 0:1], centred[:], AX.X, ALU.max, apply_absolute_value=True
                                  ).then_inc(quant_step, 1)
                dve.wait_ge(quant_step, steps + 2)
                dve.reciprocal(absmax[:, 1:2], absmax[:, 0:1]).then_inc(quant_step, 1)
                dve.wait_ge(quant_step, steps + 3)
                dve.tensor_scalar(absmax[:, 2:3], absmax[:, 1:2], Q_B, None, ALU.mult).then_inc(quant_step, 1)
                dve.wait_ge(spread_ready, at.n + 1)
                dve.scalar_tensor_tensor(absmax[:, 3:4], absmax[:, 1:2], 0.0, powers[:, r, 5:6], ALU.mult, ALU.add
                                         ).then_inc(quant_step, 1)
                dve.wait_ge(quant_step, steps + 5)
                dve.tensor_scalar(u[:], centred[:], absmax[:, 2:3], Q_B, ALU.mult, ALU.min).then_inc(u_step, 1)
                dve.scalar_tensor_tensor(row_scale[:, at.n], absmax[:, 0:1], absmax[:, 3:4], gamma_128[:],
                                         ALU.mult, ALU.mult).then_inc(scale_ready, 1)
                need(dve, u_turned, at.n - 1)
                dve.wait_ge(u_step, at.n * 2 + 1)
                dve.tensor_scalar(u_parts[:, r, 0], u[:], -Q_B, None, ALU.max).then_inc(u_step, 1)
                dve.wait_ge(u_step, at.n * 2 + 2)
                dve.scalar_tensor_tensor(u_parts[:, r, 1], u[:], -Q_B, u_parts[:, r, 0], ALU.max, ALU.subtract
                                         ).then_inc(u_ready, 1)

            dve.tensor_scalar(gamma_128[:], gammas[:, 0:1], 1 / Q_B, None, ALU.mult)

            def step(at):
                if at.back(3).within(TILES):
                    quantise(at.back(3))
                if at.within(TILES):
                    divide(at)
                if at.back(2).within(TILES):
                    add_residual(at.back(2))

            run_steps(dve, TILES, 3, 5, step)

        @block.scalar
        def _(act):
            def save_attn(at):
                act.wait_ge(attn_turned, at.n + 1)
                need(act, y_ready, at.n - 1)
                nc.scalar.copy(attnT[:, at.slot(2)], attnT_bank).then_inc(attnT_saved, 1)

            def save_u(at):
                need_apart(act, u_turned, at.n + 1, waited)
                nc.scalar.copy(uT[:, at.n], uT_bank).then_inc(uT_saved, 1)

            def step(at):
                if at.back(1).within(TILES):
                    save_attn(at.back(1))
                if at.back(4).within(TILES):
                    save_u(at.back(4))

            run_steps(act, TILES, 4, 5, step)

        @block.gpsimd
        def _(pool):
            def add_bias(at):
                pool.wait_ge(x_in_loaded[at.slot(TURN)], at.quad * 16 + 16)
                need(pool, x1_ready, at.n - 1)
                pool.tensor_tensor(x_bias[:, at.slot(2)], x_in[:, at.slot(TURN)], bout_sb[:], ALU.add
                                   ).then_inc(x_bias_ready, 1)

            def spread(at):
                r = at.slot(2)
                now = lambda i: powers[:, r, i:i + 1]
                count = [0]

                def then(ins):
                    count[0] += 1
                    ins.then_inc(spread_step, 1)
                    need_apart(pool, spread_step, at.n * 6 + count[0], waited)

                need_apart(pool, stats_ready, at.n + 1, waited)
                need_apart(pool, scale_ready, at.n - 1, waited)
                then(pool.tensor_scalar(now(0), moments[:, r, 1:2], LN_EPS, None, ALU.add))
                then(pool.tensor_tensor(now(1), now(0), half_power[:], ALU.pow))
                then(pool.tensor_tensor(now(2), now(1), now(1), ALU.mult))
                then(pool.tensor_tensor(now(3), now(2), moments[:, r, 1:2], ALU.mult))
                then(pool.tensor_scalar(now(3), now(3), FFN_EPS, None, ALU.add))
                then(pool.tensor_tensor(now(4), now(3), half_power[:], ALU.pow))
                pool.tensor_tensor(now(5), now(4), now(1), ALU.mult).then_inc(spread_ready, 1)

            pool.memset(half_power[:], -0.5).then_inc(power_set, 1)
            pool.wait_ge(power_set, 1)
            pool.wait_ge(bout_loaded, 16)

            def step(at):
                if at.within(TILES):
                    add_bias(at)
                if at.back(2).within(TILES):
                    spread(at.back(2))

            run_steps(pool, TILES, 2, 5, step)


def ffn(nc, ident16, o_all, uT, row_scale, gammas, x1, fcT, projT, out):
    with ExitStack() as stack:
        sb, pb, sem = allocators(nc, stack, "ffn")
        spare = o_all[:].rearrange("p g q -> p (g q)")
        h = spare[:, 0:2 * FFN].rearrange("p (s c) -> p s c", s=2)
        h_parts = spare[:, 2 * FFN:4 * FFN].bitcast(F16).rearrange("p (s t c) -> p s t c", s=2, t=2)
        hT = spare[:, 4 * FFN:6 * FFN].bitcast(F16).rearrange("p (s j k r) -> p s j k r", s=2, j=4, r=P)
        stats = sb("stats", [P, FFN // DIM, 6], F32)
        moments = sb("moments", [P, 2, 2], F32)
        powers = sb("powers", [P, 2, 2], F32)
        half_power = sb("half_power", [P, 1], F32)
        absmax = sb("absmax", [P, 4], F32)
        out_scale = sb("out_scale", [P, TURN, 1], F32)
        gamma_128 = sb("gamma_128", [P, 1], F32)
        y = sb("y", [P, 2, DIM], F32)
        banks = pb("banks", [P, 8, DIM], F32)

        fc_ready, h_ready = sem("fc_ready"), sem("h_ready")
        stats_done, stats_ready, eps_added, spread_ready, power_set = (
            sem("stats_done"), sem("stats_ready"), sem("eps_added"), sem("spread_ready"), sem("power_set"))
        quant_step, gamma_set, parts_ready, scale_ready = (
            sem("quant_step"), sem("gamma_set"), sem("parts_ready"), sem("scale_ready"))
        h_turned, hT_saved, proj_ready, y_ready = sem("h_turned"), sem("hT_saved"), sem("proj_ready"), sem("y_ready")
        out_stored = [sem(f"out_stored_{i}") for i in range(2)]
        QUARTERS = FFN // DIM
        waited = sem("waited")
        block = stack.enter_context(nc.Block())

        @block.sync
        def _(sp):
            out_rows = out.rearrange("b (c p) d -> (b c) p d", p=P)

            def store(at):
                sp.wait_ge(y_ready, at.n + 1)
                sp.dma_start(out_rows[at.n], y[:, at.slot(2)]).then_inc(out_stored[at.slot(2)], 16)

            run_steps(sp, TILES, 0, 4, store)
            for i in range(2):
                sp.wait_ge(out_stored[i], 16 * TILES // 2)

        @block.tensor
        def _(pe):
            def expand(at, o):
                need(pe, h_ready, (at.n - 1) * QUARTERS + o + 1)
                for k in range(KX):
                    for part in range(2):
                        mm = nc.tensor.matmul(banks[:, o], uT[:, at.n, (part * KX + k) * P:(part * KX + k + 1) * P],
                                              fcT[:, k, o * DIM:(o + 1) * DIM],
                                              start=(k + part == 0), stop=(k == KX - 1 and part == 1))
                mm.then_inc(fc_ready, 1)

            def turn_h(at, j):
                if j == 0:
                    pe.wait_ge(parts_ready, at.n + 1)
                need(pe, hT_saved, at.n * 4 + j - 1)
                for i in range(8):
                    first = (j % 2 * 8 + i) * P
                    mm = nc.tensor.transpose(banks[:, 4 + j % 2].bitcast(F16)[:, i * P:(i + 1) * P],
                                             h_parts[:, at.slot(2), j // 2, first:first + P], ident16[:])
                mm.then_inc(h_turned, 1)

            def contract(at):
                pe.wait_ge(hT_saved, at.n * 4 + 4)
                need(pe, y_ready, at.n - 1)
                for k in range(KF):
                    for part in range(2):
                        mm = nc.tensor.matmul(banks[:, 6 + at.slot(2)],
                                              hT[:, at.slot(2), part * 2 + k // 8, k % 8, :], projT[:, k, :],
                                              start=(k + part == 0), stop=(k == KF - 1 and part == 1))
                mm.then_inc(proj_ready, 1)

            def step(at):
                before = at.back(2)
                for half in range(2):
                    if before.within(TILES):
                        turn_h(before, 2 * half)
                        turn_h(before, 2 * half + 1)
                    if at.within(TILES):
                        expand(at, 2 * half)
                        expand(at, 2 * half + 1)
                if before.within(TILES):
                    contract(before)

            run_steps(pe, TILES, 2, 5, step)

        @block.scalar
        def _(act):
            def activate(at, o):
                need_apart(act, fc_ready, at.n * QUARTERS + o + 1, waited)
                if o == 0:
                    need_apart(act, parts_ready, at.n - 1, waited)
                nc.scalar.activation(h[:, at.slot(2), o * DIM:(o + 1) * DIM], banks[:, o], ACT.Gelu,
                                     scale=row_scale[:, at.n]).then_inc(h_ready, 1)

            def save_turned(at, j):
                act.wait_ge(h_turned, at.n * 4 + j + 1)
                need(act, proj_ready, at.n - 1)
                nc.scalar.copy(hT[:, at.slot(2), j].rearrange("p k r -> p (k r)"),
                               banks[:, 4 + j % 2].bitcast(F16)).then_inc(hT_saved, 1)

            def step(at):
                before = at.back(2)
                for half in range(2):
                    if before.within(TILES):
                        save_turned(before, 2 * half)
                        save_turned(before, 2 * half + 1)
                    if at.within(TILES):
                        activate(at, 2 * half)
                        activate(at, 2 * half + 1)

            run_steps(act, TILES, 2, 5, step)

        @block.vector
        def _(dve):
            def statistics(at):
                r = at.slot(2)
                for o in range(QUARTERS):
                    dve.wait_ge(h_ready, at.n * QUARTERS + o + 1)
                    dve.bn_stats(stats[:, o], h[:, r, o * DIM:(o + 1) * DIM]).then_inc(stats_done, 1)
                need_apart(dve, stats_done, at.n * QUARTERS + QUARTERS, waited)
                dve.bn_aggr(moments[:, r], stats[:].rearrange("p o s -> p (o s)")).then_inc(stats_ready, 1)

            def quantise(at):
                r, steps = at.slot(2), at.n * 7
                now = h[:, r, :]
                dve.wait_ge(stats_ready, at.n + 1)
                dve.tensor_scalar(now, now, moments[:, r, 0:1], None, ALU.subtract).then_inc(quant_step, 1)
                dve.wait_ge(quant_step, steps + 1)
                dve.tensor_reduce(absmax[:, 0:1], now, AX.X, ALU.max, apply_absolute_value=True
                                  ).then_inc(quant_step, 1)
                dve.wait_ge(quant_step, steps + 2)
                dve.reciprocal(absmax[:, 1:2], absmax[:, 0:1]).then_inc(quant_step, 1)
                dve.wait_ge(quant_step, steps + 3)
                dve.tensor_scalar(absmax[:, 2:3], absmax[:, 1:2], Q_B, None, ALU.mult).then_inc(quant_step, 1)
                dve.wait_ge(spread_ready, at.n + 1)
                dve.scalar_tensor_tensor(absmax[:, 3:4], absmax[:, 1:2], 0.0, powers[:, r, 1:2], ALU.mult, ALU.add
                                         ).then_inc(quant_step, 1)
                dve.wait_ge(quant_step, steps + 5)
                dve.tensor_scalar(now, now, absmax[:, 2:3], Q_B, ALU.mult, ALU.min).then_inc(quant_step, 1)
                dve.scalar_tensor_tensor(out_scale[:, at.slot(TURN)], absmax[:, 0:1], absmax[:, 3:4], gamma_128[:],
                                         ALU.mult, ALU.mult).then_inc(scale_ready, 1)
                need(dve, h_turned, (at.n - 1) * 4)
                dve.wait_ge(quant_step, steps + 6)
                dve.tensor_scalar(h_parts[:, r, 0], now, -Q_B, None, ALU.max).then_inc(quant_step, 1)
                dve.wait_ge(quant_step, steps + 7)
                dve.scalar_tensor_tensor(h_parts[:, r, 1], now, -Q_B, h_parts[:, r, 0], ALU.max, ALU.subtract
                                         ).then_inc(parts_ready, 1)

            def finish(at):
                r = at.slot(2)
                dve.wait_ge(proj_ready, at.n + 1)
                dve.wait_ge(scale_ready, at.n + 1)
                before = at.back(2)
                if before.looped or before.n >= 0:
                    dve.wait_ge(out_stored[r], before.use_of_two * 16)
                dve.scalar_tensor_tensor(y[:, r], banks[:, 6 + r], out_scale[:, at.slot(TURN)], x1[:, at.n],
                                         ALU.mult, ALU.add).then_inc(y_ready, 1)

            dve.tensor_scalar(gamma_128[:], gammas[:, 1:2], 1 / Q_B, None, ALU.mult).then_inc(gamma_set, 1)
            dve.wait_ge(gamma_set, 1)

            def step(at):
                if at.back(3).within(TILES):
                    finish(at.back(3))
                if at.back(1).within(TILES):
                    statistics(at.back(1))
                    quantise(at.back(1))

            run_steps(dve, TILES, 3, 5, step)

        @block.gpsimd
        def _(pool):
            def spread(at):
                r = at.slot(2)
                need_apart(pool, stats_ready, at.n + 1, waited)
                need_apart(pool, scale_ready, at.n - 1, waited)
                pool.tensor_scalar(powers[:, r, 0:1], moments[:, r, 1:2], FFN_EPS, None, ALU.add
                                   ).then_inc(eps_added, 1)
                pool.wait_ge(eps_added, at.n + 1)
                pool.tensor_tensor(powers[:, r, 1:2], powers[:, r, 0:1], half_power[:], ALU.pow
                                   ).then_inc(spread_ready, 1)

            pool.memset(half_power[:], -0.5).then_inc(power_set, 1)
            pool.wait_ge(power_set, 1)
            run_steps(pool, TILES, 0, 4, spread)


def xattn_ffn(nc, x, ctx, pos, wq, wkv, wout, bout, w_fc, w_proj, out):
    q_parts = nc.dram_tensor("q_parts", [GROUPS, PARTS, GW, SEQ], BF16).ap()
    k_parts = nc.dram_tensor("k_parts", [GROUPS, PARTS, GW, SEQ], BF16).ap()
    with ExitStack() as stack:
        sb, _, sem = allocators(nc, stack, "xattn_ffn")
        ident = sb("ident", [P, P], F32)
        identh = sb("identh", [P, P], F16)
        identb = sb("identb", [P, P], BF16)
        filled = sem("filled")
        with nc.Block() as block:

            @block.gpsimd
            def _(pool):
                for n, square in enumerate((ident, identh, identb)):
                    pool.memset(square[:], 0.0).then_inc(filled, 1)
                    pool.wait_ge(filled, 2 * n + 1)
                    pool.affine_select(out=square[:], in_=square[:], compare_op=ALU.not_equal, fill=1.0, base=0,
                                       pattern=[[-1, P]], channel_multiplier=1).then_inc(filled, 1)

        with ExitStack() as attention:
            sb2, _, _ = allocators(nc, attention, "kept")
            o_all = sb2("o_all", [P, GROUPS, SEQ], F32)
            with nc.sbuf_tensor("v_all", [P, GROUPS, CHUNKS, GW], F32) as v_all:
                project(nc, x, ctx, pos, wq, wkv, ident, v_all, q_parts, k_parts)
                attend(nc, identb, v_all, q_parts, k_parts, o_all)
            fcT = sb2("fcT", [P, KX, FFN], F16)
            projT = sb2("projT", [P, KF, DIM], F16)
            gammas = sb2("gammas", [P, 2], F32)
            ternarise(nc, w_fc, w_proj, identh, fcT, projT, gammas)
            x1 = sb2("x1", [P, TILES, DIM], F32)
            uT = sb2("uT", [P, TILES, 2 * DIM], F16)
            row_scale = sb2("row_scale", [P, TILES, 1], F32)
            mix(nc, x, wout, bout, ident, identh, o_all, gammas, x1, uT, row_scale)
            ffn(nc, identh, o_all, uT, row_scale, gammas, x1, fcT, projT, out)


_INS = ["x", "ctx_1024", "fside_BxSx2_0", "L0_xattn_Wq", "L0_xattn_Wkv", "L0_xattn_Wout", "L0_xattn_bout",
        "L0_ffn_w_fc", "L0_ffn_w_proj"]
_OUTS = [((BATCH, SEQ, DIM), "float32")]


def kernel(**inputs):
    import numpy as _np
    import concourse.bacc as _bacc
    from concourse import mybir as _mybir
    from concourse.bass_utils import run_bass_kernel_spmd as _run

    nc = _bacc.Bacc("TRN2", target_bir_lowering=False, num_devices=1)
    arrays, args = {}, []
    for name in _INS:
        a = _np.ascontiguousarray(inputs[name])
        arrays[f"in_{name}_dram"] = a
        args.append(nc.dram_tensor(f"in_{name}_dram", a.shape, _mybir.dt.from_np(a.dtype), kind="ExternalInput").ap())
    for i, (shape, dtype) in enumerate(_OUTS):
        dt = _mybir.dt.from_np(_np.dtype(dtype))
        args.append(nc.dram_tensor(f"out_{i}_dram", shape, dt, kind="ExternalOutput").ap())
    xattn_ffn(nc, *args)
    r = _run(nc, [arrays], core_ids=[0])
    got = tuple(r.results[0][f"out_{i}_dram"] for i in range(len(_OUTS)))
    return got[0]
```

```python
import math
from contextlib import ExitStack

import concourse.bass as bass
from concourse import mybir

F32 = mybir.dt.float32
BF16 = mybir.dt.bfloat16
F16 = mybir.dt.float16
ACT = mybir.ActivationFunctionType
ALU = mybir.AluOpType
AX = mybir.AxisListType

P = 128
BATCH, SEQ, DIM, CTX = 4, 512, 512, 256
HEADS, HEAD = 32, 16
FFN = 4 * DIM
ROWS = BATCH * SEQ
TILES = ROWS // P
CHUNKS = SEQ // P
KX, KC = DIM // P, CTX // P
KF = FFN // P
GH = 4
HG = HEADS // GH
GROUPS = BATCH * HG
GW = GH * HEAD
PARTS = 3
STACK = 6 * HEAD
AXES, FREQS = 2, 4
ANGLES = AXES * FREQS
LN_EPS, FFN_EPS = 1e-5, 1e-6
Q_B = 128.0
ROUNDER = 1.5 * 2.0 ** 23
TWO_PI_HIGH = 6.28125
TWO_PI_LOW = 2 * math.pi - TWO_PI_HIGH
PI_BELOW = 3.1415925
TURN = 4


class At:

    def __init__(self, turn, k):
        self.turn, self.k = turn, k
        self.looped = not isinstance(turn, int)
        self.n = turn * TURN + k
        self.quad = turn + k // TURN

    def back(self, by):
        return At(self.turn, self.k - by)

    def within(self, count):
        return self.looped or 0 <= self.k < count

    @property
    def use_of_two(self):
        return self.turn * 2 + self.k // 2 + 1

    def slot(self, m):
        return self.k % m


def run_steps(eng, count, later, head, step):
    for s in range(head):
        step(At(0, s))
    turns = (count - head) // TURN
    with eng.Fori(0, turns) as turn:
        for u in range(TURN):
            step(At(turn, head + u))
    for s in range(head + turns * TURN, count + later):
        step(At(0, s))


def need(eng, semaphore, value):
    if not isinstance(value, int) or value > 0:
        eng.wait_ge(semaphore, value)


def need_apart(eng, semaphore, value, over):
    if not isinstance(value, int) or value > 0:
        eng.wait_ge(semaphore, value).then_inc(over, 1)


def allocators(nc, stack, stage):

    def sb(name, shape, dt):
        return stack.enter_context(nc.sbuf_tensor(f"{stage}_{name}", shape, dt))

    def pb(name, shape, dt):
        return stack.enter_context(nc.psum_tensor(f"{stage}_{name}", shape, dt))

    def sem(name):
        return stack.enter_context(nc.semaphore(f"{stage}_{name}"))

    return sb, pb, sem


def project(nc, x, ctx, pos, wq, wkv, w_fc, w_proj, ident, spare, v_all, gammas, limits, q_parts, k_parts):
    with ExitStack() as stack:
        sb, pb, sem = allocators(nc, stack, "project")
        ctx_sb = sb("ctx_sb", [P, TURN, CTX], F32)
        w_raw = spare[:, 0:KX]
        wk_raw = spare[:, KX:KX + KC]
        ffn_piece = spare[:, 8:8 + 2 * TURN].rearrange("p (i w) d -> p i w d", w=2)
        ffn_abs = spare[:, 16:18]
        x_sb = spare[:, 18:18 + TURN]
        abs_sums = sb("abs_sums", [P, 2, TILES], F32)
        abs_sum = sb("abs_sum", [P, 2], F32)
        gamma_eps = sb("gamma_eps", [P, 2], F32)
        ones = sb("ones", [P, P], F32)
        wq_sb = sb("wq_sb", [P, KX, DIM], F32)
        wk_sb = sb("wk_sb", [P, KC, DIM], F32)
        wv_sb = sb("wv_sb", [P, KC, DIM], F32)
        pos_sb = sb("pos_sb", [P, TILES, AXES], F32)
        angle = sb("angle", [P, TILES, AXES, FREQS], F32)
        whole = sb("whole", [P, TILES * ANGLES], F32)
        over = sb("over", [P, TILES * ANGLES], F32)
        shifted = sb("shifted", [P, TILES * ANGLES], F32)
        cosine = sb("cosine", [P, TILES, ANGLES, 2], F32)
        sine = sb("sine", [P, TILES, ANGLES], F32)
        neg_sine = sb("neg_sine", [P, TILES, ANGLES], F32)
        stats = sb("stats", [P, 2, 6], F32)
        moments = sb("moments", [P, 2, 2], F32)
        half_power = sb("half_power", [P, 1], F32)
        rstd = sb("rstd", [P, 2, 2], F32)
        xn = sb("xn", [P, 2, DIM], F32)
        xT = sb("xT", [P, 2, DIM], F32)
        ctxT = sb("ctxT", [P, 2, CTX], F32)
        straight = [sb(f"straight_{s}", [P, DIM], F32) for s in "kq"]
        crossed = [sb(f"crossed_{s}", [P, DIM], F32) for s in "kq"]
        rotated = [sb(f"rotated_{s}", [P, DIM], F32) for s in "kq"]
        rest = [sb(f"rest_{s}", [P, DIM], F32) for s in "kq"]
        parts = sb("parts", [P, 2, 2, PARTS, KX, 2 * P], BF16)
        banks = pb("banks", [P, 8, DIM], F32)
        xT_bank, ctxT_bank, v_bank = banks[:, 0], banks[:, 1, 0:CTX], banks[:, 2]
        in_bank = [banks[:, 3], banks[:, 4]]
        turned_bank = [banks[:, 5], banks[:, 6]]

        w_loaded = {w: sem(f"{w}_loaded") for w in ("wk", "wv", "wq", "pos")}
        x_loaded = [sem(f"x_loaded_{i}") for i in range(TURN)]
        ctx_loaded = [sem(f"ctx_loaded_{i}") for i in range(TURN)]
        w_ordered = sem("w_ordered")
        piece_loaded = [sem(f"piece_loaded_{i}") for i in range(TURN)]
        piece_summed, ones_ready, abs_summed, total_ready, gamma_step = (
            sem("piece_summed"), sem("ones_ready"), sem("abs_summed"), sem("total_ready"), sem("gamma_step"))
        tables_step, angles_ready, sines_ready, tables_ready = (
            sem("tables_step"), sem("angles_ready"), sem("sines_ready"), sem("tables_ready"))
        stats_done, stats_ready, power_ready, rstd_ready = (
            sem("stats_done"), sem("stats_ready"), sem("power_ready"), sem("rstd_ready"))
        xn_ready, x_turned, ctx_turned, xT_saved, ctxT_saved = (
            sem("xn_ready"), sem("x_turned"), sem("ctx_turned"), sem("xT_saved"), sem("ctxT_saved"))
        v_projected, v_saved = sem("v_projected"), sem("v_saved")
        projected = [sem(f"{s}_projected") for s in "kq"]
        multiplied = [sem(f"{s}_multiplied") for s in "kq"]
        summed = [sem(f"{s}_summed") for s in "kq"]
        turned = [sem(f"{s}_turned") for s in "kq"]
        first_done = [sem(f"{s}_first_done") for s in "kq"]
        rest_done = [sem(f"{s}_rest_done") for s in "kq"]
        second_done = [sem(f"{s}_second_done") for s in "kq"]
        third_done = [sem(f"{s}_third_done") for s in "kq"]
        parts_stored = [sem(f"parts_stored_{i}") for i in range(2)]
        PAIR_STORES = 16 * 2 * 2 * PARTS
        START = 1

        waited = sem("waited")
        block = stack.enter_context(nc.Block())

        @block.sync
        def _(sp):
            x_rows = x.rearrange("b (c p) d -> (b c) p d", p=P)
            ctx_rows = ctx.rearrange("b (c p) d -> (b c) p d", p=P)
            wkv_rows = wkv.rearrange("(k p) n -> p k n", p=P)

            def load_ctx(at):
                need(sp, ctx_turned, at.n - TURN + 1)
                sp.dma_start(ctx_sb[:, at.slot(TURN)], ctx_rows[at.n]).then_inc(ctx_loaded[at.slot(TURN)], 16)

            def load_x(at):
                need(sp, xn_ready, at.n - TURN + 1)
                sp.dma_start(x_sb[:, at.slot(TURN)], x_rows[at.n]).then_inc(x_loaded[at.slot(TURN)], 16)

            def load_piece(at):
                i = at.slot(TURN)
                need(sp, piece_summed, (at.n - TURN + 1) * 2)
                sp.dma_start(ffn_piece[:, i, 0], w_fc.rearrange("(o p) d -> o p d", p=P)[at.n]
                             ).then_inc(piece_loaded[i], 16)
                sp.dma_start(ffn_piece[:, i, 1],
                             w_proj.rearrange("(o p) d -> o p d", p=P)[at.quad, :, i * DIM:(i + 1) * DIM]
                             ).then_inc(piece_loaded[i], 16)

            load_ctx(At(0, 0))
            sp.dma_start(wk_raw, wkv_rows[:, :, 0:DIM]).then_inc(w_loaded["wk"], 16)
            load_x(At(0, 0))
            sp.dma_start(wv_sb[:], wkv_rows[:, :, DIM:2 * DIM]).then_inc(w_loaded["wv"], 16)
            sp.dma_start(w_raw, wq.rearrange("(k p) n -> p k n", p=P)).then_inc(w_loaded["wq"], 16)
            sp.dma_start(pos_sb[:], pos.rearrange("b (c p) a -> p (b c) a", p=P)).then_inc(w_loaded["pos"], 16)

            def store(at):
                pair = at.slot(4) // 2
                for s, where in ((0, k_parts), (1, q_parts)):
                    view = where.rearrange("(b k g) t e c -> b g t e k c", b=BATCH, k=KX)
                    sp.wait_ge(second_done[s], at.n + 1)
                    sp.wait_ge(third_done[s], at.n + 1)
                    for part in range(PARTS):
                        for g in range(2):
                            sp.dma_start(view[at.quad, g, part, :, :, pair * 2 * P:(pair + 1) * 2 * P],
                                         parts[g * GW:(g + 1) * GW, pair, s, part]).then_inc(parts_stored[pair], 16)

            def step(at):
                if at.within(TILES) and not (isinstance(at.n, int) and at.n == 0):
                    load_ctx(at)
                    load_x(at)
                if at.back(2).within(TILES):
                    load_piece(at.back(2))
                if at.back(6).within(TILES) and at.back(6).slot(2) == 1:
                    store(at.back(6))

            run_steps(sp, TILES, 6, 8, step)
            for pair in range(2):
                sp.wait_ge(parts_stored[pair], PAIR_STORES * BATCH + START)

        @block.tensor
        def _(pe):
            def turn_inputs(at):
                r = at.slot(2)
                pe.wait_ge(ctx_loaded[at.slot(TURN)], at.quad * 16 + 16)
                need(pe, ctxT_saved, at.n)
                for k in range(KC):
                    mm = nc.tensor.transpose(ctxT_bank[:, k * P:(k + 1) * P],
                                             ctx_sb[:, at.slot(TURN), k * P:(k + 1) * P], ident[:])
                mm.then_inc(ctx_turned, 1)
                pe.wait_ge(xn_ready, at.n + 1)
                need(pe, xT_saved, at.n)
                for k in range(KX):
                    mm = nc.tensor.transpose(xT_bank[:, k * P:(k + 1) * P], xn[:, r, k * P:(k + 1) * P], ident[:])
                mm.then_inc(x_turned, 1)

            def product(out, lhs, rhs, blocks, done):
                for k in range(blocks):
                    mm = nc.tensor.matmul(out, lhs[:, k * P:(k + 1) * P], rhs[:, k, :],
                                          start=(k == 0), stop=(k == blocks - 1))
                mm.then_inc(done, 1)

            def project_kv(at):
                r = at.slot(2)
                pe.wait_ge(ctxT_saved, at.n + 1)
                need(pe, multiplied[0], at.n)
                product(in_bank[0], ctxT[:, r], wk_sb, KC, projected[0])
                need(pe, v_saved, at.n)
                product(v_bank, ctxT[:, r], wv_sb, KC, v_projected)

            def project_q(at):
                pe.wait_ge(xT_saved, at.n + 1)
                need(pe, multiplied[1], at.n)
                product(in_bank[1], xT[:, at.slot(2)], wq_sb, KX, projected[1])

            def turn_rotated(at):
                for s in range(2):
                    pe.wait_ge(summed[s], at.n + 1)
                    need(pe, rest_done[s], at.n)
                    for k in range(KX):
                        mm = nc.tensor.transpose(turned_bank[s][:, k * P:(k + 1) * P],
                                                 rotated[s][:, k * P:(k + 1) * P], ident[:])
                    mm.then_inc(turned[s], 1)

            pe.wait_ge(w_ordered, 2)
            pe.wait_ge(w_loaded["wv"], 16)

            def step(at):
                if at.back(2).within(TILES):
                    turn_inputs(at.back(2))
                if at.back(3).within(TILES):
                    project_kv(at.back(3))
                if at.back(4).within(TILES):
                    turn_rotated(at.back(4))
                if at.back(3).within(TILES):
                    project_q(at.back(3))

            run_steps(pe, TILES, 4, 5, step)
            pe.wait_ge(abs_summed, 1)
            pe.wait_ge(ones_ready, 1)
            nc.tensor.matmul(ctxT_bank[:, 0:2], ones[:], abs_sum[:], start=True, stop=True).then_inc(total_ready, 1)

        @block.vector
        def _(dve):
            def weigh_ffn():
                dve.wait_ge(piece_summed, 2 * TILES)
                dve.tensor_reduce(abs_sum[:], abs_sums[:], AX.X, ALU.add).then_inc(abs_summed, 1)
                dve.wait_ge(total_ready, 1)
                dve.tensor_scalar(gammas[:], ctxT_bank[:, 0:2], 1.0 / (FFN * DIM), None, ALU.mult
                                  ).then_inc(gamma_step, 1)
                dve.wait_ge(gamma_step, 1)
                dve.tensor_scalar(gamma_eps[:], gammas[:], FFN_EPS, None, ALU.add).then_inc(gamma_step, 1)
                dve.wait_ge(gamma_step, 2)
                dve.tensor_scalar(limits[:, 0], gamma_eps[:], 0.5, None, ALU.mult)
                dve.tensor_scalar(limits[:, 1], gamma_eps[:], -0.5, None, ALU.mult)

            def make_tables():
                flat = angle[:].rearrange("p t a f -> p (t a f)")
                done = [0]

                def then(ins, more=1):
                    done[0] += more
                    ins.then_inc(tables_step, 1)

                def settled():
                    dve.wait_ge(tables_step, done[0])

                def reduce(values):
                    then(dve.tensor_scalar(whole[:], values, 1 / (2 * math.pi), ROUNDER, ALU.mult, ALU.add))
                    settled()
                    then(dve.tensor_scalar(over[:], whole[:], -ROUNDER, None, ALU.add))
                    settled()
                    then(dve.scalar_tensor_tensor(whole[:], over[:], -TWO_PI_HIGH, values, ALU.mult, ALU.add))
                    settled()
                    then(dve.scalar_tensor_tensor(values, over[:], -TWO_PI_LOW, whole[:], ALU.mult, ALU.add))
                    settled()

                def clamp(values):
                    then(dve.tensor_scalar(values, values, PI_BELOW, -PI_BELOW, ALU.min, ALU.max))

                dve.wait_ge(w_loaded["pos"], 16)
                for f in range(FREQS):
                    then(dve.tensor_scalar(angle[:, :, :, f], pos_sb[:], 10000.0 ** (-f / FREQS), None, ALU.mult))
                settled()
                reduce(flat)
                then(dve.tensor_scalar(shifted[:], flat, math.pi / 2, None, ALU.add))
                settled()
                reduce(shifted[:])
                clamp(flat)
                clamp(shifted[:])
                settled()
                dve.engine_nop().then_inc(angles_ready, 1)
                dve.wait_ge(sines_ready, 2)
                dve.tensor_scalar(neg_sine[:], sine[:], -1.0, None, ALU.mult).then_inc(tables_ready, 1)

            def statistics(at):
                r = at.slot(2)
                dve.wait_ge(x_loaded[at.slot(TURN)], at.quad * 16 + 16)
                dve.bn_stats(stats[:, r], x_sb[:, at.slot(TURN)]).then_inc(stats_done, 1)
                need_apart(dve, stats_done, at.n + 1, waited)
                need_apart(dve, xn_ready, at.n - 1, waited)
                dve.bn_aggr(moments[:, r], stats[:, r]).then_inc(stats_ready, 1)

            def normalise(at):
                r = at.slot(2)
                dve.wait_ge(rstd_ready, at.n + 1)
                need(dve, x_turned, at.n - 1)
                dve.tensor_scalar(xn[:, r], x_sb[:, at.slot(TURN)], moments[:, r, 0:1], rstd[:, r, 1:2],
                                  ALU.subtract, ALU.mult).then_inc(xn_ready, 1)

            def rope_products(at, s):
                table = lambda t, w: t.unsqueeze(1).unsqueeze(3).to_broadcast([P, HG, w, GH])
                cos = cosine[:, at.n].rearrange("p a r -> p (a r)")
                dve.wait_ge(projected[s], at.n + 1)
                need(dve, summed[s], at.n)
                view = lambda t: t.rearrange("p (g d h) -> p g d h", g=HG, h=GH)
                pairs = lambda t, r: t.rearrange("p (g a r h) -> p g a r h", g=HG, r=2, h=GH)[:, :, :, r]
                dve.tensor_tensor(view(straight[s][:]), view(in_bank[s]), table(cos, HEAD), ALU.mult)
                dve.tensor_tensor(pairs(crossed[s][:], 0), pairs(in_bank[s], 1),
                                  table(neg_sine[:, at.n], ANGLES), ALU.mult)
                dve.tensor_tensor(pairs(crossed[s][:], 1), pairs(in_bank[s], 0),
                                  table(sine[:, at.n], ANGLES), ALU.mult).then_inc(multiplied[s], 1)

            def take_first(at, s):
                dve.wait_ge(turned[s], at.n + 1)
                dve.wait_ge(first_done[s], at.n + 1)
                need(dve, second_done[s], at.n)
                need(dve, third_done[s], at.n)
                dve.tensor_tensor(rest[s][:].rearrange("p (k c) -> p k c", k=KX),
                                  turned_bank[s].rearrange("p (k c) -> p k c", k=KX),
                                  part_now(at, s, 0), ALU.subtract).then_inc(rest_done[s], 1)

            def part_now(at, s, part):
                half = at.slot(2)
                return parts[:, at.slot(4) // 2, s, part, :, half * P:(half + 1) * P]

            statistics(At(0, 0))
            make_tables()
            dve.wait_ge(tables_ready, 1)

            def step(at):
                if at.within(TILES) and not (isinstance(at.n, int) and at.n == 0):
                    statistics(at)
                if at.back(1).within(TILES):
                    normalise(at.back(1))
                if at.back(3).within(TILES):
                    rope_products(at.back(3), 0)
                if at.back(4).within(TILES):
                    take_first(at.back(4), 0)
                    take_first(at.back(4), 1)
                if at.back(3).within(TILES):
                    rope_products(at.back(3), 1)

            run_steps(dve, TILES, 4, 5, step)
            weigh_ffn()

        @block.scalar
        def _(act):
            def part_now(at, s, part):
                half = at.slot(2)
                return parts[:, at.slot(4) // 2, s, part, :, half * P:(half + 1) * P]

            def order_weights():
                order = lambda t, k: t.rearrange("p k (g h d) -> p (k g) d h", h=GH, d=HEAD)
                plain = lambda t: t.rearrange("p k (g d h) -> p (k g) d h", h=GH, d=HEAD)
                act.wait_ge(w_loaded["wk"], 16)
                nc.scalar.copy(plain(wk_sb[:]), order(wk_raw, KC)).then_inc(w_ordered, 1)
                act.wait_ge(w_loaded["wq"], 16)
                nc.scalar.copy(plain(wq_sb[:]), order(w_raw, KX)).then_inc(w_ordered, 1)

            def save_inputs(at):
                r = at.slot(2)
                act.wait_ge(ctx_turned, at.n + 1)
                need(act, v_projected, at.n - 1)
                nc.scalar.copy(ctxT[:, r], ctxT_bank).then_inc(ctxT_saved, 1)
                act.wait_ge(x_turned, at.n + 1)
                need(act, projected[1], at.n - 1)
                nc.scalar.copy(xT[:, r], xT_bank).then_inc(xT_saved, 1)

            def save_v(at):
                need_apart(act, v_projected, at.n + 1, waited)
                out = v_all[:].rearrange("p (b g) c e -> p b c g e", b=BATCH)[:, at.quad, at.slot(CHUNKS)]
                nc.scalar.copy(out, v_bank.rearrange("p (g e) -> p g e", g=HG)).then_inc(v_saved, 1)

            def first_two(at, s):
                pair = at.slot(4) // 2
                need(act, parts_stored[pair], at.quad * PAIR_STORES + START)
                act.wait_ge(turned[s], at.n + 1)
                nc.scalar.copy(part_now(at, s, 0), turned_bank[s].rearrange("p (k c) -> p k c", k=KX)
                               ).then_inc(first_done[s], 1)
                act.wait_ge(rest_done[s], at.n + 1)
                nc.scalar.copy(part_now(at, s, 1), rest[s][:].rearrange("p (k c) -> p k c", k=KX)
                               ).then_inc(second_done[s], 1)

            def sum_pieces(at):
                act.wait_ge(piece_loaded[at.slot(TURN)], at.quad * 32 + 32)
                for w in range(2):
                    nc.scalar.activation(ffn_abs[:, w], ffn_piece[:, at.slot(TURN), w], ACT.Abs,
                                         accum_out=abs_sums[:, w, at.n:at.n + 1] if not at.looped else
                                         abs_sums[:, w, bass.ds(at.n, 1)]).then_inc(piece_summed, 1)

            order_weights()
            act.wait_ge(angles_ready, 1)
            nc.scalar.activation(sine[:].rearrange("p t a -> p (t a)"), angle[:].rearrange("p t a f -> p (t a f)"),
                                 ACT.Sin).then_inc(sines_ready, 1)
            nc.scalar.activation(cosine[:].rearrange("p t a r -> p (t a) r"),
                                 shifted[:].unsqueeze(2).to_broadcast([P, TILES * ANGLES, 2]),
                                 ACT.Sin).then_inc(sines_ready, 1)

            def step(at):
                if at.back(2).within(TILES):
                    save_inputs(at.back(2))
                if at.back(4).within(TILES):
                    first_two(at.back(4), 0)
                if at.back(3).within(TILES):
                    save_v(at.back(3))
                if at.back(4).within(TILES):
                    first_two(at.back(4), 1)
                if at.back(4).within(TILES):
                    sum_pieces(at.back(4))

            run_steps(act, TILES, 4, 5, step)

        @block.gpsimd
        def _(pool):
            def spread(at):
                r = at.slot(2)
                need_apart(pool, stats_ready, at.n + 1, waited)
                need_apart(pool, xn_ready, at.n - 1, waited)
                pool.tensor_scalar(rstd[:, r, 0:1], moments[:, r, 1:2], LN_EPS, None, ALU.add).then_inc(power_ready, 1)
                pool.wait_ge(power_ready, at.n + 2)
                pool.tensor_tensor(rstd[:, r, 1:2], rstd[:, r, 0:1], half_power[:], ALU.pow).then_inc(rstd_ready, 1)

            def sum_products(at, s):
                pool.wait_ge(multiplied[s], at.n + 1)
                need(pool, turned[s], at.n)
                pool.tensor_tensor(rotated[s][:], straight[s][:], crossed[s][:], ALU.add).then_inc(summed[s], 1)

            def last_part(at, s):
                half = at.slot(2)
                now = lambda part: parts[:, at.slot(4) // 2, s, part, :, half * P:(half + 1) * P]
                pool.wait_ge(second_done[s], at.n + 1)
                pool.tensor_tensor(now(2), rest[s][:].rearrange("p (k c) -> p k c", k=KX), now(1),
                                   ALU.subtract).then_inc(third_done[s], 1)

            pool.memset(half_power[:], -0.5).then_inc(power_ready, 1)
            pool.memset(ones[:], 1.0).then_inc(ones_ready, 1)
            for pair in range(2):
                pool.sem_inc(parts_stored[pair], START)

            def step(at):
                if at.within(TILES):
                    spread(at)
                if at.back(3).within(TILES):
                    sum_products(at.back(3), 0)
                if at.back(4).within(TILES):
                    last_part(at.back(4), 0)
                    last_part(at.back(4), 1)
                if at.back(3).within(TILES):
                    sum_products(at.back(3), 1)

            run_steps(pool, TILES, 4, 5, step)


def attend(nc, w_fc, w_proj, identb, ident16, limits, v_all, q_parts, k_parts, o_all, wT):
    with ExitStack() as stack:
        sb, pb, sem = allocators(nc, stack, "attend")
        q_stack = sb("q_stack", [P, TURN, GH, SEQ], BF16)
        k_stack = sb("k_stack", [P, TURN, GH, SEQ], BF16)
        probs = sb("probs", [P, CHUNKS, GH, SEQ], F32)
        v_ones = sb("v_ones", [P, 2, CHUNKS, GH, 2 * HEAD], F32)
        maxima = sb("maxima", [P, 2, GH * CHUNKS], F32)
        neg_max = sb("neg_max", [P, 2, GH * CHUNKS], F32)
        max_parts = sb("max_parts", [P, 2, 2 * GH * CHUNKS], BF16)
        max_rows = sb("max_rows", [2 * GH * CHUNKS, 2, P], BF16)
        raw = sb("raw", [P, 2, DIM], F32)
        below = sb("below", [P, DIM], F16)
        ternary = sb("ternary", [P, 2, DIM], F16)
        banks = pb("banks", [P, 8, SEQ], F32)
        score_slot = [banks[:, 0:2], banks[:, 2:4]]
        PV_BANK = banks[:, 7]
        HALFWAY = 8
        RING = [4 + i % 3 for i in range(15)] + [5, 6]
        TURN_BANK = RING[HALFWAY]
        ST_BANK = RING[:HALFWAY] + RING[HALFWAY + 1:]
        ST_BEFORE = [max(j for j in range(k - 16, k) if ST_BANK[j % 16] == ST_BANK[k]) for k in range(16)]
        BEFORE_TURN = max(k for k in range(HALFWAY) if ST_BANK[k] == TURN_BANK)
        AFTER_TURN = min(k for k in range(HALFWAY, 16) if ST_BANK[k] == TURN_BANK)
        STACK_LOADS = 16 * 7

        stacks_loaded = [sem(f"stacks_loaded_{i}") for i in range(TURN)]
        max_loaded = [sem(f"max_loaded_{i}") for i in range(TURN)]
        ones_ready, v_staged = sem("ones_ready"), sem("v_staged")
        scores_ready, scores_read = sem("scores_ready"), sem("scores_read")
        neg_ready, high_ready, split_ready = sem("neg_ready"), sem("high_ready"), sem("split_ready")
        st_ready, exp_done = sem("st_ready"), sem("exp_done")
        pv_done, o_saved = sem("pv_done"), sem("o_saved")
        raw_loaded = [sem(f"raw_loaded_{i}") for i in range(2)]
        cut, ternary_ready = sem("cut"), sem("ternary_ready")
        both_turned, max_saved, weight_saved = sem("both_turned"), sem("max_saved"), sem("weight_saved")
        max_bank = banks[0:2 * GH * CHUNKS, TURN_BANK, 0:P // 2].bitcast(BF16)
        weight_bank = banks[:, TURN_BANK, P // 2:P // 2 + DIM // 2].bitcast(F16)

        waited = sem("waited")
        block = stack.enter_context(nc.Block())

        @block.sync
        def _(sp):
            def load_stacks(at):
                slot = at.slot(TURN)
                need(sp, st_ready, (at.n - TURN + 1) * 16)
                for stack_sb, where, runs in (
                    (q_stack, q_parts, ((0, 0, 3), (3, 0, 2), (5, 0, 1))),
                    (k_stack, k_parts, ((0, 1, 1), (1, 0, 1), (2, 0, 1), (3, 0, 3))),
                ):
                    src = where[at.n].rearrange("t (d h) c -> (t d) (h c)", h=GH)
                    for to, part, count in runs:
                        sp.dma_start(
                            stack_sb[to * HEAD:(to + count) * HEAD, slot].rearrange("p h c -> p (h c)"),
                            src[part * HEAD:(part + count) * HEAD],
                        ).then_inc(stacks_loaded[slot], 16)

            def load_max(at):
                sp.wait_ge(max_saved, at.n + 1)
                sp.dma_start(
                    q_stack[STACK:STACK + 2, at.slot(TURN)].rearrange("p h (c q) -> p (h c) q", c=CHUNKS),
                    max_rows[:, at.slot(2)],
                ).then_inc(max_loaded[at.slot(TURN)], 16)

            def load_weight(at):
                half = at.slot(TURN) // 2
                need(sp, ternary_ready, at.n - 1)
                if at.slot(2) == 0:
                    sp.dma_start(raw[:, 0], w_fc.rearrange("(i h p) d -> h i p d", h=2, p=P)[half, at.quad]
                                 ).then_inc(raw_loaded[0], 16)
                else:
                    sp.dma_start(raw[:, 1].rearrange("p (r c) -> p r c", r=2),
                                 w_proj.rearrange("(h r p) (i c) -> h i p r c", h=2, p=P, c=2 * P)[half, at.quad]
                                 ).then_inc(raw_loaded[1], 16)

            def step(at):
                if at.within(GROUPS):
                    load_stacks(at)
                    load_weight(at)
                if at.back(2).within(GROUPS):
                    load_max(at.back(2))

            run_steps(sp, GROUPS, 3, 4, step)

        @block.tensor
        def _(pe):
            def scores(at, j):
                head, slot = j // 2, at.slot(TURN)
                if j == 0:
                    pe.wait_ge(stacks_loaded[slot], at.quad * STACK_LOADS + STACK_LOADS)
                need(pe, scores_read, at.n * 2 * GH + j - 1)
                for i in range(2):
                    c = j % 2 * 2 + i
                    mm = nc.tensor.matmul(score_slot[j % 2][:, i],
                                          q_stack[0:STACK, slot, head, c * P:(c + 1) * P],
                                          k_stack[0:STACK, slot, head, :], start=True, stop=True)
                mm.then_inc(scores_ready, 1)

            def turn_both(at):
                pe.wait_ge(split_ready, at.n + 1)
                if at.looped or at.n > 0:
                    pe.wait_ge(exp_done, (at.n - 1) * 16 + BEFORE_TURN + 1)
                nc.tensor.transpose(max_bank, max_parts[:, at.slot(2)], identb[:])
                pe.wait_ge(ternary_ready, at.n + 1)
                for i in range(4):
                    mm = nc.tensor.transpose(weight_bank[:, i * P:(i + 1) * P],
                                             ternary[:, at.slot(2), i * P:(i + 1) * P], ident16[:])
                mm.then_inc(both_turned, 1)

            def scores_turned(at, k):
                c, head, slot = k // GH, k % GH, at.slot(TURN)
                if k == 0:
                    if not at.looped:
                        pe.wait_ge(ones_ready, 2)
                    pe.wait_ge(max_loaded[slot], at.quad * 16 + 16)
                if not at.looped and at.n == 0 and k == ST_BANK.index(TURN_BANK):
                    pe.wait_ge(weight_saved, 1)
                elif k != AFTER_TURN:
                    need(pe, exp_done, at.n * 16 + ST_BEFORE[k] + 1)
                elif at.looped or at.n < GROUPS - 1:
                    pe.wait_ge(weight_saved, at.n + 2)
                else:
                    pe.wait_ge(exp_done, at.n * 16 + BEFORE_TURN + 1)
                nc.tensor.matmul(banks[:, ST_BANK[k]], k_stack[0:STACK + 2, slot, head, c * P:(c + 1) * P],
                                 q_stack[0:STACK + 2, slot, head, :], start=True, stop=True).then_inc(st_ready, 1)

            def weigh_v(at, c):
                pe.wait_ge(exp_done, at.n * 16 + GH * (c + 1))
                if c == 0:
                    pe.wait_ge(v_staged, at.n + 1)
                    need(pe, o_saved, at.n)
                for j in range(GH):
                    mm = nc.tensor.matmul(PV_BANK[32 * j:32 * j + 32], v_ones[:, at.slot(2), c, j, :],
                                          probs[:, c, j, :], start=(c == 0), stop=(c == CHUNKS - 1))
                mm.then_inc(pv_done, 1)

            def step(at):
                turned, before = at.back(2), at.back(3)
                for c in range(CHUNKS):
                    if turned.within(GROUPS):
                        scores_turned(turned, 4 * c)
                        scores_turned(turned, 4 * c + 1)
                    if at.within(GROUPS):
                        scores(at, 2 * c)
                    if c == 0 and before.within(GROUPS):
                        weigh_v(before, CHUNKS - 1)
                    if c > 0 and turned.within(GROUPS):
                        weigh_v(turned, c - 1)
                    if turned.within(GROUPS):
                        scores_turned(turned, 4 * c + 2)
                        scores_turned(turned, 4 * c + 3)
                    if at.within(GROUPS):
                        scores(at, 2 * c + 1)
                    if c == 1 and at.back(1).within(GROUPS):
                        turn_both(at.back(1))

            run_steps(pe, GROUPS, 3, 4, step)

        @block.vector
        def _(dve):
            def row_maxima(at, j):
                dve.wait_ge(scores_ready, at.n * 2 * GH + j + 1)
                if j == 0:
                    need(dve, split_ready, at.n - 1)
                dve.tensor_reduce(maxima[:, at.slot(2), 2 * j:2 * j + 2], score_slot[j % 2],
                                  AX.X, ALU.max).then_inc(scores_read, 1)

            def save_sums(at):
                need_apart(dve, pv_done, (at.n + 1) * CHUNKS, waited)
                dve.tensor_copy(o_all[:, at.n], PV_BANK).then_inc(o_saved, 1)

            def step(at):
                for j in range(2 * GH):
                    if j == 1 and at.back(3).within(GROUPS):
                        save_sums(at.back(3))
                    if at.within(GROUPS):
                        row_maxima(at, j)

            run_steps(dve, GROUPS, 3, 4, step)

        @block.scalar
        def _(act):
            def exponentials(at, k):
                c, head = k // GH, k % GH
                act.wait_ge(st_ready, at.n * 16 + k + 1)
                if head == 0:
                    need(act, pv_done, (at.n - 1) * CHUNKS + c + 1)
                nc.scalar.activation(probs[:, c, head, :], banks[:, ST_BANK[k]], ACT.Exp,
                                     scale=1 / math.sqrt(HEAD)).then_inc(exp_done, 1)

            def save_both(at):
                need_apart(act, both_turned, at.n + 1, waited)
                last = at.back(2)
                if last.looped or last.n >= 0:
                    act.wait_ge(max_loaded[last.slot(TURN)], last.quad * 16 + 16)
                nc.scalar.copy(max_rows[:, at.slot(2)], max_bank).then_inc(max_saved, 1)
                nc.scalar.copy(wT[:, at.n], weight_bank).then_inc(weight_saved, 1)

            def step(at):
                for k in range(16):
                    if at.back(2).within(GROUPS):
                        exponentials(at.back(2), k)
                    if k == HALFWAY - 1 and at.back(1).within(GROUPS):
                        save_both(at.back(1))

            run_steps(act, GROUPS, 3, 4, step)

        @block.gpsimd
        def _(pool):
            def stage_v(at):
                need(pool, pv_done, (at.n - 1) * CHUNKS)
                pool.tensor_copy(v_ones[:, at.slot(2), :, :, 0:HEAD],
                                 v_all[:, at.n].rearrange("p c (h d) -> p c h d", h=GH)).then_inc(v_staged, 1)

            def split_maxima(at):
                r, half = at.slot(2), GH * CHUNKS
                need_apart(pool, scores_read, (at.n + 1) * 2 * GH, waited)
                pool.tensor_scalar(neg_max[:, r], maxima[:, r], -1.0, None, ALU.mult).then_inc(neg_ready, 1)
                need_apart(pool, neg_ready, at.n + 1, waited)
                if at.looped or at.n >= 2:
                    need_apart(pool, both_turned, at.n - 1, waited)
                pool.tensor_scalar(max_parts[:, r, 0:half], neg_max[:, r], 1.0, None, ALU.mult
                                   ).then_inc(high_ready, 1)
                pool.wait_ge(high_ready, at.n + 1)
                pool.tensor_tensor(max_parts[:, r, half:2 * half], neg_max[:, r], max_parts[:, r, 0:half],
                                   ALU.subtract).then_inc(split_ready, 1)

            def ternarise(at):
                w = at.slot(2)
                need_apart(pool, raw_loaded[w], at.use_of_two * 16, waited)
                need_apart(pool, ternary_ready, at.n, waited)
                pool.tensor_scalar(below[:], raw[:, w], limits[:, 1, w:w + 1], None, ALU.is_lt).then_inc(cut, 1)
                need_apart(pool, both_turned, at.n - 1, waited)
                pool.tensor_scalar(ternary[:, w], raw[:, w], limits[:, 0, w:w + 1], None, ALU.is_gt).then_inc(cut, 1)
                pool.wait_ge(cut, at.n * 2 + 2)
                pool.tensor_tensor(ternary[:, w], ternary[:, w], below[:], ALU.subtract).then_inc(ternary_ready, 1)

            pool.memset(v_ones[:], 1.0).then_inc(ones_ready, 1)
            pool.wait_ge(ones_ready, 1)
            pool.memset(k_stack[STACK:STACK + 2].bitcast(mybir.dt.uint32), 0x3F803F80).then_inc(ones_ready, 1)
            pool.wait_ge(ones_ready, 2)

            def step(at):
                if at.back(1).within(GROUPS):
                    stage_v(at.back(1))
                if at.within(GROUPS):
                    ternarise(at)
                    split_maxima(at)

            run_steps(pool, GROUPS, 2, 4, step)


def mix(nc, x, wout, bout, ident, ident16, o_all, gammas, x1, uT, row_scale):
    with ExitStack() as stack:
        sb, pb, sem = allocators(nc, stack, "mix")
        x_in = sb("x_in", [P, TURN, DIM], F32)
        o_in = sb("o_in", [P, 2, HG, P], F32)
        wout_sb = sb("wout_sb", [P, KX, DIM], F32)
        bout_sb = sb("bout_sb", [P, DIM], F32)
        x_bias = sb("x_bias", [P, 2, DIM], F32)
        inverse = sb("inverse", [P, HEADS], F32)
        attn = sb("attn", [P, 2, DIM], F32)
        attnT = sb("attnT", [P, 2, DIM], F32)
        stats = sb("stats", [P, 6], F32)
        moments = sb("moments", [P, 2, 2], F32)
        powers = sb("powers", [P, 2, 6], F32)
        gamma_128 = sb("gamma_128", [P, 1], F32)
        half_power = sb("half_power", [P, 1], F32)
        centred = sb("centred", [P, DIM], F32)
        absmax = sb("absmax", [P, 4], F32)
        u = sb("u", [P, DIM], F32)
        u_parts = sb("u_parts", [P, 2, 2, DIM], F16)
        banks = pb("banks", [P, 8, DIM], F32)
        rows_bank, attnT_bank, y_bank, uT_bank = banks[:, 0:2], banks[:, 2], banks[:, 3], banks[:, 4].bitcast(F16)

        x_in_loaded = [sem(f"x_in_loaded_{i}") for i in range(TURN)]
        o_in_loaded = [sem(f"o_in_loaded_{i}") for i in range(2)]
        wout_loaded, bout_loaded, power_set = sem("wout_loaded"), sem("bout_loaded"), sem("power_set")
        rows_ready, inverse_ready, attn_ready = sem("rows_ready"), sem("inverse_ready"), sem("attn_ready")
        attn_turned, attnT_saved, y_ready = sem("attn_turned"), sem("attnT_saved"), sem("y_ready")
        x_bias_ready, x1_ready, stats_done, stats_ready = (
            sem("x_bias_ready"), sem("x1_ready"), sem("stats_done"), sem("stats_ready"))
        spread_step, spread_ready, scale_ready = sem("spread_step"), sem("spread_ready"), sem("scale_ready")
        quant_step, u_step, u_ready, u_turned, uT_saved = (
            sem("quant_step"), sem("u_step"), sem("u_ready"), sem("u_turned"), sem("uT_saved"))
        waited = sem("waited")
        block = stack.enter_context(nc.Block())

        @block.sync
        def _(sp):
            x_rows = x.rearrange("b (c p) d -> (b c) p d", p=P)
            sp.dma_start(bout_sb[:], bout.rearrange("(a d) -> a d", a=1).to_broadcast([P, DIM])
                         ).then_inc(bout_loaded, 16)

            def load(at):
                need(sp, x_bias_ready, at.n - TURN + 1)
                sp.dma_start(x_in[:, at.slot(TURN)], x_rows[at.n]).then_inc(x_in_loaded[at.slot(TURN)], 16)
                need(sp, rows_ready, at.n - 1)
                c = at.slot(CHUNKS)
                sp.dma_start(o_in[:, at.slot(2)],
                             o_all[:].rearrange("p (b g) q -> p b g q", b=BATCH)[:, at.quad, :, c * P:(c + 1) * P]
                             ).then_inc(o_in_loaded[at.slot(2)], 16)

            load(At(0, 0))
            sp.dma_start(wout_sb[:], wout.rearrange("(k p) n -> p k n", p=P)).then_inc(wout_loaded, 16)
            for s in range(1, TURN):
                load(At(0, s))
            run_steps(sp, TILES - TURN, 0, 0, lambda at: load(at.back(-TURN)))

        @block.tensor
        def _(pe):
            def turn_sums(at):
                need(pe, attn_ready, at.n)
                pe.wait_ge(o_in_loaded[at.slot(2)], at.use_of_two * 16)
                for g in range(HG):
                    mm = nc.tensor.transpose(rows_bank[:, g // 4, g % 4 * P:(g % 4 + 1) * P],
                                             o_in[:, at.slot(2), g, :], ident[:])
                mm.then_inc(rows_ready, 1)

            def turn_attn(at):
                pe.wait_ge(attn_ready, at.n + 1)
                need(pe, attnT_saved, at.n)
                for k in range(KX):
                    mm = nc.tensor.transpose(attnT_bank[:, k * P:(k + 1) * P],
                                             attn[:, at.slot(2), k * P:(k + 1) * P], ident[:])
                mm.then_inc(attn_turned, 1)

            def project_out(at):
                pe.wait_ge(attnT_saved, at.n + 1)
                need(pe, x1_ready, at.n)
                for k in range(KX):
                    mm = nc.tensor.matmul(y_bank, attnT[:, at.slot(2), k * P:(k + 1) * P], wout_sb[:, k, :],
                                          start=(k == 0), stop=(k == KX - 1))
                mm.then_inc(y_ready, 1)

            def turn_u(at):
                pe.wait_ge(u_ready, at.n + 1)
                need(pe, uT_saved, at.n)
                for part in range(2):
                    for k in range(KX):
                        i = part * KX + k
                        mm = nc.tensor.transpose(uT_bank[:, i * P:(i + 1) * P],
                                                 u_parts[:, at.slot(2), part, k * P:(k + 1) * P], ident16[:])
                mm.then_inc(u_turned, 1)

            pe.wait_ge(wout_loaded, 16)

            def step(at):
                if at.within(TILES):
                    turn_sums(at)
                if at.back(1).within(TILES):
                    turn_attn(at.back(1))
                if at.back(4).within(TILES):
                    turn_u(at.back(4))
                if at.back(2).within(TILES):
                    project_out(at.back(2))

            run_steps(pe, TILES, 4, 5, step)

        @block.vector
        def _(dve):
            def divide(at):
                rows = rows_bank.rearrange("p a (m e) -> p (a m) e", e=2 * HEAD)
                dve.wait_ge(rows_ready, at.n + 1)
                dve.reciprocal(inverse[:], rows[:, :, HEAD]).then_inc(inverse_ready, 1)
                dve.wait_ge(inverse_ready, at.n + 1)
                need(dve, attn_turned, at.n - 1)
                dve.tensor_tensor(attn[:, at.slot(2)].rearrange("p (m d) -> p m d", d=HEAD), rows[:, :, 0:HEAD],
                                  inverse[:].unsqueeze(2).to_broadcast([P, HEADS, HEAD]), ALU.mult
                                  ).then_inc(attn_ready, 1)

            def add_residual(at):
                dve.wait_ge(y_ready, at.n + 1)
                dve.wait_ge(x_bias_ready, at.n + 1)
                dve.tensor_tensor(x1[:, at.n], y_bank, x_bias[:, at.slot(2)], ALU.add).then_inc(x1_ready, 1)
                need_apart(dve, x1_ready, at.n + 1, waited)
                dve.bn_stats(stats[:], x1[:, at.n]).then_inc(stats_done, 1)
                need_apart(dve, stats_done, at.n + 1, waited)
                need_apart(dve, scale_ready, at.n - 1, waited)
                dve.bn_aggr(moments[:, at.slot(2)], stats[:]).then_inc(stats_ready, 1)

            def quantise(at):
                r, steps = at.slot(2), at.n * 5
                dve.wait_ge(stats_ready, at.n + 1)
                dve.tensor_scalar(centred[:], x1[:, at.n], moments[:, r, 0:1], None, ALU.subtract
                                  ).then_inc(quant_step, 1)
                dve.wait_ge(quant_step, steps + 1)
                dve.tensor_reduce(absmax[:, 0:1], centred[:], AX.X, ALU.max, apply_absolute_value=True
                                  ).then_inc(quant_step, 1)
                dve.wait_ge(quant_step, steps + 2)
                dve.reciprocal(absmax[:, 1:2], absmax[:, 0:1]).then_inc(quant_step, 1)
                dve.wait_ge(quant_step, steps + 3)
                dve.tensor_scalar(absmax[:, 2:3], absmax[:, 1:2], Q_B, None, ALU.mult).then_inc(quant_step, 1)
                dve.wait_ge(spread_ready, at.n + 1)
                dve.scalar_tensor_tensor(absmax[:, 3:4], absmax[:, 1:2], 0.0, powers[:, r, 5:6], ALU.mult, ALU.add
                                         ).then_inc(quant_step, 1)
                dve.wait_ge(quant_step, steps + 5)
                dve.tensor_scalar(u[:], centred[:], absmax[:, 2:3], Q_B, ALU.mult, ALU.min).then_inc(u_step, 1)
                dve.scalar_tensor_tensor(row_scale[:, at.n], absmax[:, 0:1], absmax[:, 3:4], gamma_128[:],
                                         ALU.mult, ALU.mult).then_inc(scale_ready, 1)
                need(dve, u_turned, at.n - 1)
                dve.wait_ge(u_step, at.n * 2 + 1)
                dve.tensor_scalar(u_parts[:, r, 0], u[:], -Q_B, None, ALU.max).then_inc(u_step, 1)
                dve.wait_ge(u_step, at.n * 2 + 2)
                dve.scalar_tensor_tensor(u_parts[:, r, 1], u[:], -Q_B, u_parts[:, r, 0], ALU.max, ALU.subtract
                                         ).then_inc(u_ready, 1)

            dve.tensor_scalar(gamma_128[:], gammas[:, 0:1], 1 / Q_B, None, ALU.mult)

            def step(at):
                if at.back(3).within(TILES):
                    quantise(at.back(3))
                if at.within(TILES):
                    divide(at)
                if at.back(2).within(TILES):
                    add_residual(at.back(2))

            run_steps(dve, TILES, 3, 5, step)

        @block.scalar
        def _(act):
            def save_attn(at):
                act.wait_ge(attn_turned, at.n + 1)
                need(act, y_ready, at.n - 1)
                nc.scalar.copy(attnT[:, at.slot(2)], attnT_bank).then_inc(attnT_saved, 1)

            def save_u(at):
                need_apart(act, u_turned, at.n + 1, waited)
                nc.scalar.copy(uT[:, at.n], uT_bank).then_inc(uT_saved, 1)

            def step(at):
                if at.back(1).within(TILES):
                    save_attn(at.back(1))
                if at.back(4).within(TILES):
                    save_u(at.back(4))

            run_steps(act, TILES, 4, 5, step)

        @block.gpsimd
        def _(pool):
            def add_bias(at):
                pool.wait_ge(x_in_loaded[at.slot(TURN)], at.quad * 16 + 16)
                need(pool, x1_ready, at.n - 1)
                pool.tensor_tensor(x_bias[:, at.slot(2)], x_in[:, at.slot(TURN)], bout_sb[:], ALU.add
                                   ).then_inc(x_bias_ready, 1)

            def spread(at):
                r = at.slot(2)
                now = lambda i: powers[:, r, i:i + 1]
                count = [0]

                def then(ins):
                    count[0] += 1
                    ins.then_inc(spread_step, 1)
                    need_apart(pool, spread_step, at.n * 6 + count[0], waited)

                need_apart(pool, stats_ready, at.n + 1, waited)
                need_apart(pool, scale_ready, at.n - 1, waited)
                then(pool.tensor_scalar(now(0), moments[:, r, 1:2], LN_EPS, None, ALU.add))
                then(pool.tensor_tensor(now(1), now(0), half_power[:], ALU.pow))
                then(pool.tensor_tensor(now(2), now(1), now(1), ALU.mult))
                then(pool.tensor_tensor(now(3), now(2), moments[:, r, 1:2], ALU.mult))
                then(pool.tensor_scalar(now(3), now(3), FFN_EPS, None, ALU.add))
                then(pool.tensor_tensor(now(4), now(3), half_power[:], ALU.pow))
                pool.tensor_tensor(now(5), now(4), now(1), ALU.mult).then_inc(spread_ready, 1)

            pool.memset(half_power[:], -0.5).then_inc(power_set, 1)
            pool.wait_ge(power_set, 1)
            pool.wait_ge(bout_loaded, 16)

            def step(at):
                if at.within(TILES):
                    add_bias(at)
                if at.back(2).within(TILES):
                    spread(at.back(2))

            run_steps(pool, TILES, 2, 5, step)


def ffn(nc, ident16, o_all, uT, row_scale, gammas, x1, wT, out):
    with ExitStack() as stack:
        sb, pb, sem = allocators(nc, stack, "ffn")
        spare = o_all[:].rearrange("p g q -> p (g q)")
        h = spare[:, 0:2 * FFN].rearrange("p (s c) -> p s c", s=2)
        h_parts = spare[:, 2 * FFN:4 * FFN].bitcast(F16).rearrange("p (s t c) -> p s t c", s=2, t=2)
        hT = spare[:, 4 * FFN:6 * FFN].bitcast(F16).rearrange("p (s j k r) -> p s j k r", s=2, j=4, r=P)
        fcT = wT[:].rearrange("p (o q w) (k c) -> p w k o q c", q=4, w=2, k=KX)[:, 0]
        projT = wT[:].rearrange("p (i h w) (r k c) -> p w i k h r c", h=2, w=2, r=2, k=2)[:, 1]
        stats = sb("stats", [P, FFN // DIM, 6], F32)
        moments = sb("moments", [P, 2, 2], F32)
        powers = sb("powers", [P, 2, 2], F32)
        half_power = sb("half_power", [P, 1], F32)
        absmax = sb("absmax", [P, 4], F32)
        out_scale = sb("out_scale", [P, TURN, 1], F32)
        gamma_128 = sb("gamma_128", [P, 1], F32)
        y = sb("y", [P, 2, DIM], F32)
        banks = pb("banks", [P, 8, DIM], F32)

        fc_ready, h_ready = sem("fc_ready"), sem("h_ready")
        stats_done, stats_ready, eps_added, spread_ready, power_set = (
            sem("stats_done"), sem("stats_ready"), sem("eps_added"), sem("spread_ready"), sem("power_set"))
        quant_step, gamma_set, parts_ready, scale_ready = (
            sem("quant_step"), sem("gamma_set"), sem("parts_ready"), sem("scale_ready"))
        h_turned, hT_saved, proj_ready, y_ready = sem("h_turned"), sem("hT_saved"), sem("proj_ready"), sem("y_ready")
        out_stored = [sem(f"out_stored_{i}") for i in range(2)]
        QUARTERS = FFN // DIM
        waited = sem("waited")
        block = stack.enter_context(nc.Block())

        @block.sync
        def _(sp):
            out_rows = out.rearrange("b (c p) d -> (b c) p d", p=P)

            def store(at):
                sp.wait_ge(y_ready, at.n + 1)
                sp.dma_start(out_rows[at.n], y[:, at.slot(2)]).then_inc(out_stored[at.slot(2)], 16)

            run_steps(sp, TILES, 0, 4, store)
            for i in range(2):
                sp.wait_ge(out_stored[i], 16 * TILES // 2)

        @block.tensor
        def _(pe):
            def expand(at, o):
                need(pe, h_ready, (at.n - 1) * QUARTERS + o + 1)
                for k in range(KX):
                    for part in range(2):
                        mm = nc.tensor.matmul(banks[:, o], uT[:, at.n, (part * KX + k) * P:(part * KX + k + 1) * P],
                                              fcT[:, k, o],
                                              start=(k + part == 0), stop=(k == KX - 1 and part == 1))
                mm.then_inc(fc_ready, 1)

            def turn_h(at, j):
                if j == 0:
                    pe.wait_ge(parts_ready, at.n + 1)
                need(pe, hT_saved, at.n * 4 + j - 1)
                for i in range(8):
                    first = (j % 2 * 8 + i) * P
                    mm = nc.tensor.transpose(banks[:, 4 + j % 2].bitcast(F16)[:, i * P:(i + 1) * P],
                                             h_parts[:, at.slot(2), j // 2, first:first + P], ident16[:])
                mm.then_inc(h_turned, 1)

            def contract(at):
                pe.wait_ge(hT_saved, at.n * 4 + 4)
                need(pe, y_ready, at.n - 1)
                for k in range(KF):
                    for part in range(2):
                        mm = nc.tensor.matmul(banks[:, 6 + at.slot(2)],
                                              hT[:, at.slot(2), part * 2 + k // 8, k % 8, :], projT[:, k // 2, k % 2],
                                              start=(k + part == 0), stop=(k == KF - 1 and part == 1))
                mm.then_inc(proj_ready, 1)

            def step(at):
                before = at.back(2)
                for half in range(2):
                    if before.within(TILES):
                        turn_h(before, 2 * half)
                        turn_h(before, 2 * half + 1)
                    if at.within(TILES):
                        expand(at, 2 * half)
                        expand(at, 2 * half + 1)
                if before.within(TILES):
                    contract(before)

            run_steps(pe, TILES, 2, 5, step)

        @block.scalar
        def _(act):
            def activate(at, o):
                need_apart(act, fc_ready, at.n * QUARTERS + o + 1, waited)
                if o == 0:
                    need_apart(act, parts_ready, at.n - 1, waited)
                nc.scalar.activation(h[:, at.slot(2), o * DIM:(o + 1) * DIM], banks[:, o], ACT.Gelu,
                                     scale=row_scale[:, at.n]).then_inc(h_ready, 1)

            def save_turned(at, j):
                act.wait_ge(h_turned, at.n * 4 + j + 1)
                need(act, proj_ready, at.n - 1)
                nc.scalar.copy(hT[:, at.slot(2), j].rearrange("p k r -> p (k r)"),
                               banks[:, 4 + j % 2].bitcast(F16)).then_inc(hT_saved, 1)

            def step(at):
                before = at.back(2)
                for half in range(2):
                    if before.within(TILES):
                        save_turned(before, 2 * half)
                        save_turned(before, 2 * half + 1)
                    if at.within(TILES):
                        activate(at, 2 * half)
                        activate(at, 2 * half + 1)

            run_steps(act, TILES, 2, 5, step)

        @block.vector
        def _(dve):
            def statistics(at):
                r = at.slot(2)
                for o in range(QUARTERS):
                    dve.wait_ge(h_ready, at.n * QUARTERS + o + 1)
                    dve.bn_stats(stats[:, o], h[:, r, o * DIM:(o + 1) * DIM]).then_inc(stats_done, 1)
                need_apart(dve, stats_done, at.n * QUARTERS + QUARTERS, waited)
                dve.bn_aggr(moments[:, r], stats[:].rearrange("p o s -> p (o s)")).then_inc(stats_ready, 1)

            def quantise(at):
                r, steps = at.slot(2), at.n * 7
                now = h[:, r, :]
                dve.wait_ge(stats_ready, at.n + 1)
                dve.tensor_scalar(now, now, moments[:, r, 0:1], None, ALU.subtract).then_inc(quant_step, 1)
                dve.wait_ge(quant_step, steps + 1)
                dve.tensor_reduce(absmax[:, 0:1], now, AX.X, ALU.max, apply_absolute_value=True
                                  ).then_inc(quant_step, 1)
                dve.wait_ge(quant_step, steps + 2)
                dve.reciprocal(absmax[:, 1:2], absmax[:, 0:1]).then_inc(quant_step, 1)
                dve.wait_ge(quant_step, steps + 3)
                dve.tensor_scalar(absmax[:, 2:3], absmax[:, 1:2], Q_B, None, ALU.mult).then_inc(quant_step, 1)
                dve.wait_ge(spread_ready, at.n + 1)
                dve.scalar_tensor_tensor(absmax[:, 3:4], absmax[:, 1:2], 0.0, powers[:, r, 1:2], ALU.mult, ALU.add
                                         ).then_inc(quant_step, 1)
                dve.wait_ge(quant_step, steps + 5)
                dve.tensor_scalar(now, now, absmax[:, 2:3], Q_B, ALU.mult, ALU.min).then_inc(quant_step, 1)
                dve.scalar_tensor_tensor(out_scale[:, at.slot(TURN)], absmax[:, 0:1], absmax[:, 3:4], gamma_128[:],
                                         ALU.mult, ALU.mult).then_inc(scale_ready, 1)
                need(dve, h_turned, (at.n - 1) * 4)
                dve.wait_ge(quant_step, steps + 6)
                dve.tensor_scalar(h_parts[:, r, 0], now, -Q_B, None, ALU.max).then_inc(quant_step, 1)
                dve.wait_ge(quant_step, steps + 7)
                dve.scalar_tensor_tensor(h_parts[:, r, 1], now, -Q_B, h_parts[:, r, 0], ALU.max, ALU.subtract
                                         ).then_inc(parts_ready, 1)

            def finish(at):
                r = at.slot(2)
                dve.wait_ge(proj_ready, at.n + 1)
                dve.wait_ge(scale_ready, at.n + 1)
                before = at.back(2)
                if before.looped or before.n >= 0:
                    dve.wait_ge(out_stored[r], before.use_of_two * 16)
                dve.scalar_tensor_tensor(y[:, r], banks[:, 6 + r], out_scale[:, at.slot(TURN)], x1[:, at.n],
                                         ALU.mult, ALU.add).then_inc(y_ready, 1)

            dve.tensor_scalar(gamma_128[:], gammas[:, 1:2], 1 / Q_B, None, ALU.mult).then_inc(gamma_set, 1)
            dve.wait_ge(gamma_set, 1)

            def step(at):
                if at.back(3).within(TILES):
                    finish(at.back(3))
                if at.back(1).within(TILES):
                    statistics(at.back(1))
                    quantise(at.back(1))

            run_steps(dve, TILES, 3, 5, step)

        @block.gpsimd
        def _(pool):
            def spread(at):
                r = at.slot(2)
                need_apart(pool, stats_ready, at.n + 1, waited)
                need_apart(pool, scale_ready, at.n - 1, waited)
                pool.tensor_scalar(powers[:, r, 0:1], moments[:, r, 1:2], FFN_EPS, None, ALU.add
                                   ).then_inc(eps_added, 1)
                pool.wait_ge(eps_added, at.n + 1)
                pool.tensor_tensor(powers[:, r, 1:2], powers[:, r, 0:1], half_power[:], ALU.pow
                                   ).then_inc(spread_ready, 1)

            pool.memset(half_power[:], -0.5).then_inc(power_set, 1)
            pool.wait_ge(power_set, 1)
            run_steps(pool, TILES, 0, 4, spread)


def xattn_ffn(nc, x, ctx, pos, wq, wkv, wout, bout, w_fc, w_proj, out):
    q_parts = nc.dram_tensor("q_parts", [GROUPS, PARTS, GW, SEQ], BF16).ap()
    k_parts = nc.dram_tensor("k_parts", [GROUPS, PARTS, GW, SEQ], BF16).ap()
    with ExitStack() as stack:
        sb, _, sem = allocators(nc, stack, "xattn_ffn")
        ident = sb("ident", [P, P], F32)
        identh = sb("identh", [P, P], F16)
        identb = sb("identb", [P, P], BF16)
        filled = sem("filled")
        with nc.Block() as block:

            @block.gpsimd
            def _(pool):
                for n, square in enumerate((ident, identh, identb)):
                    pool.memset(square[:], 0.0).then_inc(filled, 1)
                    pool.wait_ge(filled, 2 * n + 1)
                    pool.affine_select(out=square[:], in_=square[:], compare_op=ALU.not_equal, fill=1.0, base=0,
                                       pattern=[[-1, P]], channel_multiplier=1).then_inc(filled, 1)

        with ExitStack() as attention:
            sb2, _, _ = allocators(nc, attention, "kept")
            o_all = sb2("o_all", [P, GROUPS, SEQ], F32)
            wT = sb2("wT", [P, GROUPS, DIM], F16)
            gammas = sb2("gammas", [P, 2], F32)
            limits = sb2("limits", [P, 2, 2], F32)
            with nc.sbuf_tensor("v_all", [P, GROUPS, CHUNKS, GW], F32) as v_all:
                project(nc, x, ctx, pos, wq, wkv, w_fc, w_proj, ident, o_all, v_all, gammas, limits, q_parts, k_parts)
                attend(nc, w_fc, w_proj, identb, identh, limits, v_all, q_parts, k_parts, o_all, wT)
            x1 = sb2("x1", [P, TILES, DIM], F32)
            uT = sb2("uT", [P, TILES, 2 * DIM], F16)
            row_scale = sb2("row_scale", [P, TILES, 1], F32)
            mix(nc, x, wout, bout, ident, identh, o_all, gammas, x1, uT, row_scale)
            ffn(nc, identh, o_all, uT, row_scale, gammas, x1, wT, out)


_INS = ["x", "ctx_1024", "fside_BxSx2_0", "L0_xattn_Wq", "L0_xattn_Wkv", "L0_xattn_Wout", "L0_xattn_bout",
        "L0_ffn_w_fc", "L0_ffn_w_proj"]
_OUTS = [((BATCH, SEQ, DIM), "float32")]


def kernel(**inputs):
    import numpy as _np
    import concourse.bacc as _bacc
    from concourse import mybir as _mybir
    from concourse.bass_utils import run_bass_kernel_spmd as _run

    nc = _bacc.Bacc("TRN2", target_bir_lowering=False, num_devices=1)
    arrays, args = {}, []
    for name in _INS:
        a = _np.ascontiguousarray(inputs[name])
        arrays[f"in_{name}_dram"] = a
        args.append(nc.dram_tensor(f"in_{name}_dram", a.shape, _mybir.dt.from_np(a.dtype), kind="ExternalInput").ap())
    for i, (shape, dtype) in enumerate(_OUTS):
        dt = _mybir.dt.from_np(_np.dtype(dtype))
        args.append(nc.dram_tensor(f"out_{i}_dram", shape, dt, kind="ExternalOutput").ap())
    xattn_ffn(nc, *args)
    r = _run(nc, [arrays], core_ids=[0])
    got = tuple(r.results[0][f"out_{i}_dram"] for i in range(len(_OUTS)))
    return got[0]
```

```python
import math
from contextlib import ExitStack

import concourse.bass as bass
from concourse import mybir

F32 = mybir.dt.float32
F32R = mybir.dt.float32r
BF16 = mybir.dt.bfloat16
F16 = mybir.dt.float16
ACT = mybir.ActivationFunctionType
ALU = mybir.AluOpType
AX = mybir.AxisListType

P = 128
BATCH, SEQ, DIM, CTX = 4, 512, 512, 256
HEADS, HEAD = 32, 16
FFN = 4 * DIM
ROWS = BATCH * SEQ
TILES = ROWS // P
CHUNKS = SEQ // P
KX, KC = DIM // P, CTX // P
KF = FFN // P
GH = 4
HG = HEADS // GH
GROUPS = BATCH * HG
GW = GH * HEAD
PARTS = 3
STACK = 6 * HEAD
AXES, FREQS = 2, 4
ANGLES = AXES * FREQS
LN_EPS, FFN_EPS = 1e-5, 1e-6
Q_B = 128.0
ROUNDER = 1.5 * 2.0 ** 23
TWO_PI_HIGH = 6.28125
TWO_PI_LOW = 2 * math.pi - TWO_PI_HIGH
PI_BELOW = 3.1415925
PAIR_STORES = 16 * 2 * 2 * PARTS
START = 1
STACK_LOADS = 16 * 7
PRELOADED = 2
TURN = 4


class At:

    def __init__(self, turn, k):
        self.turn, self.k = turn, k
        self.looped = not isinstance(turn, int)
        self.n = turn * TURN + k
        self.quad = turn + k // TURN

    def back(self, by):
        return At(self.turn, self.k - by)

    def within(self, count):
        return self.looped or 0 <= self.k < count

    @property
    def use_of_two(self):
        return self.turn * 2 + self.k // 2 + 1

    def slot(self, m):
        return self.k % m


def run_steps(eng, count, later, head, step):
    for s in range(head):
        step(At(0, s))
    turns = (count - head) // TURN
    with eng.Fori(0, turns) as turn:
        for u in range(TURN):
            step(At(turn, head + u))
    for s in range(head + turns * TURN, count + later):
        step(At(0, s))


def need(eng, semaphore, value):
    if not isinstance(value, int) or value > 0:
        eng.wait_ge(semaphore, value)


def need_apart(eng, semaphore, value, over):
    if not isinstance(value, int) or value > 0:
        eng.wait_ge(semaphore, value).then_inc(over, 1)


def allocators(nc, stack, stage):

    def sb(name, shape, dt):
        return stack.enter_context(nc.sbuf_tensor(f"{stage}_{name}", shape, dt))

    def pb(name, shape, dt):
        return stack.enter_context(nc.psum_tensor(f"{stage}_{name}", shape, dt))

    def sem(name):
        return stack.enter_context(nc.semaphore(f"{stage}_{name}"))

    return sb, pb, sem


def load_stacks(sp, at, q_parts, k_parts, q_stack, k_stack, stacks_loaded):
    slot = at.slot(TURN)
    for stack_sb, where, runs in (
        (q_stack, q_parts, ((0, 0, 3), (3, 0, 2), (5, 0, 1))),
        (k_stack, k_parts, ((0, 1, 1), (1, 0, 1), (2, 0, 1), (3, 0, 3))),
    ):
        src = where[at.n].rearrange("t (d h) c -> (t d) (h c)", h=GH)
        for to, part, count in runs:
            sp.dma_start(
                stack_sb[to * HEAD:(to + count) * HEAD, slot].rearrange("p h c -> p (h c)"),
                src[part * HEAD:(part + count) * HEAD],
            ).then_inc(stacks_loaded[slot], 16)


def project(nc, x, ctx, pos, wq, wkv, w_fc, w_proj, ident, spare, wT, v_all, gammas, limits, q_parts, k_parts,
            q_stack, k_stack, stacks_loaded, parts_stored):
    with ExitStack() as stack:
        sb, pb, sem = allocators(nc, stack, "project")
        wq_raw = spare[:, 0:KX]
        wk_raw = spare[:, KX:KX + KC]
        wv_raw = spare[:, KX + KC:KX + 2 * KC]
        ffn_piece = spare[:, 8:8 + 2 * TURN].rearrange("p (i w) d -> p i w d", w=2)
        ffn_abs = spare[:, 16:18]
        x_sb = spare[:, 18:18 + TURN]
        straight, crossed, rotated, rest = [[spare[:, 22 + 2 * i + s] for s in range(2)] for i in range(4)]
        ctx_sb = spare[:, 30:32].rearrange("p a (b c) -> p (a b) c", c=CTX)
        spare_16 = wT[:].rearrange("p n d -> p (n d)")
        PARTS_SIZE = 2 * 2 * PARTS * KX * 2 * P
        parts = spare_16[:, 0:PARTS_SIZE].bitcast(BF16).rearrange("p (i s t k r) -> p i s t k r", i=2, s=2, t=PARTS,
                                                                  k=KX)
        spare_32 = spare_16[:, PARTS_SIZE:].bitcast(F32)
        xn = spare_32[:, 0:2 * DIM].rearrange("p (i d) -> p i d", i=2)
        whole, over, shifted, sine, neg_sine = [
            spare_32[:, 2 * DIM + i * TILES * ANGLES:2 * DIM + (i + 1) * TILES * ANGLES] for i in range(5)]
        cosine = spare_32[:, 2 * DIM + 5 * TILES * ANGLES:2 * DIM + 7 * TILES * ANGLES]
        by_tile = lambda t: t.rearrange("p (t a) -> p t a", t=TILES)
        abs_sums = sb("abs_sums", [P, 2, TILES], F32)
        abs_sum = sb("abs_sum", [P, 2], F32)
        gamma_eps = sb("gamma_eps", [P, 2], F32)
        ones = sb("ones", [P, P], F32)
        wq_sb, wk_sb, wv_sb = (
            [sb(f"{w}_{part}", [P, blocks, DIM], F32R) for part in ("high", "low")]
            for w, blocks in (("wq", KX), ("wk", KC), ("wv", KC)))
        xT = [sb(f"xT_{part}", [P, 2, DIM], F32R) for part in ("high", "low")]
        ctxT = [sb(f"ctxT_{part}", [P, 2, CTX], F32R) for part in ("high", "low")]
        pos_sb = sb("pos_sb", [P, TILES, AXES], F32)
        angle = sb("angle", [P, TILES, AXES, FREQS], F32)
        stats = sb("stats", [P, 2, 6], F32)
        moments = sb("moments", [P, 2, 2], F32)
        half_power = sb("half_power", [P, 1], F32)
        rstd = sb("rstd", [P, 2, 2], F32)
        banks = pb("banks", [P, 8, DIM], F32)
        xT_bank, ctxT_bank, v_bank = banks[:, 0], banks[:, 1, 0:CTX], banks[:, 2]
        in_bank = [banks[:, 3], banks[:, 4]]
        turned_bank = [banks[:, 5], banks[:, 6]]

        w_loaded = {w: sem(f"{w}_loaded") for w in ("wk", "wv", "wq", "pos")}
        x_loaded = [sem(f"x_loaded_{i}") for i in range(TURN)]
        ctx_loaded = [sem(f"ctx_loaded_{i}") for i in range(TURN)]
        w_high_ready, w_low_ready = sem("w_high_ready"), sem("w_low_ready")
        x_low_ready, ctx_low_ready = sem("x_low_ready"), sem("ctx_low_ready")
        piece_loaded = [sem(f"piece_loaded_{i}") for i in range(TURN)]
        piece_summed, ones_ready, abs_summed, total_ready, gamma_step = (
            sem("piece_summed"), sem("ones_ready"), sem("abs_summed"), sem("total_ready"), sem("gamma_step"))
        tables_step, angles_ready, sines_ready, tables_ready = (
            sem("tables_step"), sem("angles_ready"), sem("sines_ready"), sem("tables_ready"))
        stats_done, stats_ready, power_ready, rstd_ready = (
            sem("stats_done"), sem("stats_ready"), sem("power_ready"), sem("rstd_ready"))
        xn_ready, x_turned, ctx_turned, xT_saved, ctxT_saved = (
            sem("xn_ready"), sem("x_turned"), sem("ctx_turned"), sem("xT_saved"), sem("ctxT_saved"))
        v_projected, v_saved = sem("v_projected"), sem("v_saved")
        projected = [sem(f"{s}_projected") for s in "kq"]
        multiplied = [sem(f"{s}_multiplied") for s in "kq"]
        summed = [sem(f"{s}_summed") for s in "kq"]
        turned = [sem(f"{s}_turned") for s in "kq"]
        first_done = [sem(f"{s}_first_done") for s in "kq"]
        rest_done = [sem(f"{s}_rest_done") for s in "kq"]
        second_done = [sem(f"{s}_second_done") for s in "kq"]
        third_done = [sem(f"{s}_third_done") for s in "kq"]
        order = lambda t, k: t.rearrange("p k (g h d) -> p (k g) d h", h=GH, d=HEAD)
        plain = lambda t: t[:].rearrange("p k (g d h) -> p (k g) d h", h=GH, d=HEAD)

        waited = sem("waited")
        block = stack.enter_context(nc.Block())

        @block.sync
        def _(sp):
            x_rows = x.rearrange("b (c p) d -> (b c) p d", p=P)
            ctx_rows = ctx.rearrange("b (c p) d -> (b c) p d", p=P)
            wkv_rows = wkv.rearrange("(k p) n -> p k n", p=P)

            def load_ctx(at):
                need(sp, ctx_turned, at.n - TURN + 1)
                sp.dma_start(ctx_sb[:, at.slot(TURN)], ctx_rows[at.n]).then_inc(ctx_loaded[at.slot(TURN)], 16)

            def load_x(at):
                need(sp, xn_ready, at.n - TURN + 1)
                sp.dma_start(x_sb[:, at.slot(TURN)], x_rows[at.n]).then_inc(x_loaded[at.slot(TURN)], 16)

            def load_piece(at):
                i = at.slot(TURN)
                need(sp, piece_summed, (at.n - TURN + 1) * 2)
                sp.dma_start(ffn_piece[:, i, 0], w_fc.rearrange("(o p) d -> o p d", p=P)[at.n]
                             ).then_inc(piece_loaded[i], 16)
                sp.dma_start(ffn_piece[:, i, 1],
                             w_proj.rearrange("(o p) d -> o p d", p=P)[at.quad, :, i * DIM:(i + 1) * DIM]
                             ).then_inc(piece_loaded[i], 16)

            sp.dma_start(pos_sb[:], pos.rearrange("b (c p) a -> p (b c) a", p=P)).then_inc(w_loaded["pos"], 16)
            load_ctx(At(0, 0))
            sp.dma_start(wk_raw, wkv_rows[:, :, 0:DIM]).then_inc(w_loaded["wk"], 16)
            load_x(At(0, 0))
            sp.dma_start(wv_raw, wkv_rows[:, :, DIM:2 * DIM]).then_inc(w_loaded["wv"], 16)
            load_x(At(0, 1))
            load_ctx(At(0, 1))
            sp.dma_start(wq_raw, wq.rearrange("(k p) n -> p k n", p=P)).then_inc(w_loaded["wq"], 16)

            def store(at):
                pair = at.slot(4) // 2
                views = [where.rearrange("(b k g) t e c -> b g t e k c", b=BATCH, k=KX) for where in (k_parts, q_parts)]
                done = [first_done, second_done, third_done]
                for s, part in ((0, 0), (0, 1), (1, 0), (0, 2), (1, 1), (1, 2)):
                    sp.wait_ge(done[part][s], at.n + 1)
                    for g in range(2):
                        sp.dma_start(views[s][at.quad, g, part, :, :, pair * 2 * P:(pair + 1) * 2 * P],
                                     parts[g * GW:(g + 1) * GW, pair, s, part]).then_inc(parts_stored[pair], 16)

            def step(at):
                if at.within(TILES) and not (isinstance(at.n, int) and at.n < 2):
                    load_ctx(at)
                    load_x(at)
                if at.back(2).within(TILES):
                    load_piece(at.back(2))
                if at.back(5).within(TILES) and at.back(5).slot(2) == 1:
                    store(at.back(5))
                group = at.back(TILES)
                if not at.looped and 0 <= group.n < PRELOADED:
                    for pair in range(2):
                        sp.wait_ge(parts_stored[pair], PAIR_STORES + START)
                    load_stacks(sp, group, q_parts, k_parts, q_stack, k_stack, stacks_loaded)

            run_steps(sp, TILES, 6, 8, step)

        @block.tensor
        def _(pe):
            def turn_inputs(at):
                r = at.slot(2)
                pe.wait_ge(ctx_loaded[at.slot(TURN)], at.quad * 16 + 16)
                need(pe, ctx_low_ready, at.n)
                for k in range(KC):
                    mm = nc.tensor.transpose(ctxT_bank[:, k * P:(k + 1) * P],
                                             ctx_sb[:, at.slot(TURN), k * P:(k + 1) * P], ident[:])
                mm.then_inc(ctx_turned, 1)
                pe.wait_ge(xn_ready, at.n + 1)
                need(pe, x_low_ready, at.n)
                for k in range(KX):
                    mm = nc.tensor.transpose(xT_bank[:, k * P:(k + 1) * P], xn[:, r, k * P:(k + 1) * P], ident[:])
                mm.then_inc(x_turned, 1)

            def product(out, lhs, slot, rhs, low_ready, done):
                blocks = rhs[0].shape[1]
                for a, b in ((0, 0), (0, 1), (1, 0)):
                    if a == 1:
                        pe.wait_ge(*low_ready)
                    for k in range(blocks):
                        mm = nc.tensor.matmul(out, lhs[a][:, slot, k * P:(k + 1) * P], rhs[b][:, k, :],
                                              start=(a + b + k == 0), stop=(a == 1 and k == blocks - 1))
                mm.then_inc(done, 1)

            def project_kv(at):
                r = at.slot(2)
                if not at.looped:
                    pe.wait_ge(w_low_ready, 2)
                pe.wait_ge(ctxT_saved, at.n + 1)
                need(pe, multiplied[0], at.n)
                product(in_bank[0], ctxT, r, wk_sb, (ctx_low_ready, at.n + 1), projected[0])
                need(pe, v_saved, at.n)
                product(v_bank, ctxT, r, wv_sb, (ctx_low_ready, at.n + 1), v_projected)

            def project_q(at):
                if not at.looped:
                    pe.wait_ge(w_low_ready, 3)
                pe.wait_ge(xT_saved, at.n + 1)
                need(pe, multiplied[1], at.n)
                product(in_bank[1], xT, at.slot(2), wq_sb, (x_low_ready, at.n + 1), projected[1])

            def turn_rotated(at, s):
                pe.wait_ge(summed[s], at.n + 1)
                need(pe, rest_done[s], at.n)
                for k in range(KX):
                    mm = nc.tensor.transpose(turned_bank[s][:, k * P:(k + 1) * P],
                                             rotated[s][:, k * P:(k + 1) * P], ident[:])
                mm.then_inc(turned[s], 1)


            def step(at):
                if at.back(2).within(TILES):
                    turn_inputs(at.back(2))
                if at.back(4).within(TILES):
                    turn_rotated(at.back(4), 0)
                if at.back(3).within(TILES):
                    project_kv(at.back(3))
                if at.back(4).within(TILES):
                    turn_rotated(at.back(4), 1)
                if at.back(3).within(TILES):
                    project_q(at.back(3))

            run_steps(pe, TILES, 4, 5, step)
            pe.wait_ge(abs_summed, 1)
            pe.wait_ge(ones_ready, 1)
            nc.tensor.matmul(ctxT_bank[:, 0:2], ones[:], abs_sum[:], start=True, stop=True).then_inc(total_ready, 1)

        @block.vector
        def _(dve):
            def weigh_ffn():
                dve.wait_ge(piece_summed, 2 * TILES)
                dve.tensor_reduce(abs_sum[:], abs_sums[:], AX.X, ALU.add).then_inc(abs_summed, 1)
                dve.wait_ge(total_ready, 1)
                dve.tensor_scalar(gammas[:], ctxT_bank[:, 0:2], 1.0 / (FFN * DIM), None, ALU.mult
                                  ).then_inc(gamma_step, 1)
                dve.wait_ge(gamma_step, 1)
                dve.tensor_scalar(gamma_eps[:], gammas[:], FFN_EPS, None, ALU.add).then_inc(gamma_step, 1)
                dve.wait_ge(gamma_step, 2)
                dve.tensor_scalar(limits[:, 0], gamma_eps[:], 0.5, None, ALU.mult)
                dve.tensor_scalar(limits[:, 1], gamma_eps[:], -0.5, None, ALU.mult)

            def make_tables():
                flat = angle[:].rearrange("p t a f -> p (t a f)")
                done = [0]

                def then(ins, more=1):
                    done[0] += more
                    ins.then_inc(tables_step, 1)

                def settled():
                    dve.wait_ge(tables_step, done[0])

                def reduce(values):
                    then(dve.tensor_scalar(whole, values, 1 / (2 * math.pi), ROUNDER, ALU.mult, ALU.add))
                    settled()
                    then(dve.tensor_scalar(over, whole, -ROUNDER, None, ALU.add))
                    settled()
                    then(dve.scalar_tensor_tensor(whole, over, -TWO_PI_HIGH, values, ALU.mult, ALU.add))
                    settled()
                    then(dve.scalar_tensor_tensor(values, over, -TWO_PI_LOW, whole, ALU.mult, ALU.add))
                    settled()

                def clamp(values):
                    then(dve.tensor_scalar(values, values, PI_BELOW, -PI_BELOW, ALU.min, ALU.max))

                dve.wait_ge(w_loaded["pos"], 16)
                for f in range(FREQS):
                    then(dve.tensor_scalar(angle[:, :, :, f], pos_sb[:], 10000.0 ** (-f / FREQS), None, ALU.mult))
                settled()
                reduce(flat)
                then(dve.tensor_scalar(shifted, flat, math.pi / 2, None, ALU.add))
                settled()
                reduce(shifted)
                clamp(flat)
                clamp(shifted)
                settled()
                dve.engine_nop().then_inc(angles_ready, 1)
                dve.wait_ge(sines_ready, 2)
                dve.tensor_scalar(neg_sine, sine, -1.0, None, ALU.mult).then_inc(tables_ready, 1)

            def statistics(at):
                r = at.slot(2)
                dve.wait_ge(x_loaded[at.slot(TURN)], at.quad * 16 + 16)
                dve.bn_stats(stats[:, r], x_sb[:, at.slot(TURN)]).then_inc(stats_done, 1)
                need_apart(dve, stats_done, at.n + 1, waited)
                need_apart(dve, xn_ready, at.n - 1, waited)
                dve.bn_aggr(moments[:, r], stats[:, r]).then_inc(stats_ready, 1)

            def normalise(at):
                r = at.slot(2)
                dve.wait_ge(rstd_ready, at.n + 1)
                need(dve, x_turned, at.n - 1)
                dve.tensor_scalar(xn[:, r], x_sb[:, at.slot(TURN)], moments[:, r, 0:1], rstd[:, r, 1:2],
                                  ALU.subtract, ALU.mult).then_inc(xn_ready, 1)

            def rope_products(at, s):
                table = lambda t, w: t.unsqueeze(1).unsqueeze(3).to_broadcast([P, HG, w, GH])
                cos = by_tile(cosine)[:, at.n]
                dve.wait_ge(projected[s], at.n + 1)
                need(dve, summed[s], at.n)
                view = lambda t: t.rearrange("p (g d h) -> p g d h", g=HG, h=GH)
                pairs = lambda t, r: t.rearrange("p (g a r h) -> p g a r h", g=HG, r=2, h=GH)[:, :, :, r]
                dve.tensor_tensor(view(straight[s]), view(in_bank[s]), table(cos, HEAD), ALU.mult)
                dve.tensor_tensor(pairs(crossed[s], 0), pairs(in_bank[s], 1),
                                  table(by_tile(neg_sine)[:, at.n], ANGLES), ALU.mult)
                dve.tensor_tensor(pairs(crossed[s], 1), pairs(in_bank[s], 0),
                                  table(by_tile(sine)[:, at.n], ANGLES), ALU.mult).then_inc(multiplied[s], 1)

            def take_first(at, s):
                dve.wait_ge(turned[s], at.n + 1)
                dve.wait_ge(first_done[s], at.n + 1)
                need(dve, second_done[s], at.n)
                need(dve, third_done[s], at.n)
                dve.tensor_tensor(rest[s].rearrange("p (k c) -> p k c", k=KX),
                                  turned_bank[s].rearrange("p (k c) -> p k c", k=KX),
                                  part_now(at, s, 0), ALU.subtract).then_inc(rest_done[s], 1)

            def part_now(at, s, part):
                half = at.slot(2)
                return parts[:, at.slot(4) // 2, s, part, :, half * P:(half + 1) * P]

            def weight_low(n, low, raw, high):
                dve.wait_ge(w_high_ready, n)
                dve.tensor_tensor(low, raw, high.bitcast(F32), ALU.subtract).then_inc(w_low_ready, 1)

            def inputs_low(at):
                r = at.slot(2)
                dve.wait_ge(ctxT_saved, at.n + 1)
                need(dve, v_projected, at.n - 1)
                dve.tensor_tensor(ctxT[1][:, r], ctxT_bank, ctxT[0][:, r].bitcast(F32), ALU.subtract
                                  ).then_inc(ctx_low_ready, 1)
                dve.wait_ge(xT_saved, at.n + 1)
                need(dve, projected[1], at.n - 1)
                dve.tensor_tensor(xT[1][:, r], xT_bank, xT[0][:, r].bitcast(F32), ALU.subtract
                                  ).then_inc(x_low_ready, 1)

            statistics(At(0, 0))
            weight_low(1, plain(wk_sb[1]), order(wk_raw, KC), plain(wk_sb[0]))
            make_tables()
            dve.wait_ge(tables_ready, 1)

            def step(at):
                if at.back(4).within(TILES):
                    rope_products(at.back(4), 1)
                if at.back(2).within(TILES):
                    inputs_low(at.back(2))
                if at.back(4).within(TILES):
                    take_first(at.back(4), 0)
                if at.back(1).within(TILES):
                    normalise(at.back(1))
                if not at.looped and at.n == 1:
                    weight_low(2, wv_sb[1][:], wv_raw, wv_sb[0][:])
                if at.within(TILES) and not (isinstance(at.n, int) and at.n == 0):
                    statistics(at)
                if not at.looped and at.n == 2:
                    weight_low(3, plain(wq_sb[1]), order(wq_raw, KX), plain(wq_sb[0]))
                if at.back(3).within(TILES):
                    rope_products(at.back(3), 0)
                if at.back(4).within(TILES):
                    take_first(at.back(4), 1)

            run_steps(dve, TILES, 4, 5, step)
            weigh_ffn()

        @block.scalar
        def _(act):
            def part_now(at, s, part):
                half = at.slot(2)
                return parts[:, at.slot(4) // 2, s, part, :, half * P:(half + 1) * P]

            def save_inputs(at):
                r = at.slot(2)
                act.wait_ge(ctx_turned, at.n + 1)
                need(act, v_projected, at.n - 1)
                nc.scalar.copy(ctxT[0][:, r], ctxT_bank).then_inc(ctxT_saved, 1)
                act.wait_ge(x_turned, at.n + 1)
                need(act, projected[1], at.n - 1)
                nc.scalar.copy(xT[0][:, r], xT_bank).then_inc(xT_saved, 1)

            def save_v(at):
                need_apart(act, v_projected, at.n + 1, waited)
                out = v_all[:].rearrange("p (b g) c e -> p b c g e", b=BATCH)[:, at.quad, at.slot(CHUNKS)]
                nc.scalar.copy(out, v_bank.rearrange("p (g e) -> p g e", g=HG)).then_inc(v_saved, 1)

            def first_two(at, s):
                pair = at.slot(4) // 2
                need(act, parts_stored[pair], at.quad * PAIR_STORES + START)
                act.wait_ge(turned[s], at.n + 1)
                nc.scalar.copy(part_now(at, s, 0), turned_bank[s].rearrange("p (k c) -> p k c", k=KX)
                               ).then_inc(first_done[s], 1)
                act.wait_ge(rest_done[s], at.n + 1)
                nc.scalar.copy(part_now(at, s, 1), rest[s].rearrange("p (k c) -> p k c", k=KX)
                               ).then_inc(second_done[s], 1)

            def sum_pieces(at):
                act.wait_ge(piece_loaded[at.slot(TURN)], at.quad * 32 + 32)
                for w in range(2):
                    nc.scalar.activation(ffn_abs[:, w], ffn_piece[:, at.slot(TURN), w], ACT.Abs,
                                         accum_out=abs_sums[:, w, at.n:at.n + 1] if not at.looped else
                                         abs_sums[:, w, bass.ds(at.n, 1)]).then_inc(piece_summed, 1)

            act.wait_ge(w_loaded["wk"], 16)
            nc.scalar.copy(plain(wk_sb[0]), order(wk_raw, KC)).then_inc(w_high_ready, 1)
            act.wait_ge(w_loaded["wv"], 16)
            nc.scalar.copy(wv_sb[0][:], wv_raw).then_inc(w_high_ready, 1)
            act.wait_ge(angles_ready, 1)
            nc.scalar.activation(sine,
                                 angle[:].rearrange("p t a f -> p (t a f)"), ACT.Sin).then_inc(sines_ready, 1)
            nc.scalar.activation(cosine.rearrange("p (t r) -> p t r", r=2),
                                 shifted.unsqueeze(2).to_broadcast([P, TILES * ANGLES, 2]),
                                 ACT.Sin).then_inc(sines_ready, 1)

            def step(at):
                if at.back(2).within(TILES):
                    save_inputs(at.back(2))
                if not at.looped and at.n == 2:
                    act.wait_ge(w_loaded["wq"], 16)
                    nc.scalar.copy(plain(wq_sb[0]), order(wq_raw, KX)).then_inc(w_high_ready, 1)
                if at.back(4).within(TILES):
                    first_two(at.back(4), 0)
                if at.back(3).within(TILES):
                    sum_pieces(at.back(3))
                if at.back(3).within(TILES):
                    save_v(at.back(3))
                if at.back(4).within(TILES):
                    first_two(at.back(4), 1)

            run_steps(act, TILES, 4, 5, step)

        @block.gpsimd
        def _(pool):
            def spread(at):
                r = at.slot(2)
                need_apart(pool, stats_ready, at.n + 1, waited)
                need_apart(pool, xn_ready, at.n - 1, waited)
                pool.tensor_scalar(rstd[:, r, 0:1], moments[:, r, 1:2], LN_EPS, None, ALU.add).then_inc(power_ready, 1)
                pool.wait_ge(power_ready, at.n + 2)
                pool.tensor_tensor(rstd[:, r, 1:2], rstd[:, r, 0:1], half_power[:], ALU.pow).then_inc(rstd_ready, 1)

            def sum_products(at, s):
                pool.wait_ge(multiplied[s], at.n + 1)
                need(pool, turned[s], at.n)
                pool.tensor_tensor(rotated[s], straight[s], crossed[s], ALU.add).then_inc(summed[s], 1)

            def last_part(at, s):
                half = at.slot(2)
                now = lambda part: parts[:, at.slot(4) // 2, s, part, :, half * P:(half + 1) * P]
                pool.wait_ge(second_done[s], at.n + 1)
                pool.tensor_tensor(now(2), rest[s].rearrange("p (k c) -> p k c", k=KX), now(1),
                                   ALU.subtract).then_inc(third_done[s], 1)

            pool.memset(half_power[:], -0.5).then_inc(power_ready, 1)
            pool.memset(ones[:], 1.0).then_inc(ones_ready, 1)
            for pair in range(2):
                pool.sem_inc(parts_stored[pair], START)

            def step(at):
                if at.back(4).within(TILES):
                    sum_products(at.back(4), 1)
                    last_part(at.back(4), 0)
                if at.within(TILES):
                    spread(at)
                if at.back(3).within(TILES):
                    sum_products(at.back(3), 0)
                if at.back(4).within(TILES):
                    last_part(at.back(4), 1)

            run_steps(pool, TILES, 4, 5, step)


def attend(nc, w_fc, w_proj, identb, ident16, limits, v_all, q_parts, k_parts, q_stack, k_stack,
           stacks_loaded, parts_stored, o_all, wT):
    with ExitStack() as stack:
        sb, pb, sem = allocators(nc, stack, "attend")
        probs = sb("probs", [P, CHUNKS, GH, SEQ], F32)
        v_ones = sb("v_ones", [P, 2, CHUNKS, GH, 2 * HEAD], F32)
        maxima = sb("maxima", [P, 2, GH * CHUNKS], F32)
        neg_max = sb("neg_max", [P, 2, GH * CHUNKS], F32)
        max_parts = sb("max_parts", [P, 2, 2 * GH * CHUNKS], BF16)
        max_rows = sb("max_rows", [2 * GH * CHUNKS, 2, P], BF16)
        raw = sb("raw", [P, 2, DIM], F32)
        below = sb("below", [P, DIM], F16)
        ternary = sb("ternary", [P, 2, DIM], F16)
        banks = pb("banks", [P, 8, SEQ], F32)
        score_slot = [banks[:, 0:2], banks[:, 2:4]]
        PV_BANK = banks[:, 7]
        HALFWAY = 8
        RING = [4 + i % 3 for i in range(15)] + [5, 6]
        TURN_BANK = RING[HALFWAY]
        ST_BANK = RING[:HALFWAY] + RING[HALFWAY + 1:]
        ST_BEFORE = [max(j for j in range(k - 16, k) if ST_BANK[j % 16] == ST_BANK[k]) for k in range(16)]
        BEFORE_TURN = max(k for k in range(HALFWAY) if ST_BANK[k] == TURN_BANK)
        AFTER_TURN = min(k for k in range(HALFWAY, 16) if ST_BANK[k] == TURN_BANK)

        max_loaded = [sem(f"max_loaded_{i}") for i in range(TURN)]
        ones_ready, v_staged = sem("ones_ready"), sem("v_staged")
        scores_ready, scores_read = sem("scores_ready"), sem("scores_read")
        neg_ready, high_ready, split_ready = sem("neg_ready"), sem("high_ready"), sem("split_ready")
        st_ready, exp_done = sem("st_ready"), sem("exp_done")
        pv_done, o_saved = sem("pv_done"), sem("o_saved")
        raw_loaded = [sem(f"raw_loaded_{i}") for i in range(2)]
        cut, ternary_ready = sem("cut"), sem("ternary_ready")
        both_turned, max_saved, weight_saved = sem("both_turned"), sem("max_saved"), sem("weight_saved")
        max_bank = banks[0:2 * GH * CHUNKS, TURN_BANK, 0:P // 2].bitcast(BF16)
        weight_bank = banks[:, TURN_BANK, P // 2:P // 2 + DIM // 2].bitcast(F16)

        waited = sem("waited")
        block = stack.enter_context(nc.Block())

        @block.sync
        def _(sp):
            def load_max(at):
                sp.wait_ge(max_saved, at.n + 1)
                sp.dma_start(
                    q_stack[STACK:STACK + 2, at.slot(TURN)].rearrange("p h (c q) -> p (h c) q", c=CHUNKS),
                    max_rows[:, at.slot(2)],
                ).then_inc(max_loaded[at.slot(TURN)], 16)

            def load_weight(at):
                half = at.slot(TURN) // 2
                need(sp, ternary_ready, at.n - 1)
                if at.slot(2) == 0:
                    sp.dma_start(raw[:, 0], w_fc.rearrange("(i h p) d -> h i p d", h=2, p=P)[half, at.quad]
                                 ).then_inc(raw_loaded[0], 16)
                else:
                    sp.dma_start(raw[:, 1].rearrange("p (r c) -> p r c", r=2),
                                 w_proj.rearrange("(h r p) (i c) -> h i p r c", h=2, p=P, c=2 * P)[half, at.quad]
                                 ).then_inc(raw_loaded[1], 16)

            def step(at):
                if at.within(GROUPS):
                    load_weight(at)
                if not at.looped and at.n == TURN - 1:
                    for pair in range(2):
                        sp.wait_ge(parts_stored[pair], PAIR_STORES * BATCH + START)
                if at.looped or PRELOADED <= at.n < GROUPS:
                    need(sp, st_ready, (at.n - TURN + 1) * 16)
                    load_stacks(sp, at, q_parts, k_parts, q_stack, k_stack, stacks_loaded)
                if at.back(2).within(GROUPS):
                    load_max(at.back(2))

            run_steps(sp, GROUPS, 3, 4, step)

        @block.tensor
        def _(pe):
            def scores(at, j):
                head, slot = j // 2, at.slot(TURN)
                if j == 0:
                    pe.wait_ge(stacks_loaded[slot], at.quad * STACK_LOADS + STACK_LOADS)
                need(pe, scores_read, at.n * 2 * GH + j - 1)
                for i in range(2):
                    c = j % 2 * 2 + i
                    mm = nc.tensor.matmul(score_slot[j % 2][:, i],
                                          q_stack[0:STACK, slot, head, c * P:(c + 1) * P],
                                          k_stack[0:STACK, slot, head, :], start=True, stop=True)
                mm.then_inc(scores_ready, 1)

            def turn_both(at):
                pe.wait_ge(split_ready, at.n + 1)
                if at.looped or at.n > 0:
                    pe.wait_ge(exp_done, (at.n - 1) * 16 + BEFORE_TURN + 1)
                nc.tensor.transpose(max_bank, max_parts[:, at.slot(2)], identb[:])
                pe.wait_ge(ternary_ready, at.n + 1)
                for i in range(4):
                    mm = nc.tensor.transpose(weight_bank[:, i * P:(i + 1) * P],
                                             ternary[:, at.slot(2), i * P:(i + 1) * P], ident16[:])
                mm.then_inc(both_turned, 1)

            def scores_turned(at, k):
                c, head, slot = k // GH, k % GH, at.slot(TURN)
                if k == 0:
                    if not at.looped:
                        pe.wait_ge(ones_ready, 2)
                    pe.wait_ge(max_loaded[slot], at.quad * 16 + 16)
                if not at.looped and at.n == 0 and k == ST_BANK.index(TURN_BANK):
                    pe.wait_ge(weight_saved, 1)
                elif k != AFTER_TURN:
                    need(pe, exp_done, at.n * 16 + ST_BEFORE[k] + 1)
                elif at.looped or at.n < GROUPS - 1:
                    pe.wait_ge(weight_saved, at.n + 2)
                else:
                    pe.wait_ge(exp_done, at.n * 16 + BEFORE_TURN + 1)
                nc.tensor.matmul(banks[:, ST_BANK[k]], k_stack[0:STACK + 2, slot, head, c * P:(c + 1) * P],
                                 q_stack[0:STACK + 2, slot, head, :], start=True, stop=True).then_inc(st_ready, 1)

            def weigh_v(at, c):
                pe.wait_ge(exp_done, at.n * 16 + GH * (c + 1))
                if c == 0:
                    pe.wait_ge(v_staged, at.n + 1)
                    need(pe, o_saved, at.n)
                for j in range(GH):
                    mm = nc.tensor.matmul(PV_BANK[32 * j:32 * j + 32], v_ones[:, at.slot(2), c, j, :],
                                          probs[:, c, j, :], start=(c == 0), stop=(c == CHUNKS - 1))
                mm.then_inc(pv_done, 1)

            def step(at):
                turned, before = at.back(2), at.back(3)
                for c in range(CHUNKS):
                    if turned.within(GROUPS):
                        scores_turned(turned, 4 * c)
                    if at.within(GROUPS):
                        scores(at, 2 * c)
                    if turned.within(GROUPS):
                        scores_turned(turned, 4 * c + 1)
                    if c == 0 and before.within(GROUPS):
                        weigh_v(before, CHUNKS - 1)
                    if c > 0 and turned.within(GROUPS):
                        weigh_v(turned, c - 1)
                    if turned.within(GROUPS):
                        scores_turned(turned, 4 * c + 2)
                        scores_turned(turned, 4 * c + 3)
                    if at.within(GROUPS):
                        scores(at, 2 * c + 1)
                    if c == 1 and at.back(1).within(GROUPS):
                        turn_both(at.back(1))

            run_steps(pe, GROUPS, 3, 4, step)

        @block.vector
        def _(dve):
            def row_maxima(at, j):
                dve.wait_ge(scores_ready, at.n * 2 * GH + j + 1)
                if j == 0:
                    need(dve, split_ready, at.n - 1)
                dve.tensor_reduce(maxima[:, at.slot(2), 2 * j:2 * j + 2], score_slot[j % 2],
                                  AX.X, ALU.max).then_inc(scores_read, 1)

            def save_sums(at):
                need_apart(dve, pv_done, (at.n + 1) * CHUNKS, waited)
                dve.tensor_copy(o_all[:, at.n], PV_BANK).then_inc(o_saved, 1)

            def step(at):
                for j in range(2 * GH):
                    if j == 1 and at.back(3).within(GROUPS):
                        save_sums(at.back(3))
                    if at.within(GROUPS):
                        row_maxima(at, j)

            run_steps(dve, GROUPS, 3, 4, step)

        @block.scalar
        def _(act):
            def exponentials(at, k):
                c, head = k // GH, k % GH
                act.wait_ge(st_ready, at.n * 16 + k + 1)
                if head == 0:
                    need(act, pv_done, (at.n - 1) * CHUNKS + c + 1)
                nc.scalar.activation(probs[:, c, head, :], banks[:, ST_BANK[k]], ACT.Exp,
                                     scale=1 / math.sqrt(HEAD)).then_inc(exp_done, 1)

            def save_both(at):
                need_apart(act, both_turned, at.n + 1, waited)
                last = at.back(2)
                if last.looped or last.n >= 0:
                    act.wait_ge(max_loaded[last.slot(TURN)], last.quad * 16 + 16)
                nc.scalar.copy(max_rows[:, at.slot(2)], max_bank).then_inc(max_saved, 1)
                nc.scalar.copy(wT[:, at.n], weight_bank).then_inc(weight_saved, 1)

            for pair in range(2):
                act.wait_ge(parts_stored[pair], PAIR_STORES * BATCH + START)

            def step(at):
                for k in range(16):
                    if at.back(2).within(GROUPS):
                        exponentials(at.back(2), k)
                    if k == HALFWAY - 1 and at.back(1).within(GROUPS):
                        save_both(at.back(1))

            run_steps(act, GROUPS, 3, 4, step)

        @block.gpsimd
        def _(pool):
            def stage_v(at):
                need(pool, pv_done, (at.n - 1) * CHUNKS)
                pool.tensor_copy(v_ones[:, at.slot(2), :, :, 0:HEAD],
                                 v_all[:, at.n].rearrange("p c (h d) -> p c h d", h=GH)).then_inc(v_staged, 1)

            def split_maxima(at):
                r, half = at.slot(2), GH * CHUNKS
                need_apart(pool, scores_read, (at.n + 1) * 2 * GH, waited)
                pool.tensor_scalar(neg_max[:, r], maxima[:, r], -1.0, None, ALU.mult).then_inc(neg_ready, 1)
                need_apart(pool, neg_ready, at.n + 1, waited)
                if at.looped or at.n >= 2:
                    need_apart(pool, both_turned, at.n - 1, waited)
                pool.tensor_scalar(max_parts[:, r, 0:half], neg_max[:, r], 1.0, None, ALU.mult
                                   ).then_inc(high_ready, 1)
                pool.wait_ge(high_ready, at.n + 1)
                pool.tensor_tensor(max_parts[:, r, half:2 * half], neg_max[:, r], max_parts[:, r, 0:half],
                                   ALU.subtract).then_inc(split_ready, 1)

            def ternarise(at):
                w = at.slot(2)
                need_apart(pool, raw_loaded[w], at.use_of_two * 16, waited)
                need_apart(pool, ternary_ready, at.n, waited)
                pool.tensor_scalar(below[:], raw[:, w], limits[:, 1, w:w + 1], None, ALU.is_lt).then_inc(cut, 1)
                need_apart(pool, both_turned, at.n - 1, waited)
                pool.tensor_scalar(ternary[:, w], raw[:, w], limits[:, 0, w:w + 1], None, ALU.is_gt).then_inc(cut, 1)
                pool.wait_ge(cut, at.n * 2 + 2)
                pool.tensor_tensor(ternary[:, w], ternary[:, w], below[:], ALU.subtract).then_inc(ternary_ready, 1)

            pool.memset(v_ones[:], 1.0).then_inc(ones_ready, 1)
            pool.wait_ge(ones_ready, 1)
            pool.memset(k_stack[STACK:STACK + 2].bitcast(mybir.dt.uint32), 0x3F803F80).then_inc(ones_ready, 1)
            pool.wait_ge(ones_ready, 2)

            def step(at):
                if at.back(1).within(GROUPS):
                    stage_v(at.back(1))
                if at.within(GROUPS):
                    ternarise(at)
                    split_maxima(at)

            run_steps(pool, GROUPS, 2, 4, step)


def mix(nc, x, wout, bout, ident, ident16, o_all, gammas, x1, uT, row_scale):
    with ExitStack() as stack:
        sb, pb, sem = allocators(nc, stack, "mix")
        x_in = sb("x_in", [P, TURN, DIM], F32)
        STRAIGHT = 6
        o_in = sb("o_in", [P, 2, HG, P], F32)
        wout_sb = sb("wout_sb", [P, KX, DIM], F32)
        bout_sb = sb("bout_sb", [P, DIM], F32)
        inverse = sb("inverse", [P, 2, HEADS], F32)
        attn = sb("attn", [P, 2, DIM], F32)
        attnT = sb("attnT", [P, 2, DIM], F32)
        stats = sb("stats", [P, 2, 6], F32)
        moments = sb("moments", [P, 2, 2], F32)
        powers = sb("powers", [P, 2, 7], F32)
        gamma_128 = sb("gamma_128", [P, 1], F32)
        half_power = sb("half_power", [P, 1], F32)
        centred = sb("centred", [P, 2, DIM], F32)
        absmax = sb("absmax", [P, 2, 4], F32)
        u = sb("u", [P, DIM], F32)
        u_parts = sb("u_parts", [P, 2, 2, DIM], F16)
        banks = pb("banks", [P, 8, DIM], F32)
        rows_bank, y_bank = [banks[:, 0:2], banks[:, 2:4]], [banks[:, 4], banks[:, 5]]
        attnT_bank, uT_bank = banks[:, 6], banks[:, 7].bitcast(F16)

        x_in_loaded = [sem(f"x_in_loaded_{i}") for i in range(TURN)]
        o_in_loaded = [sem(f"o_in_loaded_{i}") for i in range(2)]
        wout_loaded, bout_loaded, power_set = sem("wout_loaded"), sem("bout_loaded"), sem("power_set")
        rows_ready, inverse_ready, attn_ready = sem("rows_ready"), sem("inverse_ready"), sem("attn_ready")
        attn_turned, attnT_saved, y_ready = sem("attn_turned"), sem("attnT_saved"), sem("y_ready")
        x_bias_ready, x1_ready, stats_done, stats_ready = (
            sem("x_bias_ready"), sem("x1_ready"), sem("stats_done"), sem("stats_ready"))
        spread_step, spread_ready, scale_ready = sem("spread_step"), sem("spread_ready"), sem("scale_ready")
        mean_negated = sem("mean_negated")
        centred_ready, quant_step, u_clipped, u_first = (
            sem("centred_ready"), sem("quant_step"), sem("u_clipped"), sem("u_first"))
        u_ready, u_turned, uT_saved = sem("u_ready"), sem("u_turned"), sem("uT_saved")
        o_rows = lambda b: o_all[:].rearrange("p (b g) q -> p b g q", b=BATCH)[:, b]
        waited = sem("waited")
        block = stack.enter_context(nc.Block())

        @block.sync
        def _(sp):
            x_rows = x.rearrange("b (c p) d -> (b c) p d", p=P)
            def load(at):
                if at.looped:
                    sp.wait_ge(rows_ready, at.n - 1)
                    c = at.slot(CHUNKS)
                    sp.dma_start(o_in[:, at.slot(2)], o_rows(at.quad)[:, :, c * P:(c + 1) * P]
                                 ).then_inc(o_in_loaded[at.slot(2)], 16)
                need(sp, x1_ready, at.n - TURN + 1)
                sp.dma_start(x_in[:, at.slot(TURN)], x_rows[at.n]).then_inc(x_in_loaded[at.slot(TURN)], 16)

            sp.dma_start(wout_sb[:], wout.rearrange("(k p) n -> p k n", p=P)).then_inc(wout_loaded, 16)
            sp.dma_start(bout_sb[:], bout.rearrange("(a d) -> a d", a=1).to_broadcast([P, DIM])
                         ).then_inc(bout_loaded, 16)
            run_steps(sp, TILES, 0, STRAIGHT, load)

        @block.tensor
        def _(pe):
            def turn_sums(at):
                need(pe, attn_ready, at.n - 1)
                if at.looped:
                    pe.wait_ge(o_in_loaded[at.slot(2)], (at.use_of_two - STRAIGHT // 2) * 16)
                    rows = o_in[:, at.slot(2)]
                else:
                    rows = o_rows(at.quad)[:, :, at.slot(CHUNKS) * P:(at.slot(CHUNKS) + 1) * P]
                for g in range(HG):
                    mm = nc.tensor.transpose(rows_bank[at.slot(2)][:, g // 4, g % 4 * P:(g % 4 + 1) * P],
                                             rows[:, g, :], ident[:])
                mm.then_inc(rows_ready, 1)

            def turn_attn(at):
                pe.wait_ge(attn_ready, at.n + 1)
                need(pe, attnT_saved, at.n)
                for k in range(KX):
                    mm = nc.tensor.transpose(attnT_bank[:, k * P:(k + 1) * P],
                                             attn[:, at.slot(2), k * P:(k + 1) * P], ident[:])
                mm.then_inc(attn_turned, 1)

            def project_out(at):
                if not at.looped:
                    pe.wait_ge(wout_loaded, 16)
                pe.wait_ge(attnT_saved, at.n + 1)
                need(pe, x1_ready, at.n - 1)
                for k in range(KX):
                    mm = nc.tensor.matmul(y_bank[at.slot(2)], attnT[:, at.slot(2), k * P:(k + 1) * P], wout_sb[:, k, :],
                                          start=(k == 0), stop=(k == KX - 1))
                mm.then_inc(y_ready, 1)

            def turn_u(at):
                pe.wait_ge(u_ready, at.n + 1)
                need(pe, uT_saved, at.n)
                for part in range(2):
                    for k in range(KX):
                        i = part * KX + k
                        mm = nc.tensor.transpose(uT_bank[:, i * P:(i + 1) * P],
                                                 u_parts[:, at.slot(2), part, k * P:(k + 1) * P], ident16[:])
                mm.then_inc(u_turned, 1)

            def step(at):
                if at.within(TILES):
                    turn_sums(at)
                if at.back(1).within(TILES):
                    turn_attn(at.back(1))
                if at.back(2).within(TILES):
                    project_out(at.back(2))
                if at.back(5).within(TILES):
                    turn_u(at.back(5))

            run_steps(pe, TILES, 5, STRAIGHT, step)

        @block.vector
        def _(dve):
            rows = lambda at: rows_bank[at.slot(2)].rearrange("p a (m e) -> p (a m) e", e=2 * HEAD)

            def invert_sums(at):
                need(dve, attn_ready, at.n - 1)
                dve.wait_ge(rows_ready, at.n + 1)
                dve.reciprocal(inverse[:, at.slot(2)], rows(at)[:, :, HEAD]).then_inc(inverse_ready, 1)

            def divide(at):
                dve.wait_ge(inverse_ready, at.n + 1)
                need(dve, attn_turned, at.n - 1)
                dve.tensor_tensor(attn[:, at.slot(2)].rearrange("p (m d) -> p m d", d=HEAD), rows(at)[:, :, 0:HEAD],
                                  inverse[:, at.slot(2)].unsqueeze(2).to_broadcast([P, HEADS, HEAD]), ALU.mult
                                  ).then_inc(attn_ready, 1)

            def add_residual(at):
                dve.wait_ge(y_ready, at.n + 1)
                dve.wait_ge(x_bias_ready, at.n + 1)
                dve.tensor_tensor(x1[:, at.n], y_bank[at.slot(2)], x_in[:, at.slot(TURN)], ALU.add
                                  ).then_inc(x1_ready, 1)

            def statistics(at):
                need_apart(dve, x1_ready, at.n + 1, waited)
                need_apart(dve, stats_ready, at.n - 1, waited)
                dve.bn_stats(stats[:, at.slot(2)], x1[:, at.n]).then_inc(stats_done, 1)

            def join_statistics(at):
                need_apart(dve, stats_done, at.n + 1, waited)
                need_apart(dve, scale_ready, at.n - 1, waited)
                dve.bn_aggr(moments[:, at.slot(2)], stats[:, at.slot(2)]).then_inc(stats_ready, 1)

            now = lambda at, i: absmax[:, at.slot(2), i:i + 1]

            def largest(at):
                dve.wait_ge(centred_ready, at.n + 1)
                need(dve, scale_ready, at.n - 1)
                dve.tensor_reduce(now(at, 0), centred[:, at.slot(2)], AX.X, ALU.max, apply_absolute_value=True
                                  ).then_inc(quant_step, 1)

            def invert_largest(at):
                dve.wait_ge(quant_step, at.n * 4 + 1)
                dve.reciprocal(now(at, 1), now(at, 0)).then_inc(quant_step, 1)

            def take_factor(at):
                dve.wait_ge(quant_step, at.n * 4 + 2)
                dve.tensor_scalar(now(at, 2), now(at, 1), Q_B, None, ALU.mult).then_inc(quant_step, 1)

            def take_factor_back(at):
                dve.wait_ge(spread_ready, at.n + 1)
                dve.scalar_tensor_tensor(now(at, 3), now(at, 1), 0.0, powers[:, at.slot(2), 5:6], ALU.mult, ALU.add
                                         ).then_inc(quant_step, 1)

            def clip_above(at):
                dve.wait_ge(quant_step, at.n * 4 + 4)
                need(dve, u_ready, at.n)
                dve.tensor_scalar(u[:], centred[:, at.slot(2)], now(at, 2), Q_B, ALU.mult, ALU.min
                                  ).then_inc(u_clipped, 1)

            def scale_rows(at):
                dve.scalar_tensor_tensor(row_scale[:, at.n], now(at, 0), now(at, 3), gamma_128[:],
                                         ALU.mult, ALU.mult).then_inc(scale_ready, 1)

            def first_part(at):
                need(dve, u_turned, at.n - 1)
                dve.wait_ge(u_clipped, at.n + 1)
                dve.tensor_scalar(u_parts[:, at.slot(2), 0], u[:], -Q_B, None, ALU.max).then_inc(u_first, 1)

            def second_part(at):
                dve.wait_ge(u_first, at.n + 1)
                dve.scalar_tensor_tensor(u_parts[:, at.slot(2), 1], u[:], -Q_B, u_parts[:, at.slot(2), 0],
                                         ALU.max, ALU.subtract).then_inc(u_ready, 1)

            dve.tensor_scalar(gamma_128[:], gammas[:, 0:1], 1 / Q_B, None, ALU.mult)

            def step(at):
                for part, tile in (
                    (invert_sums, at), (largest, at.back(4)), (divide, at),
                    (invert_largest, at.back(4)), (add_residual, at.back(3)), (take_factor, at.back(4)),
                    (statistics, at.back(3)), (take_factor_back, at.back(4)), (join_statistics, at.back(3)),
                    (clip_above, at.back(4)), (scale_rows, at.back(4)),
                    (first_part, at.back(4)), (second_part, at.back(4)),
                ):
                    if tile.within(TILES):
                        part(tile)

            run_steps(dve, TILES, 4, 6, step)

        @block.scalar
        def _(act):
            def centre(at):
                need_apart(act, mean_negated, at.n + 1, waited)
                need_apart(act, u_clipped, at.n - 1, waited)
                nc.scalar.activation(centred[:, at.slot(2)], x1[:, at.n], ACT.Identity,
                                     bias=powers[:, at.slot(2), 6:7]).then_inc(centred_ready, 1)

            def save_attn(at):
                act.wait_ge(attn_turned, at.n + 1)
                need(act, y_ready, at.n - 1)
                nc.scalar.copy(attnT[:, at.slot(2)], attnT_bank).then_inc(attnT_saved, 1)

            def save_u(at):
                need_apart(act, u_turned, at.n + 1, waited)
                nc.scalar.copy(uT[:, at.n], uT_bank).then_inc(uT_saved, 1)

            def step(at):
                if at.back(1).within(TILES):
                    save_attn(at.back(1))
                if at.back(3).within(TILES):
                    centre(at.back(3))
                if at.back(5).within(TILES):
                    save_u(at.back(5))

            run_steps(act, TILES, 5, 6, step)

        @block.gpsimd
        def _(pool):
            def add_bias(at):
                pool.wait_ge(x_in_loaded[at.slot(TURN)], at.quad * 16 + 16)
                pool.tensor_tensor(x_in[:, at.slot(TURN)], x_in[:, at.slot(TURN)], bout_sb[:], ALU.add
                                   ).then_inc(x_bias_ready, 1)

            def spread(at):
                r = at.slot(2)
                now = lambda i: powers[:, r, i:i + 1]
                count = [0]

                def then(ins):
                    count[0] += 1
                    ins.then_inc(spread_step, 1)
                    need_apart(pool, spread_step, at.n * 6 + count[0], waited)

                need_apart(pool, stats_ready, at.n + 1, waited)
                need_apart(pool, scale_ready, at.n - 1, waited)
                pool.tensor_scalar(now(6), moments[:, r, 0:1], -1.0, None, ALU.mult).then_inc(mean_negated, 1)
                then(pool.tensor_scalar(now(0), moments[:, r, 1:2], LN_EPS, None, ALU.add))
                then(pool.tensor_tensor(now(1), now(0), half_power[:], ALU.pow))
                then(pool.tensor_tensor(now(2), now(1), now(1), ALU.mult))
                then(pool.tensor_tensor(now(3), now(2), moments[:, r, 1:2], ALU.mult))
                then(pool.tensor_scalar(now(3), now(3), FFN_EPS, None, ALU.add))
                then(pool.tensor_tensor(now(4), now(3), half_power[:], ALU.pow))
                pool.tensor_tensor(now(5), now(4), now(1), ALU.mult).then_inc(spread_ready, 1)

            pool.memset(half_power[:], -0.5).then_inc(power_set, 1)
            pool.wait_ge(power_set, 1)
            pool.wait_ge(bout_loaded, 16)

            def step(at):
                if at.back(2).within(TILES):
                    add_bias(at.back(2))
                if at.back(3).within(TILES):
                    spread(at.back(3))

            run_steps(pool, TILES, 3, 5, step)


def ffn(nc, ident16, o_all, uT, row_scale, gammas, x1, wT, out):
    with ExitStack() as stack:
        sb, pb, sem = allocators(nc, stack, "ffn")
        spare = o_all[:].rearrange("p g q -> p (g q)")
        h = spare[:, 0:4 * FFN].rearrange("p (s c) -> p s c", s=TURN)
        h_parts = spare[:, 4 * FFN:6 * FFN].bitcast(F16).rearrange("p (s t c) -> p s t c", s=2, t=2)
        hT = spare[:, 6 * FFN:8 * FFN].bitcast(F16).rearrange("p (s j k r) -> p s j k r", s=2, j=4, r=P)
        fcT = wT[:].rearrange("p (o q w) (k c) -> p w k o q c", q=4, w=2, k=KX)[:, 0]
        projT = wT[:].rearrange("p (i h w) (r k c) -> p w i k h r c", h=2, w=2, r=2, k=2)[:, 1]
        stats = sb("stats", [P, FFN // DIM, 6], F32)
        moments = sb("moments", [P, 2, 2], F32)
        powers = sb("powers", [P, 2, 2], F32)
        half_power = sb("half_power", [P, 1], F32)
        absmax = sb("absmax", [P, 4], F32)
        out_scale = sb("out_scale", [P, TURN, 1], F32)
        gamma_128 = sb("gamma_128", [P, 1], F32)
        y = sb("y", [P, 2, DIM], F32)
        banks = pb("banks", [P, 8, DIM], F32)

        fc_ready, h_ready = sem("fc_ready"), sem("h_ready")
        stats_done, stats_ready, eps_added, spread_ready, power_set = (
            sem("stats_done"), sem("stats_ready"), sem("eps_added"), sem("spread_ready"), sem("power_set"))
        quant_step, gamma_set, parts_ready, scale_ready = (
            sem("quant_step"), sem("gamma_set"), sem("parts_ready"), sem("scale_ready"))
        h_turned, hT_saved, proj_ready, y_ready = sem("h_turned"), sem("hT_saved"), sem("proj_ready"), sem("y_ready")
        out_stored = [sem(f"out_stored_{i}") for i in range(2)]
        QUARTERS = FFN // DIM
        waited = sem("waited")
        block = stack.enter_context(nc.Block())

        @block.sync
        def _(sp):
            out_rows = out.rearrange("b (c p) d -> (b c) p d", p=P)

            def store(at):
                sp.wait_ge(y_ready, at.n + 1)
                sp.dma_start(out_rows[at.n], y[:, at.slot(2)]).then_inc(out_stored[at.slot(2)], 16)

            run_steps(sp, TILES, 0, 4, store)
            for i in range(2):
                sp.wait_ge(out_stored[i], 16 * TILES // 2)

        @block.tensor
        def _(pe):
            def expand(at, o):
                need(pe, h_ready, (at.n - 1) * QUARTERS + o + 1)
                for k in range(KX):
                    for part in range(2):
                        mm = nc.tensor.matmul(banks[:, o], uT[:, at.n, (part * KX + k) * P:(part * KX + k + 1) * P],
                                              fcT[:, k, o],
                                              start=(k + part == 0), stop=(k == KX - 1 and part == 1))
                mm.then_inc(fc_ready, 1)

            def turn_h(at, j):
                if j == 0:
                    pe.wait_ge(parts_ready, at.n + 1)
                need(pe, hT_saved, at.n * 4 + j - 1)
                for i in range(8):
                    first = (j % 2 * 8 + i) * P
                    mm = nc.tensor.transpose(banks[:, 4 + j % 2].bitcast(F16)[:, i * P:(i + 1) * P],
                                             h_parts[:, at.slot(2), j // 2, first:first + P], ident16[:])
                mm.then_inc(h_turned, 1)

            def contract(at, j):
                pe.wait_ge(hT_saved, at.n * 4 + j + 1)
                if j == 0:
                    need(pe, y_ready, at.n - 1)
                for i in range(8):
                    k = j % 2 * 8 + i
                    mm = nc.tensor.matmul(banks[:, 6 + at.slot(2)], hT[:, at.slot(2), j, i, :],
                                          projT[:, k // 2, k % 2], start=(i + j == 0), stop=(j == 3 and i == 7))
                if j == 3:
                    mm.then_inc(proj_ready, 1)

            def step(at):
                before = at.back(3)
                if not at.within(TILES):
                    for work, j in ((turn_h, 0), (turn_h, 1), (contract, 0), (turn_h, 2), (contract, 1), (turn_h, 3),
                                    (contract, 2), (contract, 3)):
                        work(before, j)
                    return
                for half in range(2):
                    if before.within(TILES):
                        turn_h(before, 2 * half)
                        turn_h(before, 2 * half + 1)
                    expand(at, 2 * half)
                    expand(at, 2 * half + 1)
                if before.within(TILES):
                    for j in range(4):
                        contract(before, j)

            run_steps(pe, TILES, 3, 6, step)

        @block.scalar
        def _(act):
            def activate(at, o):
                need_apart(act, fc_ready, at.n * QUARTERS + o + 1, waited)
                if o == 0:
                    need_apart(act, parts_ready, at.n - TURN + 1, waited)
                nc.scalar.activation(h[:, at.slot(TURN), o * DIM:(o + 1) * DIM], banks[:, o], ACT.Gelu,
                                     scale=row_scale[:, at.n]).then_inc(h_ready, 1)

            def save_turned(at, j):
                act.wait_ge(h_turned, at.n * 4 + j + 1)
                need(act, proj_ready, at.n - 1)
                nc.scalar.copy(hT[:, at.slot(2), j].rearrange("p k r -> p (k r)"),
                               banks[:, 4 + j % 2].bitcast(F16)).then_inc(hT_saved, 1)

            def step(at):
                before = at.back(3)
                for half in range(2):
                    if before.within(TILES):
                        save_turned(before, 2 * half)
                        save_turned(before, 2 * half + 1)
                    if at.within(TILES):
                        activate(at, 2 * half)
                        activate(at, 2 * half + 1)

            run_steps(act, TILES, 3, 6, step)

        @block.vector
        def _(dve):
            def statistics(at):
                r = at.slot(2)
                for o in range(QUARTERS):
                    dve.wait_ge(h_ready, at.n * QUARTERS + o + 1)
                    dve.bn_stats(stats[:, o], h[:, at.slot(TURN), o * DIM:(o + 1) * DIM]).then_inc(stats_done, 1)
                need_apart(dve, stats_done, at.n * QUARTERS + QUARTERS, waited)
                dve.bn_aggr(moments[:, r], stats[:].rearrange("p o s -> p (o s)")).then_inc(stats_ready, 1)

            def quantise(at):
                r, steps = at.slot(2), at.n * 7
                now = h[:, at.slot(TURN), :]
                dve.wait_ge(stats_ready, at.n + 1)
                dve.tensor_scalar(now, now, moments[:, r, 0:1], None, ALU.subtract).then_inc(quant_step, 1)
                dve.wait_ge(quant_step, steps + 1)
                dve.tensor_reduce(absmax[:, 0:1], now, AX.X, ALU.max, apply_absolute_value=True
                                  ).then_inc(quant_step, 1)
                dve.wait_ge(quant_step, steps + 2)
                dve.reciprocal(absmax[:, 1:2], absmax[:, 0:1]).then_inc(quant_step, 1)
                dve.wait_ge(quant_step, steps + 3)
                dve.tensor_scalar(absmax[:, 2:3], absmax[:, 1:2], Q_B, None, ALU.mult).then_inc(quant_step, 1)
                dve.wait_ge(spread_ready, at.n + 1)
                dve.scalar_tensor_tensor(absmax[:, 3:4], absmax[:, 1:2], 0.0, powers[:, r, 1:2], ALU.mult, ALU.add
                                         ).then_inc(quant_step, 1)
                dve.wait_ge(quant_step, steps + 5)
                dve.tensor_scalar(now, now, absmax[:, 2:3], Q_B, ALU.mult, ALU.min).then_inc(quant_step, 1)
                dve.scalar_tensor_tensor(out_scale[:, at.slot(TURN)], absmax[:, 0:1], absmax[:, 3:4], gamma_128[:],
                                         ALU.mult, ALU.mult).then_inc(scale_ready, 1)
                need(dve, h_turned, (at.n - 1) * 4)
                dve.wait_ge(quant_step, steps + 6)
                dve.tensor_scalar(h_parts[:, r, 0], now, -Q_B, None, ALU.max).then_inc(quant_step, 1)
                dve.wait_ge(quant_step, steps + 7)
                dve.scalar_tensor_tensor(h_parts[:, r, 1], now, -Q_B, h_parts[:, r, 0], ALU.max, ALU.subtract
                                         ).then_inc(parts_ready, 1)

            def finish(at):
                r = at.slot(2)
                dve.wait_ge(proj_ready, at.n + 1)
                dve.wait_ge(scale_ready, at.n + 1)
                before = at.back(2)
                if before.looped or before.n >= 0:
                    dve.wait_ge(out_stored[r], before.use_of_two * 16)
                dve.scalar_tensor_tensor(y[:, r], banks[:, 6 + r], out_scale[:, at.slot(TURN)], x1[:, at.n],
                                         ALU.mult, ALU.add).then_inc(y_ready, 1)

            dve.tensor_scalar(gamma_128[:], gammas[:, 1:2], 1 / Q_B, None, ALU.mult).then_inc(gamma_set, 1)
            dve.wait_ge(gamma_set, 1)

            def step(at):
                if at.back(4).within(TILES):
                    finish(at.back(4))
                if at.back(1).within(TILES):
                    statistics(at.back(1))
                    quantise(at.back(1))

            run_steps(dve, TILES, 4, 7, step)

        @block.gpsimd
        def _(pool):
            def spread(at):
                r = at.slot(2)
                need_apart(pool, stats_ready, at.n + 1, waited)
                need_apart(pool, scale_ready, at.n - 1, waited)
                pool.tensor_scalar(powers[:, r, 0:1], moments[:, r, 1:2], FFN_EPS, None, ALU.add
                                   ).then_inc(eps_added, 1)
                pool.wait_ge(eps_added, at.n + 1)
                pool.tensor_tensor(powers[:, r, 1:2], powers[:, r, 0:1], half_power[:], ALU.pow
                                   ).then_inc(spread_ready, 1)

            pool.memset(half_power[:], -0.5).then_inc(power_set, 1)
            pool.wait_ge(power_set, 1)
            run_steps(pool, TILES, 0, 4, spread)


def xattn_ffn(nc, x, ctx, pos, wq, wkv, wout, bout, w_fc, w_proj, out):
    q_parts = nc.dram_tensor("q_parts", [GROUPS, PARTS, GW, SEQ], BF16).ap()
    k_parts = nc.dram_tensor("k_parts", [GROUPS, PARTS, GW, SEQ], BF16).ap()
    with ExitStack() as stack:
        sb, _, sem = allocators(nc, stack, "xattn_ffn")
        ident = sb("ident", [P, P], F32)
        identh = sb("identh", [P, P], F16)
        identb = sb("identb", [P, P], BF16)
        filled = sem("filled")
        with nc.Block() as block:

            @block.gpsimd
            def _(pool):
                for n, square in enumerate((ident, identh, identb)):
                    pool.memset(square[:], 0.0).then_inc(filled, 1)
                    pool.wait_ge(filled, 2 * n + 1)
                    pool.affine_select(out=square[:], in_=square[:], compare_op=ALU.not_equal, fill=1.0, base=0,
                                       pattern=[[-1, P]], channel_multiplier=1).then_inc(filled, 1)

        with ExitStack() as attention:
            sb2, _, _ = allocators(nc, attention, "kept")
            o_all = sb2("o_all", [P, GROUPS, SEQ], F32)
            wT = sb2("wT", [P, GROUPS, DIM], F16)
            gammas = sb2("gammas", [P, 2], F32)
            limits = sb2("limits", [P, 2, 2], F32)
            with ExitStack() as stacks:
                sb3, _, sem3 = allocators(nc, stacks, "stacks")
                v_all = sb3("v_all", [P, GROUPS, CHUNKS, GW], F32)
                q_stack = sb3("q_stack", [P, TURN, GH, SEQ], BF16)
                k_stack = sb3("k_stack", [P, TURN, GH, SEQ], BF16)
                stacks_loaded = [sem3(f"stacks_loaded_{i}") for i in range(TURN)]
                parts_stored = [sem3(f"parts_stored_{i}") for i in range(2)]
                project(nc, x, ctx, pos, wq, wkv, w_fc, w_proj, ident, o_all, wT, v_all, gammas, limits,
                        q_parts, k_parts, q_stack, k_stack, stacks_loaded, parts_stored)
                attend(nc, w_fc, w_proj, identb, identh, limits, v_all, q_parts, k_parts, q_stack, k_stack,
                       stacks_loaded, parts_stored, o_all, wT)
            x1 = sb2("x1", [P, TILES, DIM], F32)
            uT = sb2("uT", [P, TILES, 2 * DIM], F16)
            row_scale = sb2("row_scale", [P, TILES, 1], F32)
            mix(nc, x, wout, bout, ident, identh, o_all, gammas, x1, uT, row_scale)
            ffn(nc, identh, o_all, uT, row_scale, gammas, x1, wT, out)


_INS = ["x", "ctx_1024", "fside_BxSx2_0", "L0_xattn_Wq", "L0_xattn_Wkv", "L0_xattn_Wout", "L0_xattn_bout",
        "L0_ffn_w_fc", "L0_ffn_w_proj"]
_OUTS = [((BATCH, SEQ, DIM), "float32")]


def kernel(**inputs):
    import numpy as _np
    import concourse.bacc as _bacc
    from concourse import mybir as _mybir
    from concourse.bass_utils import run_bass_kernel_spmd as _run

    nc = _bacc.Bacc("TRN2", target_bir_lowering=False, num_devices=1)
    arrays, args = {}, []
    for name in _INS:
        a = _np.ascontiguousarray(inputs[name])
        arrays[f"in_{name}_dram"] = a
        args.append(nc.dram_tensor(f"in_{name}_dram", a.shape, _mybir.dt.from_np(a.dtype), kind="ExternalInput").ap())
    for i, (shape, dtype) in enumerate(_OUTS):
        dt = _mybir.dt.from_np(_np.dtype(dtype))
        args.append(nc.dram_tensor(f"out_{i}_dram", shape, dt, kind="ExternalOutput").ap())
    xattn_ffn(nc, *args)
    r = _run(nc, [arrays], core_ids=[0])
    got = tuple(r.results[0][f"out_{i}_dram"] for i in range(len(_OUTS)))
    return got[0]
```
